# Optimizing a Trainium2 kernel written in Bass

```python
import numpy as np
import jax
import jax.numpy as jnp

def _softmax(x, axis=-1):
    return jax.nn.softmax(x, axis=axis)

def _gelu(x):
    return jax.nn.gelu(x, approximate=True)

def _silu(x):
    return jax.nn.silu(x)

def _sigmoid(x):
    return jax.nn.sigmoid(x)

def _layernorm(x, axis=-1, eps=1e-05):
    m = jnp.mean(x, axis=axis, keepdims=True)
    v = jnp.var(x, axis=axis, keepdims=True)
    return (x - m) / jnp.sqrt(v + eps)

def _scatter_add(tgt, idx, src, axis=0):
    return tgt.at[idx].add(src)

def _segment_sum(src, seg, n):
    return jax.ops.segment_sum(src, seg, n)
kernel_name = 'mk_gnn_preln_d2_gnn_r64_81c540'

def setup_inputs(seed: int=0):
    np.random.seed(seed)
    _w = jnp.asarray

    def _rec_inputs():
        import jax
        import jax.numpy as jnp
        _gk = jax.random.key(seed)
        x = -0.000202 + 1 * jax.random.normal(jax.random.fold_in(_gk, 1), (50000, 128), jnp.float32)
        src = jax.random.randint(jax.random.fold_in(_gk, 2), (12500,), 0, 50000, jnp.int32)
        dst = jnp.minimum((50000 * jax.random.uniform(jax.random.fold_in(_gk, 3), (12500,)) ** 2.0).astype(jnp.int32), 49999)
        _o = jnp.argsort(dst, stable=True)
        src = src[_o]
        dst = dst[_o]
        edge_attr_128 = -5.16925e-05 + 1.00005 * jax.random.normal(jax.random.fold_in(_gk, 12), (12500, 128), jnp.float32)
        return (x, src, dst, edge_attr_128)
    x, src, dst, edge_attr_128 = _rec_inputs()

    def _L0_gnn_setup():
        import jax, jax.numpy as jnp
        import numpy as np
        N, E, D = (50000, 12500, 128)
        LN_EPS = 1e-05
        key = jax.random.key(seed)
        ks = jax.random.split(key, 8)
        x = jax.random.normal(ks[0], (N, D), dtype=jnp.float32)
        edge_index = jax.random.randint(ks[1], (2, E), 0, N, dtype=jnp.int64)
        edge_attr = jax.random.normal(ks[2], (E, D), dtype=jnp.float32)
        s_msg = 1.0 / np.sqrt(2 * D)
        s_upd = 1.0 / np.sqrt(2 * D)
        W_msg = jax.random.uniform(ks[3], (2 * D, D), jnp.float32, -s_msg, s_msg)
        b_msg = jax.random.uniform(ks[4], (D,), jnp.float32, -s_msg, s_msg)
        W_upd = jax.random.uniform(ks[5], (2 * D, D), jnp.float32, -s_upd, s_upd)
        b_upd = jax.random.uniform(ks[6], (D,), jnp.float32, -s_upd, s_upd)
        gamma = jnp.ones((D,), jnp.float32)
        beta = jnp.zeros((D,), jnp.float32)
        return {'x': x, 'edge_index': edge_index, 'edge_attr': edge_attr, 'W_msg': W_msg, 'b_msg': b_msg, 'W_upd': W_upd, 'b_upd': b_upd, 'gamma': gamma, 'beta': beta}
    _L0_gnn_all = _L0_gnn_setup()
    _L0_gnn_in = {k: v for k, v in _L0_gnn_all.items() if k in ('W_msg', 'b_msg', 'W_upd', 'b_upd', 'gamma', 'beta')}
    del _L0_gnn_all

    def _L1_gnn_setup():
        import jax, jax.numpy as jnp
        import numpy as np
        N, E, D, H, L = (50000, 12500, 128, 8, 3)
        HD = D // H

        def _layernorm(h, gamma, beta, eps=1e-05):
            mu = h.mean(-1, keepdims=True)
            var = ((h - mu) ** 2).mean(-1, keepdims=True)
            return (h - mu) * jax.lax.rsqrt(var + eps) * gamma + beta

        def _forward(x, src, dst, Wemb, Wq, bq, Wk, bk, Wv, bv, Wo, bo, ln1_g, ln1_b, W1, b1, W2, b2, ln2_g, ln2_b):
            n = x.shape[0]
            scale = np.float32(np.sqrt(HD))
            h = x @ Wemb
            for l in range(L):
                Q = (h @ Wq[l] + bq[l]).reshape(n, H, HD)
                K = (h @ Wk[l] + bk[l]).reshape(n, H, HD)
                V = (h @ Wv[l] + bv[l]).reshape(n, H, HD)
                score = jnp.einsum('ehd,ehd->eh', K[src], Q[dst]) / scale
                score = jnp.exp(jnp.clip(score, -5.0, 5.0))
                wV = jax.ops.segment_sum(V[src] * score[:, :, None], dst, num_segments=n)
                z = jax.ops.segment_sum(score, dst, num_segments=n)
                attn = (wV / (z[:, :, None] + 1e-06)).reshape(n, D)
                h = _layernorm(h + attn @ Wo[l] + bo[l], ln1_g[l], ln1_b[l])
                ffn = jax.nn.relu(h @ W1[l] + b1[l]) @ W2[l] + b2[l]
                h = _layernorm(h + ffn, ln2_g[l], ln2_b[l])
            return h
        key = jax.random.key(seed)
        ks = jax.random.split(key, 16)
        s = 1.0 / np.sqrt(D)
        g = lambda k, shape, sc: jax.random.normal(k, shape, jnp.float32) * sc
        return {'x': g(ks[0], (N, D), 1.0), 'src': jax.random.randint(ks[1], (E,), 0, N, jnp.int32), 'dst': jax.random.randint(ks[2], (E,), 0, N, jnp.int32), 'Wemb': g(ks[3], (D, D), s), 'Wq': g(ks[4], (L, D, D), s), 'bq': jnp.zeros((L, D), jnp.float32), 'Wk': g(ks[5], (L, D, D), s), 'bk': jnp.zeros((L, D), jnp.float32), 'Wv': g(ks[6], (L, D, D), s), 'bv': jnp.zeros((L, D), jnp.float32), 'Wo': g(ks[7], (L, D, D), s), 'bo': jnp.zeros((L, D), jnp.float32), 'ln1_g': jnp.ones((L, D), jnp.float32), 'ln1_b': jnp.zeros((L, D), jnp.float32), 'W1': g(ks[8], (L, D, 2 * D), s), 'b1': jnp.zeros((L, 2 * D), jnp.float32), 'W2': g(ks[9], (L, 2 * D, D), 1.0 / np.sqrt(2 * D)), 'b2': jnp.zeros((L, D), jnp.float32), 'ln2_g': jnp.ones((L, D), jnp.float32), 'ln2_b': jnp.zeros((L, D), jnp.float32)}
    _L1_gnn_all = _L1_gnn_setup()
    _L1_gnn_in = {k: v for k, v in _L1_gnn_all.items() if k in ('Wemb', 'Wq', 'bq', 'Wk', 'bk', 'Wv', 'bv', 'Wo', 'bo', 'ln1_g', 'ln1_b', 'W1', 'b1', 'W2', 'b2', 'ln2_g', 'ln2_b')}
    del _L1_gnn_all
    return {'x': x, 'src': src, 'dst': dst, 'edge_attr_128': edge_attr_128, 'L0_gnn_W_msg': _L0_gnn_in['W_msg'], 'L0_gnn_b_msg': _L0_gnn_in['b_msg'], 'L0_gnn_W_upd': _L0_gnn_in['W_upd'], 'L0_gnn_b_upd': _L0_gnn_in['b_upd'], 'L0_gnn_gamma': _L0_gnn_in['gamma'], 'L0_gnn_beta': _L0_gnn_in['beta'], 'L1_gnn_Wemb': _L1_gnn_in['Wemb'], 'L1_gnn_Wq': _L1_gnn_in['Wq'], 'L1_gnn_bq': _L1_gnn_in['bq'], 'L1_gnn_Wk': _L1_gnn_in['Wk'], 'L1_gnn_bk': _L1_gnn_in['bk'], 'L1_gnn_Wv': _L1_gnn_in['Wv'], 'L1_gnn_bv': _L1_gnn_in['bv'], 'L1_gnn_Wo': _L1_gnn_in['Wo'], 'L1_gnn_bo': _L1_gnn_in['bo'], 'L1_gnn_ln1_g': _L1_gnn_in['ln1_g'], 'L1_gnn_ln1_b': _L1_gnn_in['ln1_b'], 'L1_gnn_W1': _L1_gnn_in['W1'], 'L1_gnn_b1': _L1_gnn_in['b1'], 'L1_gnn_W2': _L1_gnn_in['W2'], 'L1_gnn_b2': _L1_gnn_in['b2'], 'L1_gnn_ln2_g': _L1_gnn_in['ln2_g'], 'L1_gnn_ln2_b': _L1_gnn_in['ln2_b']}

def reference(x, src, dst, edge_attr_128, L0_gnn_W_msg, L0_gnn_b_msg, L0_gnn_W_upd, L0_gnn_b_upd, L0_gnn_gamma, L0_gnn_beta, L1_gnn_Wemb, L1_gnn_Wq, L1_gnn_bq, L1_gnn_Wk, L1_gnn_bk, L1_gnn_Wv, L1_gnn_bv, L1_gnn_Wo, L1_gnn_bo, L1_gnn_ln1_g, L1_gnn_ln1_b, L1_gnn_W1, L1_gnn_b1, L1_gnn_W2, L1_gnn_b2, L1_gnn_ln2_g, L1_gnn_ln2_b):
    import jax
    import jax.numpy as jnp

    def _L0_gnn_ref(x, edge_index, edge_attr, W_msg, b_msg, W_upd, b_upd, gamma, beta):
        import jax, jax.numpy as jnp
        import numpy as np
        N, E, D = (50000, 12500, 128)
        LN_EPS = 1e-05
        src, dst = (edge_index[0], edge_index[1])
        n = x.shape[0]
        msg_in = jnp.concatenate([x[src], edge_attr], axis=-1)
        msg = jax.nn.relu(msg_in @ W_msg + b_msg)
        summed = jax.ops.segment_sum(msg, dst, num_segments=n)
        counts = jax.ops.segment_sum(jnp.ones((msg.shape[0],), x.dtype), dst, num_segments=n)
        mean_msg = summed / jnp.maximum(counts, 1.0)[:, None]
        h = jnp.concatenate([x, mean_msg], axis=-1) @ W_upd + b_upd
        mu = jnp.mean(h, axis=-1, keepdims=True)
        var = jnp.mean(jnp.square(h - mu), axis=-1, keepdims=True)
        h = (h - mu) * jax.lax.rsqrt(var + LN_EPS) * gamma + beta
        return jax.nn.relu(h + x)

    def _L1_gnn_ref(x, src, dst, Wemb, Wq, bq, Wk, bk, Wv, bv, Wo, bo, ln1_g, ln1_b, W1, b1, W2, b2, ln2_g, ln2_b):
        import jax, jax.numpy as jnp
        import numpy as np
        N, E, D, H, L = (50000, 12500, 128, 8, 3)
        HD = D // H

        def _layernorm(h, gamma, beta, eps=1e-05):
            mu = h.mean(-1, keepdims=True)
            var = ((h - mu) ** 2).mean(-1, keepdims=True)
            return (h - mu) * jax.lax.rsqrt(var + eps) * gamma + beta

        def _forward(x, src, dst, Wemb, Wq, bq, Wk, bk, Wv, bv, Wo, bo, ln1_g, ln1_b, W1, b1, W2, b2, ln2_g, ln2_b):
            n = x.shape[0]
            scale = np.float32(np.sqrt(HD))
            h = x @ Wemb
            for l in range(L):
                Q = (h @ Wq[l] + bq[l]).reshape(n, H, HD)
                K = (h @ Wk[l] + bk[l]).reshape(n, H, HD)
                V = (h @ Wv[l] + bv[l]).reshape(n, H, HD)
                score = jnp.einsum('ehd,ehd->eh', K[src], Q[dst]) / scale
                score = jnp.exp(jnp.clip(score, -5.0, 5.0))
                wV = jax.ops.segment_sum(V[src] * score[:, :, None], dst, num_segments=n)
                z = jax.ops.segment_sum(score, dst, num_segments=n)
                attn = (wV / (z[:, :, None] + 1e-06)).reshape(n, D)
                h = _layernorm(h + attn @ Wo[l] + bo[l], ln1_g[l], ln1_b[l])
                ffn = jax.nn.relu(h @ W1[l] + b1[l]) @ W2[l] + b2[l]
                h = _layernorm(h + ffn, ln2_g[l], ln2_b[l])
            return h
        return _forward(x, src, dst, Wemb, Wq, bq, Wk, bk, Wv, bv, Wo, bo, ln1_g, ln1_b, W1, b1, W2, b2, ln2_g, ln2_b)
    edge_index = jnp.stack([src, dst])
    h = jnp.maximum(_layernorm(x, axis=-1), 0.0)
    x = x + _L0_gnn_ref(h, edge_index, edge_attr_128, L0_gnn_W_msg, L0_gnn_b_msg, L0_gnn_W_upd, L0_gnn_b_upd, L0_gnn_gamma, L0_gnn_beta)
    h = jnp.maximum(_layernorm(x, axis=-1), 0.0)
    x = x + _L1_gnn_ref(h, src, dst, L1_gnn_Wemb, L1_gnn_Wq, L1_gnn_bq, L1_gnn_Wk, L1_gnn_bk, L1_gnn_Wv, L1_gnn_bv, L1_gnn_Wo, L1_gnn_bo, L1_gnn_ln1_g, L1_gnn_ln1_b, L1_gnn_W1, L1_gnn_b1, L1_gnn_W2, L1_gnn_b2, L1_gnn_ln2_g, L1_gnn_ln2_b)
    return x

_drawn_inputs = setup_inputs


def setup_inputs(seed=0):
    import zlib

    import numpy as np

    out = dict(_drawn_inputs(seed))
    spreads = {'L0_gnn_gamma': (1.0, 0.2),
     'L0_gnn_beta': (0.0, 0.1),
     'L1_gnn_bq': (0.0, 0.8),
     'L1_gnn_bk': (0.0, 0.8),
     'L1_gnn_bv': (0.0, 0.354),
     'L1_gnn_bo': (0.0, 0.1),
     'L1_gnn_ln1_g': (1.0, 0.2),
     'L1_gnn_ln1_b': (0.0, 0.1),
     'L1_gnn_b1': (0.0, 0.1),
     'L1_gnn_b2': (0.0, 0.1),
     'L1_gnn_ln2_g': (1.0, 0.2),
     'L1_gnn_ln2_b': (0.0, 0.1)}
    factors = {'L0_gnn_b_msg': 8.0}
    for name, (base, spread) in spreads.items():
        noise = np.random.default_rng([zlib.crc32(name.encode()), seed]).standard_normal(out[name].shape)
        drawn = base * np.exp(spread * noise) if base else spread * noise
        out[name] = jnp.asarray(drawn.astype(out[name].dtype))
    for name, factor in factors.items():
        out[name] = (out[name] * factor).astype(out[name].dtype)
    return out
```

```python
from contextlib import ExitStack

import concourse.bass as bass
from concourse import mybir

F32 = mybir.dt.float32
BF16 = mybir.dt.bfloat16
I32 = mybir.dt.int32
ALU = mybir.AluOpType
ACT = mybir.ActivationFunctionType

P = 128
R = 4
TILE = P * R
LOW = 512
SEED = 8
EPS = 1e-5
SKIP = 1 << 20
HEADS = 8


def build(nc, x, src, dst, edge_attr, W_msg, b_msg, W_upd, b_upd, gamma, beta, Wemb, Wq, bq, Wk, bk,
          Wv, bv, Wo, bo, ln1_g, ln1_b, W1, b1, W2, b2, ln2_g, ln2_b, out):
    N, E, L = x.shape[0], src.shape[0], Wq.shape[0]
    HD = P // HEADS
    NT = -(-N // TILE)
    NROWS = NT * TILE
    TAIL = (N - (NT - 1) * TILE) // R
    EC = -(-E // TILE)
    EROWS = EC * TILE
    T = EROWS // P
    EP = E // T
    assert N % R == 0 and N < NROWS and E % T == 0 and EC % 2 == 1 and NROWS <= P * LOW

    h_tab = nc.dram_tensor("h_tab", (NROWS, P), F32, kind="Internal").ap()
    y_tab = nc.dram_tensor("y_tab", (NROWS, P), F32, kind="Internal").ap()
    x1_tab = nc.dram_tensor("x1_tab", (NROWS, P), F32, kind="Internal").ap()
    msg_tab = nc.dram_tensor("msg_tab", (NROWS, P), F32, kind="Internal").ap()
    sorted_tab = nc.dram_tensor("sorted_tab", (EROWS, 4), I32, kind="Internal").ap()
    dst_line = nc.dram_tensor("dst_line", (EROWS + R,), I32, kind="Internal").ap()

    ctx = ExitStack()
    with ctx:
        def sb(name, shape, dt=F32, stack=ctx):
            return stack.enter_context(nc.sbuf_tensor(name, shape, dt))

        def sem(name):
            return ctx.enter_context(nc.semaphore(name))

        ps = ctx.enter_context(nc.psum_tensor("ps", [P, 8, 512], F32))

        ident = sb("ident", [P, P])
        ones = sb("ones", [P, 512])
        head_sum = sb("head_sum", [P, P])
        before = sb("before", [P, P])
        earlier = sb("earlier", [P, P])
        eps = sb("eps", [P, 1])
        w_msg = sb("w_msg", [P, 2, P])
        w_upd = sb("w_upd", [P, 2, P])
        w_emb = sb("w_emb", [P, P])
        NV = 9
        VQ, VK, VV, VO, VG1, VB1, VF0, VF1, VF2 = range(NV)
        vec_rows = sb("vec_rows", [P, P])
        vec_cols = sb("vec_cols", [P, L * NV + 1])
        layer_cols = sb("layer_cols", [P, NV])
        folded = sb("folded", [P, 6])
        b_upd_row = sb("b_upd_row", [P, P])
        gamma_row = sb("gamma_row", [P, P])
        beta_row = sb("beta_row", [P, P])
        bo0_row = sb("bo0_row", [P, P])
        g2_row = sb("g2_row", [P, P])
        b2_row = sb("b2_row", [P, P])
        bo_row = sb("bo_row", [P, P])
        ending = sb("ending", [P, R], I32)
        b_upd_wide = sb("b_upd_wide", [P, R, P])

        const_loaded = sem("const_loaded")
        pool_passed = sem("pool_passed")
        dve_passed = sem("dve_passed")
        consts_made = sem("consts_made")
        consts_step = sem("consts_step")
        edges_loaded = sem("edges_loaded")
        columns_made = sem("columns_made")
        columns_copied = sem("columns_copied")
        sort_prep = sem("sort_prep")
        one_hot = sem("one_hot")
        counted = sem("counted")
        base_step = sem("base_step")
        row_base = sem("row_base")
        seeded = sem("seeded")
        table_copied = sem("table_copied")
        table_added = sem("table_added")
        row_hot = sem("row_hot")
        rank_ready = sem("rank_ready")
        looked_up = sem("looked_up")
        place_step = sem("place_step")
        place_ready = sem("place_ready")
        payload_copied = sem("payload_copied")
        sorted_out = [sem(f"sorted_out{i}") for i in range(2)]
        sorted_done = sem("sorted_done")
        sorted_loaded = sem("sorted_loaded")
        dst_col_ready = sem("dst_col_ready")
        dst_line_out = sem("dst_line_out")
        dst_line_in = sem("dst_line_in")
        tables_step = sem("tables_step")
        tables_ready = sem("tables_ready")
        wide_made = sem("wide_made")
        msg_filled = sem("msg_filled")

        def named(k, names):
            return {n: sem(f"{k}_{n}") for n in names}

        edge = named("edge", ["idx", "idx_out", "turned", "turned_copy", "proj", "value", "sums", "den", "rows", "update",
                              "update_free"])
        m = edge | named("m", ["stats", "mean_var", "std", "rstd", "normed", "recip"])
        a = edge | named("a", ["key", "kq", "score", "clip", "exp", "recip", "attn"])
        gathered = [sem(f"gathered{i}") for i in range(2)]
        scattered = [sem(f"scattered{i}") for i in range(2)]
        m_done = sem("m_done")
        a_done = sem("a_done")

        node = named("node", ["stats", "mean_var", "std", "rstd", "normed", "turned", "turned_copy", "result",
                              "stored", "proj", "stats2", "mean_var2", "std2", "rstd2", "shift2", "normed2",
                              "scaled"])
        u = node | named("u", ["sum", "shifted", "joined"])
        b = node
        f = node | named("f", ["hidden", "relu", "ffn", "shifted"])
        u_loaded = [sem(f"u_loaded{i}") for i in range(8)]
        x1_loaded = [sem(f"x1_loaded{i}") for i in range(4)]
        n_loaded = [sem(f"n_loaded{i}") for i in range(4)]
        n_stored = [sem(f"n_stored{i}") for i in range(4)]
        weights_loaded = sem("weights_loaded")
        layer_step = sem("layer_step")
        folds_made = sem("folds_made")
        layer_ready = sem("layer_ready")

        with ExitStack() as sort_ctx:
            def st(name, shape, dt=F32):
                return sb(name, shape, dt, sort_ctx)
            low_hot = st("low_hot", [P, T, LOW], BF16)
            high_hot = st("high_hot", [P, T, P], BF16)
            dst_rows = st("dst_rows", [P, EROWS], I32)
            dst_i = st("dst_i", [P, T], I32)
            src_i = st("src_i", [P, T], I32)
            num_i = st("num_i", [P, T], I32)
            part_i = st("part_i", [P, T], I32)
            dst_c = st("dst_c", [P, T])
            high_c = st("high_c", [P, T])
            low_c = st("low_c", [P, T])
            payload = st("payload", [P, T, 4], I32)
            iota_i = st("iota_i", [P, LOW], I32)
            row_lo = st("row_lo", [P, 1])
            row_hi = st("row_hi", [P, 1])
            row_i = st("row_i", [P, 1], I32)
            table = st("table", [P, 2, LOW])
            counts = st("counts", [P, LOW])
            running = st("running", [P, LOW])
            row_start = st("row_start", [P, 1])
            in_range = st("in_range", [P, P])
            high_row = st("high_row", [P, 2, P])
            rank_in = st("rank_in", [P, 2])
            found = st("found", [P, 2])
            place = st("place", [P, 2], I32)
            load_out = st("load_out", [P, 2, 4], I32)

        wq, wk, wv, wo = (sb(f"w{n}", [P, P]) for n in "qkvo")
        w1 = sb("w1", [P, 2 * P])
        w2 = sb("w2", [P, 2, P])

        same = sb("same", [P, EROWS], BF16)
        src_idx = sb("src_idx", [P, EC, R], I32)
        dst_idx = sb("dst_idx", [P, EC, R], I32)
        edge_idx = sb("edge_idx", [P, EC, R], I32)
        last_idx = sb("last_idx", [P, EC, R], I32)

        with ExitStack() as table_ctx:
            def tb(name, shape, dt=F32):
                return sb(name, shape, dt, table_ctx)
            sorted_rows = tb("sorted_rows", [P, EC, R, 4], I32)
            dst_s = tb("dst_s", [P, EC, R], I32)
            dst_next = tb("dst_next", [P, EC, R], I32)
            dst_sorted = tb("dst_sorted", [P, EROWS], I32)
            same_next = tb("same_next", [P, EC, R])

        idx_a = [sb(f"idx_a{i}", [P, R], I32) for i in range(2)]
        idx_b = [sb(f"idx_b{i}", [P, R], I32) for i in range(2)]
        idx_c = [sb(f"idx_c{i}", [P, R], I32) for i in range(2)]
        rows_a = [sb(f"rows_a{i}", [P, R, P]) for i in range(2)]
        rows_b = [sb(f"rows_b{i}", [P, R, P]) for i in range(2)]
        upd = [sb(f"upd{i}", [P, R, P]) for i in range(2)]
        e_norm = sb("e_norm", [P, R, P])
        e_aT = sb("e_aT", [P, 512])
        e_bT = sb("e_bT", [P, 512])
        e_key = sb("e_key", [P, 512])
        e_kq = sb("e_kq", [P, 512])
        e_clip = sb("e_clip", [P, 512])
        e_exp = sb("e_exp", [P, 512])
        e_val = sb("e_val", [P, 512])
        e_sum = [sb(f"e_sum{i}", [P, 512]) for i in range(2)]
        e_den = [sb(f"e_den{i}", [P, 512]) for i in range(2)]
        e_rden = sb("e_rden", [P, 512])
        e_rinv = sb("e_rinv", [P, 512])
        e_attn = sb("e_attn", [P, 512])
        e_rc = sb("e_rc", [P, R])
        e_bn = sb("e_bn", [P, R, 6])
        e_mv = sb("e_mv", [P, R, 2])
        e_sd = sb("e_sd", [P, R])
        e_rs = sb("e_rs", [P, R])

        def ring(name, shape, dt=F32):
            return [sb(f"{name}{i}", shape, dt) for i in range(4)]
        n_in = [sb(f"n_in{i}", [P, R, P]) for i in range(8)]
        n_add = ring("n_add", [P, R, P])
        n_norm = ring("n_norm", [P, R, P])
        n_T = ring("n_T", [P, 512])
        n_relu = ring("n_relu", [P, 2, 512])
        n_sum = ring("n_sum", [P, R, P])
        n_norm2 = ring("n_norm2", [P, R, P])
        n_scaled = ring("n_scaled", [P, R, P])
        n_out = ring("n_out", [P, R, P])
        n_bn = ring("n_bn", [P, R, 6])
        n_mv = ring("n_mv", [P, R, 2])
        n_sd = ring("n_sd", [P, R])
        n_rs = ring("n_rs", [P, R])
        n_bn2 = ring("n_bn2", [P, R, 6])
        n_mv2 = ring("n_mv2", [P, R, 2])
        n_sd2 = ring("n_sd2", [P, R])
        n_rs2 = ring("n_rs2", [P, R])
        n_sh2 = ring("n_sh2", [P, R])

        node_view = lambda tab: tab.rearrange("(n p j) f -> n p (j f)", p=P, j=R)
        flat = lambda t: t[:, :, :].rearrange("p j f -> p (j f)")
        wide = lambda row: row[:, :].unsqueeze(1).to_broadcast([P, R, P])
        bank = lambda n: ps[:, n, :]
        blocks = lambda n: ps[:, n, :].rearrange("p (j f) -> p j f", j=R)
        by_row = lambda t, j: t.rearrange("f (p j) -> f j p", j=R)[:, j, :]

        done = lambda g: g + (SEED + 1)
        freed = lambda g, depth: g + (SEED + 1 - depth)
        uses = lambda q, n, depth: (n - q + depth - 1) // depth

        def tile_at(i, s, lag, depth=4):
            if isinstance(i, int):
                n = depth * i + s - lag
                return (n // depth, n % depth) if 0 <= n < NT else None
            return i + (s - lag) // depth, (s - lag) % depth

        def pipeline(eng, lags, step, depth=4):
            first, end = -(-lags // depth), (NT - 1) // depth
            if end <= first:
                first = end = 0
            for n in range(depth * first):
                step(n // depth, n % depth)
            if end:
                with eng.Fori(first, end) as i:
                    for s in range(depth):
                        step(i, s)
            for n in range(depth * end, NT + lags):
                step(n // depth, n % depth)

        def chunks(eng, step):
            step(0, 0, 0)
            if EC > 1:
                with eng.Fori(0, (EC - 1) // 2) as i:
                    step(2 * i + 1, 1, i)
                    step(2 * i + 2, 0, i + 1)

        def wait_alone(eng, s, value, passed):
            eng.wait_ge(s, value)
            eng.sem_inc(passed, 1)

        block = ctx.enter_context(nc.Block())

        @block.sync
        def _(sp):
            loads = [(w_msg[:, :, :], W_msg.rearrange("(c k) f -> k c f", k=P)),
                     (w_upd[:, :, :], W_upd.rearrange("(c k) f -> k c f", k=P)),
                     (w_emb[:, :], Wemb)]
            for n, v in ((VQ, bq), (VK, bk), (VV, bv), (VO, bo), (VG1, ln1_g), (VB1, ln1_b),
                         (VF0, b1[:, 0:P]), (VF1, b1[:, P:2 * P]), (VF2, b2)):
                loads.append((vec_rows[n * L:(n + 1) * L, :], v))
            loads.append((vec_rows[NV * L:NV * L + 1, :], b_msg.unsqueeze(0)))
            for t, v in ((b_upd_row, b_upd), (gamma_row, gamma), (beta_row, beta), (bo0_row, bo[0])):
                loads.append((t[:, :], v.partition_broadcast(P)))
            sp.wait_ge(consts_made, 1)
            sp.dma_start(dst_i[0:EP, :], dst.rearrange("(p t) -> p t", t=T)).then_inc(edges_loaded, 16)
            sp.dma_start(src_i[0:EP, :], src.rearrange("(p t) -> p t", t=T)).then_inc(edges_loaded, 16)
            sp.dma_start(dst_rows[:, 0:E], dst.partition_broadcast(P)).then_inc(edges_loaded, 16)
            for t, v in loads:
                sp.dma_start(t, v).then_inc(const_loaded, 16)

            sp.wait_ge(wide_made, 1)
            with sp.Fori(0, NT) as n:
                sp.dma_start(node_view(msg_tab)[n], flat(b_upd_wide)).then_inc(msg_filled, 16)

            sp.wait_ge(sorted_done, T)
            sp.dma_start(sorted_rows[:, :, :, :].rearrange("p c j w -> p c (j w)"),
                         sorted_tab.rearrange("(c p j) w -> p c (j w)", p=P, j=R)).then_inc(sorted_loaded, 16)
            sp.wait_ge(dst_col_ready, 2)
            sp.dma_start(dst_line[0:EROWS].rearrange("(c p j) -> p c j", p=P, j=R),
                         dst_s[:, :, :]).then_inc(dst_line_out, 16)
            sp.dma_start(dst_line[EROWS:EROWS + R].unsqueeze(0), ending[0:1, :]).then_inc(dst_line_out, 16)
            sp.wait_ge(dst_line_out, 32)
            sp.dma_start(dst_sorted[:, :], dst_line[0:EROWS].partition_broadcast(P)).then_inc(dst_line_in, 16)
            sp.dma_start(dst_next[:, :, :], dst_line[1:EROWS + 1].rearrange("(c p j) -> p c j", p=P, j=R)
                         ).then_inc(dst_line_in, 16)

            def load(dst_t, tab, n, is_tail, s):
                if is_tail:
                    rows = tab[(NT - 1) * TILE:N, :].rearrange("(p j) f -> p (j f)", j=R)
                    sp.dma_start(flat(dst_t)[0:TAIL, :], rows).then_inc(s, 16)
                else:
                    sp.dma_start(flat(dst_t), node_view_full(tab, n)).then_inc(s, 16)

            def node_view_full(tab, n):
                return tab[0:(tab.shape[0] // TILE) * TILE, :].rearrange("(n p j) f -> n p (j f)", p=P, j=R)[n]

            def number(t):
                return 4 * t[0] + t[1]

            sp.wait_ge(m_done, 1)
            sp.sem_inc(node["stored"], SEED)

            def update_step(i, s):
                t = tile_at(i, s, 0, 8)
                if t:
                    n = 8 * t[0] + t[1]
                    tail = isinstance(n, int) and n == NT - 1
                    sp.wait_ge(u["result"], freed(n, 8))
                    load(n_in[t[1]], x, n, tail, u_loaded[t[1]])
                    sp.wait_ge(u["sum"], freed(n, 4))
                    sp.dma_start(flat(n_add[t[1] % 4]), node_view(msg_tab)[n]).then_inc(u_loaded[t[1]], 16)
                t = tile_at(i, s, 5, 8)
                if t:
                    n = 8 * t[0] + t[1]
                    sp.wait_ge(u["result"], done(n))
                    sp.dma_start(node_view(x1_tab)[n], flat(n_out[t[1] % 4])).then_inc(n_stored[t[1] % 4], 16)
                t = tile_at(i, s, 6, 8)
                if t:
                    sp.wait_ge(n_stored[t[1] % 4], 16 * (2 * t[0] + t[1] // 4 + 1))
                    sp.sem_inc(u["stored"], 1)
            pipeline(sp, 7, update_step, 8)

            def embed_step(i, s):
                t = tile_at(i, s, 0)
                if t:
                    n = number(t)
                    sp.wait_ge(b["normed"], freed(NT + n, 4))
                    sp.dma_start(flat(n_in[t[1]]), node_view(x1_tab)[n]).then_inc(n_loaded[t[1]], 16)
                t = tile_at(i, s, 3)
                if t:
                    n = number(t)
                    sp.wait_ge(b["result"], done(NT + n))
                    sp.dma_start(node_view(h_tab)[n], flat(n_out[t[1]])).then_inc(n_stored[t[1]], 16)
                    sp.dma_start(node_view(y_tab)[n], flat(n_out[t[1]])).then_inc(n_stored[t[1]], 16)
                t = tile_at(i, s, 4)
                if t:
                    sp.wait_ge(n_stored[t[1]], 16 * uses(t[1], NT, 4) + 32 * (t[0] + 1))
                    sp.sem_inc(b["stored"], 1)
            pipeline(sp, 5, embed_step)

            def layer(l, is_last):
                for t, v in ((wq[:, :], Wq[l]), (wk[:, :], Wk[l]), (wv[:, :], Wv[l]), (wo[:, :], Wo[l]),
                             (w1[:, :], W1[l]), (w2[:, :, :], W2[l].rearrange("(c k) f -> k c f", k=P)),
                             (g2_row[:, :], ln2_g[l].partition_broadcast(P)),
                             (b2_row[:, :], ln2_b[l].partition_broadcast(P))):
                    sp.dma_start(t, v).then_inc(weights_loaded, 16)
                if not is_last:
                    sp.dma_start(bo_row[:, :], bo[l + 1].partition_broadcast(P)).then_inc(weights_loaded, 16)
                sp.wait_ge(a_done, l + 1)
                g0 = (l + 2) * NT

                def step(i, s):
                    t = tile_at(i, s, 0)
                    if t:
                        n = number(t)
                        sp.wait_ge(f["normed"], freed(g0 + n, 4))
                        sp.dma_start(flat(n_in[t[1]]), node_view(y_tab)[n]).then_inc(n_loaded[t[1]], 16)
                    t = tile_at(i, s, 3)
                    if t and is_last:
                        n = number(t)
                        sp.wait_ge(f["result"], freed(g0 + n, 4))
                        sp.dma_start(flat(n_add[t[1]]), node_view(x1_tab)[n]).then_inc(x1_loaded[t[1]], 16)
                    t = tile_at(i, s, 5)
                    if t:
                        n = number(t)
                        sp.wait_ge(f["result"], done(g0 + n))
                        if not is_last:
                            sp.dma_start(node_view(h_tab)[n], flat(n_out[t[1]])).then_inc(n_stored[t[1]], 16)
                            sp.dma_start(node_view(y_tab)[n], flat(n_out[t[1]])).then_inc(n_stored[t[1]], 16)
                        elif isinstance(n, int) and n == NT - 1:
                            rows = out[(NT - 1) * TILE:N, :].rearrange("(p j) f -> p (j f)", j=R)
                            sp.dma_start(rows, flat(n_out[t[1]])[0:TAIL, :]).then_inc(n_stored[t[1]], 32)
                        else:
                            sp.dma_start(node_view_full(out, n), flat(n_out[t[1]])).then_inc(n_stored[t[1]], 32)
                    t = tile_at(i, s, 6)
                    if t:
                        sp.wait_ge(n_stored[t[1]], 48 * uses(t[1], NT, 4) + 32 * (l * uses(t[1], NT, 4) + t[0] + 1))
                        sp.sem_inc(f["stored"], 1)
                pipeline(sp, 7, step)

            with sp.Fori(0, L - 1) as l:
                layer(l, False)
            layer(L - 1, True)

        @block.gpsimd
        def _(pool):
            made = [0]

            def step(ins):
                made[0] += 1
                ins.then_inc(consts_step, 1)
                pool.wait_ge(consts_step, made[0])

            step(pool.memset(dst_i[:, :], N))
            step(pool.memset(src_i[:, :], 0))
            step(pool.memset(dst_rows[:, E:EROWS], N))
            pool.sem_inc(consts_made, 1)
            step(pool.memset(ones[:, :], 1.0))
            step(pool.memset(ident[:, :], 0.0))
            step(pool.affine_select(out=ident[:, :], in_=ident[:, :], compare_op=ALU.not_equal, fill=1.0, base=0,
                                    pattern=[[-1, P]], channel_multiplier=1))
            step(pool.affine_select(out=before[:, :], in_=ones[:, 0:P], compare_op=ALU.is_ge, fill=0.0, base=-1,
                                    pattern=[[1, P]], channel_multiplier=-1))
            step(pool.affine_select(out=earlier[:, :], in_=ones[:, 0:P], compare_op=ALU.is_ge, fill=0.0, base=-1,
                                    pattern=[[-1, P]], channel_multiplier=1))
            hs = head_sum[:, :].rearrange("p (h d) -> p h d", h=HEADS)
            step(pool.memset(head_sum[:, :], float(HD) ** -0.5))
            step(pool.affine_select(out=hs, in_=hs, compare_op=ALU.is_ge, fill=0.0, base=0,
                                    pattern=[[-HD, HEADS], [0, HD]], channel_multiplier=1))
            step(pool.affine_select(out=hs, in_=hs, compare_op=ALU.is_ge, fill=0.0, base=HD - 1,
                                    pattern=[[HD, HEADS], [0, HD]], channel_multiplier=-1))
            step(pool.memset(eps[:, :], EPS))
            step(pool.iota(iota_i[:, :], pattern=[[1, LOW]], base=0, channel_multiplier=0))
            step(pool.iota(num_i[:, :], pattern=[[1, T]], base=0, channel_multiplier=T))
            step(pool.iota(row_i[:, :], pattern=[[0, 1]], base=0, channel_multiplier=LOW))
            step(pool.memset(ending[:, :], -1))
            pool.sem_inc(consts_made, 1)

            pool.sem_inc(payload_copied, SEED)

            def place_out(t, q, use, first):
                wait_alone(pool, place_ready, t + 1, pool_passed)
                if not first:
                    wait_alone(pool, sorted_out[q], 16 * use, pool_passed)
                pool.tensor_copy(load_out[:, q, :], payload[:, t, :] if isinstance(t, int) else
                                 payload[:, bass.ds(t, 1), :].rearrange("p a w -> p (a w)")
                                 ).then_inc(payload_copied, 1)
                wait_alone(pool, payload_copied, done(t), pool_passed)
                pool.indirect_dma_start(out=sorted_tab[:, :],
                                        out_offset=bass.IndirectOffsetOnAxis(ap=place[:, q:q + 1], axis=0),
                                        in_=load_out[:, q, :], in_offset=None).then_inc(sorted_out[q], 16)
            place_out(0, 0, 0, True)
            place_out(1, 1, 0, True)
            with pool.Fori(1, T // 2) as i:
                for q in range(2):
                    place_out(2 * i + q, q, i, False)
                    pool.sem_inc(sorted_done, 1)
            for q in range(2):
                wait_alone(pool, sorted_out[q], 16 * (T // 2), pool_passed)
                pool.sem_inc(sorted_done, 1)

            pool.wait_ge(tables_ready, 1)
            pool.wait_ge(msg_filled, 16 * NT)

            def edge_phase(s, tab_a, ia, tab_b, ib, out_tab, k):
                g0 = k * EC

                def cols(t, c):
                    return t[:, c, :] if isinstance(c, int) else \
                        t[:, bass.ds(c, 1), :].rearrange("p a j -> p (a j)")

                def gather(c, q, use):
                    wait_alone(pool, s["update"], freed(g0 + c, 2), pool_passed)
                    pool.tensor_copy(idx_a[q][:, :], cols(ia, c))
                    pool.tensor_copy(idx_b[q][:, :], cols(ib, c)).then_inc(s["idx"], 1)
                    wait_alone(pool, s["idx"], g0 + c + 1, pool_passed)
                    for t, ix, rows in ((tab_a, idx_a, rows_a), (tab_b, idx_b, rows_b)):
                        for j in range(R):
                            pool.indirect_dma_start(
                                out=rows[q][:, j, :], out_offset=None, in_=t[:, :],
                                in_offset=bass.IndirectOffsetOnAxis(ap=ix[q][:, j:j + 1], axis=0)
                            ).then_inc(gathered[q], 16)

                def scatter(c, q, use):
                    pool.tensor_copy(idx_c[q][:, :], cols(last_idx, c)).then_inc(s["idx_out"], 1)
                    wait_alone(pool, s["idx_out"], g0 + c + 1, pool_passed)
                    wait_alone(pool, s["update"], done(g0 + c), pool_passed)
                    for j in range(R):
                        pool.indirect_dma_start(
                            out=out_tab[:, :],
                            out_offset=bass.IndirectOffsetOnAxis(ap=idx_c[q][:, j:j + 1], axis=0),
                            in_=upd[q][:, j, :], in_offset=None, bounds_check=NROWS - 1, oob_is_err=False
                        ).then_inc(scattered[q], 16)

                def landed(q, use):
                    wait_alone(pool, scattered[q], 64 * (k * uses(q, EC, 2) + use + 1), pool_passed)
                    pool.sem_inc(s["update_free"], 1)

                def lagged(c, q, use):
                    scatter(c - 2, q, use - 1)
                    gather(c, q, use)
                    landed(q, use - 1)
                gather(0, 0, 0)
                if EC > 1:
                    gather(1, 1, 0)
                    lagged(2, 0, 1)
                if EC > 3:
                    with pool.Fori(1, (EC - 1) // 2) as i:
                        lagged(2 * i + 1, 1, i)
                        lagged(2 * i + 2, 0, i + 1)
                for c in range(max(EC - 2, 0), EC):
                    scatter(c, c % 2, c // 2)
                    landed(c % 2, c // 2)

            pool.sem_inc(m["update_free"], SEED)
            edge_phase(m, x, src_idx, edge_attr, edge_idx, msg_tab, 0)
            pool.sem_inc(m_done, 1)

            pool.sem_inc(u["scaled"], SEED)
            pool.sem_inc(u["shifted"], SEED)

            def update_step(i, s):
                t = tile_at(i, s, 4, 8)
                if t:
                    n, q = 8 * t[0] + t[1], t[1] % 4
                    wait_alone(pool, u["normed2"], done(n), pool_passed)
                    wait_alone(pool, u["joined"], freed(n, 4), pool_passed)
                    pool.tensor_tensor(out=n_norm2[q][:, :, :], in0=n_norm2[q][:, :, :], in1=wide(gamma_row),
                                       op=ALU.mult).then_inc(u["scaled"], 1)
                    wait_alone(pool, u["scaled"], done(n), pool_passed)
                    pool.tensor_tensor(out=n_scaled[q][:, :, :], in0=n_norm2[q][:, :, :], in1=wide(beta_row),
                                       op=ALU.add).then_inc(u["shifted"], 1)
            pipeline(pool, 7, update_step, 8)

            pool.sem_inc(f["scaled"], NT)
            pool.sem_inc(f["shifted"], SEED)

            def layer(l, is_last):
                wait_alone(pool, f["stored"], (l + 2) * NT + SEED, pool_passed)
                edge_phase(a, h_tab, src_idx, h_tab, dst_idx, y_tab, l + 1)
                pool.sem_inc(a_done, 1)
                g0 = (l + 2) * NT

                def step(i, s):
                    t = tile_at(i, s, 4)
                    if t:
                        g, q = g0 + (4 * t[0] + t[1]), t[1]
                        wait_alone(pool, f["normed2"], done(g), pool_passed)
                        pool.tensor_tensor(out=n_scaled[q][:, :, :], in0=n_norm2[q][:, :, :], in1=wide(g2_row),
                                           op=ALU.mult).then_inc(f["scaled"], 1)
                        wait_alone(pool, f["scaled"], done(g), pool_passed)
                        wait_alone(pool, f["stored"], freed(g, 4), pool_passed)
                        if is_last:
                            pool.tensor_tensor(out=n_norm2[q][:, :, :], in0=n_scaled[q][:, :, :], in1=wide(b2_row),
                                               op=ALU.add).then_inc(f["shifted"], 1)
                            wait_alone(pool, f["shifted"], done(4 * t[0] + t[1]), pool_passed)
                            wait_alone(pool, x1_loaded[q], 16 * (t[0] + 1), pool_passed)
                            pool.tensor_tensor(out=n_out[q][:, :, :], in0=n_norm2[q][:, :, :],
                                               in1=n_add[q][:, :, :], op=ALU.add).then_inc(f["result"], 1)
                        else:
                            pool.tensor_tensor(out=n_out[q][:, :, :], in0=n_scaled[q][:, :, :], in1=wide(b2_row),
                                               op=ALU.add).then_inc(f["result"], 1)
                pipeline(pool, 7, step)

            with pool.Fori(0, L - 1) as l:
                layer(l, False)
            layer(L - 1, True)

        @block.tensor
        def _(pe):
            pe.wait_ge(consts_made, 2)
            pe.wait_ge(const_loaded, 16 * 17)
            pe.transpose(ps[:, 7, 0:L * NV + 1], vec_rows[0:L * NV + 1, :],
                         ident[0:L * NV + 1, 0:L * NV + 1]).then_inc(columns_made, 1)

            def count(t, start=False, stop=False):
                pe.wait_ge(one_hot, t + 1)
                return pe.matmul(ps[:, 0, :], one(high_hot, t), one(low_hot, t), start=start, stop=stop,
                                 skip_group_check=True)

            def one(t3, t):
                return t3[:, t, :] if isinstance(t, int) else \
                    t3[:, bass.ds(t, 1), :].rearrange("p a f -> p (a f)")
            count(0, start=True)
            with pe.Fori(1, T - 1) as t:
                count(t)
            count(T - 1, stop=True).then_inc(counted, 1)
            pe.wait_ge(base_step, 2)
            pe.matmul(ps[:, 4, 0:1], before[:, :], running[:, LOW - 1:LOW], start=True,
                      stop=True).then_inc(row_base, 1)
            pe.wait_ge(base_step, 5)
            pe.matmul(ps[:, 1, :], ident[:, :], counts[:, :], start=True, stop=False,
                      skip_group_check=True).then_inc(table_added, 1)

            def look_up(t, q, first):
                pe.wait_ge(table_copied, t + 1)
                pe.wait_ge(row_hot, t + 1)
                pe.matmul(ps[:, 1, :], one(high_hot, t), one(low_hot, t), start=False, stop=False,
                          skip_group_check=True).then_inc(table_added, 1)
                if not first:
                    pe.wait_ge(place_ready, t - 1)
                pe.matmul(ps[:, 2 + q, :], high_row[:, q, :], table[:, q, :], start=True,
                          stop=True).then_inc(looked_up, 1)
            look_up(0, 0, True)
            look_up(1, 1, True)
            with pe.Fori(1, T // 2) as i:
                for q in range(2):
                    look_up(2 * i + q, q, False)

            for k in ("turned", "proj", "rows"):
                pe.sem_inc(edge[k], SEED)

            def message(c, q, use):
                pe.wait_ge(m["normed"], done(c))
                pe.wait_ge(m["turned_copy"], freed(c, 1))
                for j in range(R):
                    pe.transpose(by_row(bank(0), j), e_norm[:, j, :], ident[:, :])
                for j in range(R):
                    tr = pe.transpose(by_row(bank(1), j), rows_b[q][:, j, :], ident[:, :])
                tr.then_inc(m["turned"], 1)
                pe.wait_ge(m["turned_copy"], done(c))
                pe.wait_ge(m["value"], freed(c, 1))
                pe.matmul(bank(2), w_msg[:, 0, :], e_aT[:, :], start=True, stop=False)
                pe.matmul(bank(2), w_msg[:, 1, :], e_bT[:, :], start=False, stop=True).then_inc(m["proj"], 1)
                pe.wait_ge(m["sums"], done(c))
                pe.wait_ge(m["update"], freed(c, 1))
                for j in range(R):
                    pe.matmul(blocks(6)[:, j, :], by_row(e_sum[q][:, :], j), w_upd[:, 1, :], start=True, stop=True)
                for j in range(R):
                    mm = pe.matmul(ps[:, 7, 2 * j:2 * j + 1], by_row(e_den[q][:, :], j), ident[:, 0:1],
                                   start=True, stop=True)
                mm.then_inc(m["rows"], 1)
            chunks(pe, message)

            for k in ("turned", "proj"):
                pe.sem_inc(node[k], SEED)

            def turn(s, n, q):
                pe.wait_ge(s["normed"], done(n))
                pe.wait_ge(s["turned_copy"], freed(n, 2))
                for j in range(R):
                    tr = pe.transpose(blocks(q % 2)[:, j, :], n_norm[q][:, j, :], ident[:, :])
                tr.then_inc(s["turned"], 1)

            def update_step(i, s):
                t = tile_at(i, s, 3, 8)
                if t:
                    n, q = 8 * t[0] + t[1], t[1] % 4
                    pe.wait_ge(u["turned_copy"], done(n))
                    pe.wait_ge(u["sum"], freed(n, 2))
                    for j in range(R):
                        mm = pe.matmul(blocks(6 + q % 2)[:, j, :], n_T[q][:, j * P:(j + 1) * P], w_upd[:, 0, :],
                                       start=True, stop=True)
                    mm.then_inc(u["proj"], 1)
                t = tile_at(i, s, 2, 8)
                if t:
                    turn(u, 8 * t[0] + t[1], t[1] % 4)
            pipeline(pe, 7, update_step, 8)

            def embed_step(i, s):
                t = tile_at(i, s, 3)
                if t:
                    n, q = NT + (4 * t[0] + t[1]), t[1]
                    pe.wait_ge(b["turned_copy"], done(n))
                    pe.wait_ge(b["result"], freed(n, 2))
                    for j in range(R):
                        mm = pe.matmul(blocks(6 + q % 2)[:, j, :], n_T[q][:, j * P:(j + 1) * P], w_emb[:, :],
                                       start=True, stop=True)
                    mm.then_inc(b["proj"], 1)
                t = tile_at(i, s, 2)
                if t:
                    turn(b, NT + (4 * t[0] + t[1]), t[1])
            pipeline(pe, 5, embed_step)

            pe.sem_inc(a["score"], EC + SEED)
            for k in ("hidden", "ffn"):
                pe.sem_inc(f[k], 2 * NT + SEED)

            def layer(l, is_last):
                pe.wait_ge(layer_step, 2 * l + 1)
                for n, (w, v) in enumerate(((wq[:, :], VO), (wk[:, :], VO), (wv[:, :], VO),
                                            (w1[:, 0:P], VF2), (w1[:, P:2 * P], VF2))):
                    mm = pe.matmul(ps[:, 7, 2 * n:2 * n + 1], w, layer_cols[:, v:v + 1], start=True, stop=True)
                mm.then_inc(folds_made, 1)

                def attend(c, q, use):
                    g = (l + 1) * EC + c
                    pe.wait_ge(gathered[q], 128 * ((l + 1) * uses(q, EC, 2) + use + 1))
                    pe.wait_ge(a["turned_copy"], freed(g, 1))
                    for j in range(R):
                        pe.transpose(by_row(bank(0), j), rows_a[q][:, j, :], ident[:, :])
                    for j in range(R):
                        tr = pe.transpose(by_row(bank(1), j), rows_b[q][:, j, :], ident[:, :])
                    tr.then_inc(a["turned"], 1)
                    pe.wait_ge(a["turned_copy"], done(g))
                    pe.wait_ge(a["value"], freed(g, 1))
                    pe.matmul(bank(2), wk[:, :], e_aT[:, :], start=True, stop=True)
                    pe.matmul(bank(3), wq[:, :], e_bT[:, :], start=True, stop=True)
                    pe.matmul(bank(4), wv[:, :], e_aT[:, :], start=True, stop=True).then_inc(a["proj"], 1)
                    pe.wait_ge(a["kq"], done(g))
                    pe.matmul(bank(5), head_sum[:, :], e_kq[:, :], start=True, stop=True).then_inc(a["score"], 1)
                    pe.wait_ge(a["attn"], done(g))
                    pe.wait_ge(a["update"], freed(g, 1))
                    for j in range(R):
                        mm = pe.matmul(blocks(6)[:, j, :], by_row(e_attn[:, :], j), wo[:, :], start=True, stop=True)
                    mm.then_inc(a["rows"], 1)
                chunks(pe, attend)

                g0 = (l + 2) * NT

                def step(i, s):
                    t = tile_at(i, s, 4)
                    if t:
                        g, q = g0 + (4 * t[0] + t[1]), t[1]
                        pe.wait_ge(f["relu"], done(g))
                        pe.wait_ge(f["normed2"], freed(g, 2))
                        for j in range(R):
                            o, c = blocks(6 + q % 2)[:, j, :], slice(j * P, (j + 1) * P)
                            pe.matmul(o, n_T[q][:, c], ident[:, :], start=True, stop=False)
                            pe.matmul(o, n_relu[q][:, 0, c], w2[:, 0, :], start=False, stop=False)
                            mm = pe.matmul(o, n_relu[q][:, 1, c], w2[:, 1, :], start=False, stop=True)
                        mm.then_inc(f["ffn"], 1)
                    t = tile_at(i, s, 2)
                    if t:
                        turn(f, g0 + (4 * t[0] + t[1]), t[1])
                    t = tile_at(i, s, 3)
                    if t:
                        g, q = g0 + (4 * t[0] + t[1]), t[1]
                        pe.wait_ge(f["turned_copy"], done(g))
                        pe.wait_ge(f["relu"], freed(g, 2))
                        for k in range(2):
                            mm = pe.matmul(bank(2 + 2 * (q % 2) + k), w1[:, k * P:(k + 1) * P], n_T[q][:, :],
                                           start=True, stop=True)
                        mm.then_inc(f["hidden"], 1)
                pipeline(pe, 7, step)

            with pe.Fori(0, L - 1) as l:
                layer(l, False)
            layer(L - 1, True)

        @block.scalar
        def _(act):
            def copy_table(t, q):
                act.wait_ge(table_added, t + 1)
                if not isinstance(t, int) or t >= 2:
                    act.wait_ge(looked_up, t - 1)
                act.copy(table[:, q, :], ps[:, 1, :]).then_inc(table_copied, 1)
            copy_table(0, 0)
            copy_table(1, 1)
            with act.Fori(1, T // 2) as i:
                for q in range(2):
                    copy_table(2 * i + q, q)

            for k in ("std", "turned_copy", "value"):
                act.sem_inc(m[k], SEED)

            def message(c, q, use):
                act.wait_ge(m["mean_var"], done(c))
                act.activation(e_sd[:, :], e_mv[:, :, 1], ACT.Sqrt, bias=eps[:, 0:1]).then_inc(m["std"], 1)
                act.wait_ge(m["turned"], done(c))
                act.wait_ge(m["proj"], freed(c, 1))
                act.activation(e_aT[:, :], bank(0), ACT.Relu)
                act.copy(e_bT[:, :], bank(1)).then_inc(m["turned_copy"], 1)
                act.wait_ge(m["proj"], done(c))
                act.wait_ge(m["sums"], freed(c, 1))
                act.activation(e_val[:, :], bank(2), ACT.Relu, bias=vec_cols[:, L * NV:L * NV + 1]
                               ).then_inc(m["value"], 1)
            act.wait_ge(columns_copied, 1)
            chunks(act, message)

            for k in ("std", "turned_copy", "std2", "normed2"):
                act.sem_inc(u[k], SEED)

            def std(s, key, g, q, mv, sd):
                act.wait_ge(s["mean_var" + key], done(g))
                act.activation(sd[q][:, :], mv[q][:, :, 1], ACT.Sqrt, bias=eps[:, 0:1]).then_inc(s["std" + key], 1)

            def update_step(i, s):
                t = tile_at(i, s, 4, 8)
                if t:
                    n, q = 8 * t[0] + t[1], t[1] % 4
                    std(u, "2", n, q, n_mv2, n_sd2)
                t = tile_at(i, s, 2, 8)
                if t:
                    n, q = 8 * t[0] + t[1], t[1] % 4
                    act.wait_ge(u["turned"], done(n))
                    act.wait_ge(u["proj"], freed(n, 4))
                    act.activation(n_T[q][:, :], bank(q % 2), ACT.Relu).then_inc(u["turned_copy"], 1)
                t = tile_at(i, s, 4, 8)
                if t:
                    n, q = 8 * t[0] + t[1], t[1] % 4
                    act.wait_ge(u["shift2"], done(n))
                    act.wait_ge(u["shifted"], freed(n, 4))
                    for j in range(R):
                        ins = act.activation(n_norm2[q][:, j, :], n_sum[q][:, j, :], ACT.Identity,
                                             bias=n_sh2[q][:, j:j + 1], scale=n_rs2[q][:, j:j + 1])
                    ins.then_inc(u["normed2"], 1)
                t = tile_at(i, s, 1, 8)
                if t:
                    std(u, "", 8 * t[0] + t[1], t[1] % 4, n_mv, n_sd)
            pipeline(act, 7, update_step, 8)

            def embed_step(i, s):
                t = tile_at(i, s, 2)
                if t:
                    n, q = NT + (4 * t[0] + t[1]), t[1]
                    act.wait_ge(b["turned"], done(n))
                    act.wait_ge(b["proj"], freed(n, 4))
                    act.activation(n_T[q][:, :], bank(q % 2), ACT.Relu).then_inc(b["turned_copy"], 1)
                t = tile_at(i, s, 1)
                if t:
                    std(b, "", NT + (4 * t[0] + t[1]), t[1], n_mv, n_sd)
            pipeline(act, 5, embed_step)

            for k in ("key", "exp"):
                act.sem_inc(a[k], EC + SEED)
            act.sem_inc(f["relu"], 2 * NT + SEED)
            for k in ("std2", "normed2"):
                act.sem_inc(f[k], NT)

            def layer(l, is_last):
                act.wait_ge(layer_ready, l + 1)

                def attend(c, q, use):
                    g = (l + 1) * EC + c
                    act.wait_ge(a["turned"], done(g))
                    act.wait_ge(a["proj"], freed(g, 1))
                    act.copy(e_aT[:, :], bank(0))
                    act.copy(e_bT[:, :], bank(1)).then_inc(a["turned_copy"], 1)
                    act.wait_ge(a["proj"], done(g))
                    act.wait_ge(a["kq"], freed(g, 1))
                    act.activation(e_key[:, :], bank(2), ACT.Identity, bias=folded[:, 1:2]).then_inc(a["key"], 1)
                    act.wait_ge(a["clip"], done(g))
                    act.wait_ge(a["sums"], freed(g, 1))
                    act.activation(e_exp[:, :], e_clip[:, :], ACT.Exp).then_inc(a["exp"], 1)
                chunks(act, attend)

                g0 = (l + 2) * NT

                def step(i, s):
                    t = tile_at(i, s, 5)
                    if t:
                        std(f, "2", g0 + (4 * t[0] + t[1]), t[1], n_mv2, n_sd2)
                    t = tile_at(i, s, 2)
                    if t:
                        g, q = g0 + (4 * t[0] + t[1]), t[1]
                        act.wait_ge(f["turned"], done(g))
                        act.wait_ge(f["ffn"], freed(g, 4))
                        act.activation(n_T[q][:, :], bank(q % 2), ACT.Identity, bias=folded[:, 5:6],
                                       scale=layer_cols[:, VG1:VG1 + 1]).then_inc(f["turned_copy"], 1)
                    t = tile_at(i, s, 5)
                    if t:
                        g, q = g0 + (4 * t[0] + t[1]), t[1]
                        act.wait_ge(f["shift2"], done(g))
                        act.wait_ge(f["result"], freed(g, 4))
                        for j in range(R):
                            ins = act.activation(n_norm2[q][:, j, :], blocks(6 + q % 2)[:, j, :], ACT.Identity,
                                                 bias=n_sh2[q][:, j:j + 1], scale=n_rs2[q][:, j:j + 1])
                        ins.then_inc(f["normed2"], 1)
                    t = tile_at(i, s, 1)
                    if t:
                        std(f, "", g0 + (4 * t[0] + t[1]), t[1], n_mv, n_sd)
                    t = tile_at(i, s, 3)
                    if t:
                        g, q = g0 + (4 * t[0] + t[1]), t[1]
                        act.wait_ge(f["hidden"], done(g))
                        for k in range(2):
                            ins = act.activation(n_relu[q][:, k, :], bank(2 + 2 * (q % 2) + k), ACT.Relu,
                                                 bias=folded[:, 3 + k:4 + k])
                        ins.then_inc(f["relu"], 1)
                pipeline(act, 7, step)

            with act.Fori(0, L - 1) as l:
                layer(l, False)
            layer(L - 1, True)

        @block.vector
        def _(dve):
            dve.wait_ge(const_loaded, 16 * 17)
            dve.tensor_copy(b_upd_wide[:, :, :], wide(b_upd_row)).then_inc(wide_made, 1)
            dve.wait_ge(columns_made, 1)
            dve.tensor_copy(vec_cols[:, :], ps[:, 7, 0:L * NV + 1]).then_inc(columns_copied, 1)

            prepared = [0]

            def prep(ins):
                prepared[0] += 1
                ins.then_inc(sort_prep, 1)
                dve.wait_ge(sort_prep, prepared[0])
            dve.wait_ge(consts_made, 2)
            dve.wait_ge(edges_loaded, 48)
            prep(dve.tensor_scalar(part_i[:, :], dst_i[:, :], LOW - 1, None, ALU.bitwise_and))
            prep(dve.tensor_copy(low_c[:, :], part_i[:, :]))
            prep(dve.tensor_copy(dst_c[:, :], dst_i[:, :]))
            prep(dve.tensor_tensor(high_c[:, :], dst_c[:, :], low_c[:, :], ALU.subtract))
            prep(dve.tensor_copy(row_lo[:, :], row_i[:, :]))
            prep(dve.tensor_scalar(row_hi[:, :], row_lo[:, :], float(LOW), None, ALU.add))
            prep(dve.tensor_scalar(counts[:, :], iota_i[:, :], float(LOW), None, ALU.mult))
            prep(dve.tensor_copy(payload[:, :, 0], dst_i[:, :]))
            prep(dve.tensor_copy(payload[:, :, 1], src_i[:, :]))
            prep(dve.tensor_scalar(payload[:, :, 2], num_i[:, :], float(E - 1), None, ALU.min))
            prep(dve.tensor_copy(payload[:, :, 3], num_i[:, :]))

            def one(t3, t):
                return t3[:, t, :] if isinstance(t, int) else \
                    t3[:, bass.ds(t, 1), :].rearrange("p a f -> p (a f)")

            def col(t2, t):
                return t2[:, t:t + 1] if isinstance(t, int) else t2[:, bass.ds(t, 1)]

            with dve.Fori(0, T) as t:
                dve.tensor_scalar(one(high_hot, t), counts[:, 0:P], col(high_c, t), None, ALU.is_equal)
                dve.tensor_scalar(one(low_hot, t), iota_i[:, :], col(low_c, t), None,
                                  ALU.is_equal).then_inc(one_hot, 1)

            dve.wait_ge(counted, 1)
            dve.tensor_copy(counts[:, :], ps[:, 0, :]).then_inc(base_step, 1)
            dve.wait_ge(base_step, 1)
            dve.tensor_tensor_scan(running[:, :], ones[:, :], counts[:, :], 0.0, ALU.mult,
                                   ALU.add).then_inc(base_step, 1)
            dve.wait_ge(row_base, 1)
            dve.tensor_copy(row_start[:, :], ps[:, 4, 0:1]).then_inc(base_step, 1)
            dve.wait_ge(base_step, 3)
            dve.tensor_tensor(running[:, :], running[:, :], counts[:, :], ALU.subtract).then_inc(base_step, 1)
            dve.wait_ge(base_step, 4)
            dve.tensor_scalar(counts[:, :], running[:, :], row_start[:, 0:1], None, ALU.add).then_inc(base_step, 1)

            dst_rows_t = dst_rows[:, :].rearrange("p (e t) -> p t e", t=T)

            def place_edges(t, q, first):
                dve.tensor_scalar(in_range[:, :], one(dst_rows_t, t), row_hi[:, 0:1], None,
                                  ALU.is_lt).then_inc(place_step, 1)
                dve.wait_ge(place_step, 3 * t + 1)
                if not first:
                    dve.wait_ge(looked_up, t - 1)
                dve.scalar_tensor_tensor(high_row[:, q, :], one(dst_rows_t, t), row_lo[:, 0:1], in_range[:, :],
                                         ALU.is_ge, ALU.mult).then_inc(row_hot, 1)
                dve.scalar_tensor_tensor(running[:, 0:P], one(dst_rows_t, t), col(dst_c, t), earlier[:, :],
                                         ALU.is_equal, ALU.mult, accum_out=rank_in[:, q:q + 1]
                                         ).then_inc(place_step, 1)
                dve.wait_ge(looked_up, t + 1)
                dve.scalar_tensor_tensor(counts[:, :], ps[:, 2 + q, :], 1.0, one(low_hot, t), ALU.mult, ALU.mult,
                                         accum_out=found[:, q:q + 1]).then_inc(place_step, 1)
                dve.wait_ge(place_step, 3 * t + 3)
                if not first:
                    dve.wait_ge(sorted_out[q], 16 * (t // 2) if isinstance(t, int) else 16 * half[0])
                dve.tensor_tensor(place[:, q:q + 1], found[:, q:q + 1], rank_in[:, q:q + 1],
                                  ALU.add).then_inc(place_ready, 1)
            half = [0]
            place_edges(0, 0, True)
            place_edges(1, 1, True)
            with dve.Fori(1, T // 2) as i:
                half[0] = i
                for q in range(2):
                    place_edges(2 * i + q, q, False)

            dve.wait_ge(sorted_loaded, 16)
            sorted_col = lambda k: sorted_rows[:, :, :, k]
            dve.tensor_copy(dst_s[:, :, :], sorted_col(0)).then_inc(dst_col_ready, 1)
            dve.tensor_copy(dst_idx[:, :, :], sorted_col(0)).then_inc(dst_col_ready, 1)
            dve.tensor_copy(src_idx[:, :, :], sorted_col(1))
            dve.tensor_copy(edge_idx[:, :, :], sorted_col(2))
            dve.wait_ge(dst_line_in, 32)
            dve.memset(same[:, 0:1], 0.0)
            dve.tensor_tensor(same[:, 1:EROWS], dst_sorted[:, 1:EROWS], dst_sorted[:, 0:EROWS - 1], ALU.is_equal)
            dve.tensor_tensor(same_next[:, :, :], dst_s[:, :, :], dst_next[:, :, :],
                              ALU.is_equal).then_inc(tables_step, 1)
            dve.wait_ge(tables_step, 1)
            dve.scalar_tensor_tensor(last_idx[:, :, :], same_next[:, :, :], float(SKIP), dst_s[:, :, :],
                                     ALU.mult, ALU.add).then_inc(tables_ready, 1)
            dve.wait_ge(tables_ready, 1)

            def same_of(c):
                return same[:, c * TILE:(c + 1) * TILE] if isinstance(c, int) else \
                    same[:, bass.ds(c * TILE, TILE)]

            def begin(c, t, q):
                return 0.0 if isinstance(c, int) and c == 0 else t[1 - q][:, 511:512]

            for k in ("stats", "mean_var", "rstd", "normed", "sums", "den", "recip", "update"):
                dve.sem_inc(m[k], SEED)

            def message(c, q, use):
                dve.wait_ge(gathered[q], 128 * (use + 1))
                for j in range(R):
                    ins = dve.bn_stats(e_bn[:, j, :], rows_a[q][:, j, :])
                ins.then_inc(m["stats"], 1)
                wait_alone(dve, m["stats"], done(c), dve_passed)
                for j in range(R):
                    ins = dve.bn_aggr(e_mv[:, j, :], e_bn[:, j, :])
                ins.then_inc(m["mean_var"], 1)
                dve.wait_ge(m["std"], done(c))
                dve.reciprocal(e_rs[:, :], e_sd[:, :]).then_inc(m["rstd"], 1)
                dve.wait_ge(m["rstd"], done(c))
                dve.wait_ge(m["turned"], freed(c, 1))
                for j in range(R):
                    ins = dve.tensor_scalar(e_norm[:, j, :], rows_a[q][:, j, :], e_mv[:, j, 0:1],
                                            e_rs[:, j:j + 1], ALU.subtract, ALU.mult)
                ins.then_inc(m["normed"], 1)
                dve.wait_ge(m["rows"], freed(c, 2))
                dve.wait_ge(m["den"], freed(c, 1))
                dve.tensor_tensor_scan(e_den[q][:, :], same_of(c), ones[:, :], begin(c, e_den, q), ALU.mult,
                                       ALU.add).then_inc(m["den"], 1)
                dve.wait_ge(m["value"], done(c))
                dve.wait_ge(m["sums"], freed(c, 1))
                dve.tensor_tensor_scan(e_sum[q][:, :], same_of(c), e_val[:, :], begin(c, e_sum, q), ALU.mult,
                                       ALU.add).then_inc(m["sums"], 1)
                dve.wait_ge(m["rows"], done(c))
                cnt = ps[:, 7, 0:2 * R].rearrange("p (j k) -> p j k", k=2)[:, :, 0]
                dve.reciprocal(e_rc[:, :], cnt).then_inc(m["recip"], 1)
                dve.wait_ge(m["recip"], done(c))
                dve.wait_ge(m["update_free"], freed(c, 2))
                for j in range(R):
                    ins = dve.scalar_tensor_tensor(upd[q][:, j, :], blocks(6)[:, j, :], e_rc[:, j:j + 1],
                                                   b_upd_row[:, :], ALU.mult, ALU.add)
                ins.then_inc(m["update"], 1)
            chunks(dve, message)

            def stats(s, key, g, src_blocks, bn, mv):
                for j in range(R):
                    ins = dve.bn_stats(bn[:, j, :], src_blocks[:, j, :])
                ins.then_inc(s["stats" + key], 1)
                wait_alone(dve, s["stats" + key], done(g), dve_passed)
                for j in range(R):
                    ins = dve.bn_aggr(mv[:, j, :], bn[:, j, :])
                ins.then_inc(s["mean_var" + key], 1)

            def normalise(s, g, q, rows):
                dve.wait_ge(s["std"], done(g))
                dve.reciprocal(n_rs[q][:, :], n_sd[q][:, :]).then_inc(s["rstd"], 1)
                dve.wait_ge(s["rstd"], done(g))
                dve.wait_ge(s["turned"], freed(g, 4))
                for j in range(R):
                    ins = dve.tensor_scalar(n_norm[q][:, j, :], rows[:, j, :], n_mv[q][:, j, 0:1],
                                            n_rs[q][:, j:j + 1], ALU.subtract, ALU.mult)
                ins.then_inc(s["normed"], 1)

            def shift(s, g, q):
                dve.wait_ge(s["std2"], done(g))
                dve.reciprocal(n_rs2[q][:, :], n_sd2[q][:, :]).then_inc(s["rstd2"], 1)
                dve.wait_ge(s["rstd2"], done(g))
                dve.scalar_tensor_tensor(n_sh2[q][:, :], n_mv2[q][:, :, 0], -1.0, n_rs2[q][:, :], ALU.mult,
                                         ALU.mult).then_inc(s["shift2"], 1)

            for k in ("stats", "mean_var", "rstd", "normed", "sum", "stats2", "mean_var2", "rstd2", "shift2",
                      "joined", "result"):
                dve.sem_inc(u[k], SEED)

            def update_step(i, s):
                t = tile_at(i, s, 2, 8)
                if t:
                    normalise(u, 8 * t[0] + t[1], t[1] % 4, n_in[t[1]])
                t = tile_at(i, s, 4, 8)
                if t:
                    shift(u, 8 * t[0] + t[1], t[1] % 4)
                t = tile_at(i, s, 1, 8)
                if t:
                    n, q = 8 * t[0] + t[1], t[1] % 4
                    dve.wait_ge(u_loaded[t[1]], 32 * (t[0] + 1))
                    stats(u, "", n, n_in[t[1]], n_bn[q], n_mv[q])
                t = tile_at(i, s, 5, 8)
                if t:
                    n, q = 8 * t[0] + t[1], t[1] % 4
                    dve.wait_ge(u["shifted"], done(n))
                    dve.scalar_tensor_tensor(flat(n_scaled[q]), flat(n_norm[q]), 0.0, flat(n_scaled[q]), ALU.max,
                                             ALU.add).then_inc(u["joined"], 1)
                    dve.wait_ge(u["joined"], done(n))
                    dve.wait_ge(u["stored"], freed(n, 4))
                    dve.scalar_tensor_tensor(flat(n_out[q]), flat(n_scaled[q]), 0.0, flat(n_in[t[1]]), ALU.max,
                                             ALU.add).then_inc(u["result"], 1)
                t = tile_at(i, s, 3, 8)
                if t:
                    n, q = 8 * t[0] + t[1], t[1] % 4
                    dve.wait_ge(u["proj"], done(n))
                    dve.tensor_tensor(flat(n_sum[q]), bank(6 + q % 2), flat(n_add[q]), ALU.add
                                      ).then_inc(u["sum"], 1)
                    dve.wait_ge(u["sum"], done(n))
                    stats(u, "2", n, n_sum[q], n_bn2[q], n_mv2[q])
            pipeline(dve, 7, update_step, 8)

            def embed_step(i, s):
                t = tile_at(i, s, 2)
                if t:
                    normalise(b, NT + (4 * t[0] + t[1]), t[1], n_in[t[1]])
                t = tile_at(i, s, 1)
                if t:
                    n, q = NT + (4 * t[0] + t[1]), t[1]
                    dve.wait_ge(n_loaded[q], 16 * (t[0] + 1))
                    stats(b, "", n, n_in[q], n_bn[q], n_mv[q])
                t = tile_at(i, s, 3)
                if t:
                    n, q = NT + (4 * t[0] + t[1]), t[1]
                    dve.wait_ge(b["proj"], done(n))
                    dve.wait_ge(b["stored"], freed(n, 4))
                    dve.tensor_tensor(n_out[q][:, :, :], blocks(6 + q % 2), wide(bo0_row), ALU.add
                                      ).then_inc(b["result"], 1)
            pipeline(dve, 5, embed_step)

            for k in ("kq", "clip", "attn"):
                dve.sem_inc(a[k], EC + SEED)
            dve.sem_inc(a["recip"], 2 * EC + SEED)
            for k in ("stats2", "mean_var2", "rstd2", "shift2"):
                dve.sem_inc(f[k], NT)

            def layer(l, is_last):
                count = (9 * l + 8) if is_last else (9 * l + 9)
                dve.wait_ge(weights_loaded, 16 * count)
                names = vec_cols[:, 0:NV * L].rearrange("p (n l) -> p n l", l=L)
                pick = names[:, :, l] if isinstance(l, int) else \
                    names[:, :, bass.ds(l, 1)].rearrange("p n a -> p (n a)")
                if not is_last:
                    dve.tensor_tensor(b2_row[:, :], b2_row[:, :], bo_row[:, :], ALU.add)
                dve.tensor_copy(layer_cols[:, :], pick).then_inc(layer_step, 1)
                dve.wait_ge(layer_step, 2 * l + 1)
                dve.wait_ge(folds_made, l + 1)
                fold = ps[:, 7, 0:10].rearrange("p (n k) -> p n k", k=2)[:, :, 0]
                dve.tensor_tensor(folded[:, 0:3], layer_cols[:, VQ:VV + 1], fold[:, 0:3], ALU.subtract)
                dve.tensor_tensor(folded[:, 3:5], layer_cols[:, VF0:VF1 + 1], fold[:, 3:5], ALU.subtract)
                dve.tensor_tensor(folded[:, 5:6], layer_cols[:, VB1:VB1 + 1], layer_cols[:, VF2:VF2 + 1],
                                  ALU.add).then_inc(layer_step, 1)
                dve.wait_ge(layer_step, 2 * l + 2)
                dve.sem_inc(layer_ready, 1)

                def attend(c, q, use):
                    g = (l + 1) * EC + c
                    dve.wait_ge(a["key"], done(g))
                    dve.wait_ge(a["score"], freed(g, 1))
                    dve.scalar_tensor_tensor(e_kq[:, :], bank(3), folded[:, 0:1], e_key[:, :], ALU.add,
                                             ALU.mult).then_inc(a["kq"], 1)
                    dve.wait_ge(a["score"], done(g))
                    dve.wait_ge(a["exp"], freed(g, 1))
                    dve.tensor_scalar(e_clip[:, :], bank(5), -5.0, 5.0, ALU.max, ALU.min).then_inc(a["clip"], 1)
                    dve.wait_ge(a["exp"], done(g))
                    dve.scalar_tensor_tensor(e_val[:, :], bank(4), folded[:, 2:3], e_exp[:, :], ALU.add,
                                             ALU.mult).then_inc(a["value"], 1)
                    dve.wait_ge(a["den"], freed(g, 1))
                    dve.tensor_tensor_scan(e_den[q][:, :], same_of(c), e_exp[:, :], begin(c, e_den, q), ALU.mult,
                                           ALU.add).then_inc(a["den"], 1)
                    dve.wait_ge(a["den"], done(g))
                    dve.tensor_scalar(e_rden[:, :], e_den[q][:, :], 1e-6, None, ALU.add).then_inc(a["recip"], 1)
                    dve.wait_ge(a["value"], done(g))
                    dve.wait_ge(a["sums"], freed(g, 1))
                    dve.tensor_tensor_scan(e_sum[q][:, :], same_of(c), e_val[:, :], begin(c, e_sum, q), ALU.mult,
                                           ALU.add).then_inc(a["sums"], 1)
                    dve.wait_ge(a["recip"], 2 * g + (SEED + 1))
                    dve.reciprocal(e_rinv[:, :], e_rden[:, :]).then_inc(a["recip"], 1)
                    dve.wait_ge(a["recip"], 2 * g + (SEED + 2))
                    dve.wait_ge(a["sums"], done(g))
                    dve.wait_ge(a["rows"], freed(g, 1))
                    dve.tensor_tensor(e_attn[:, :], e_sum[q][:, :], e_rinv[:, :], ALU.mult).then_inc(a["attn"], 1)
                    dve.wait_ge(a["rows"], done(g))
                    dve.wait_ge(a["update_free"], freed(g, 2))
                    dve.tensor_tensor(flat(upd[q]), bank(6), flat(rows_b[q]), ALU.add).then_inc(a["update"], 1)
                chunks(dve, attend)

                g0 = (l + 2) * NT

                def step(i, s):
                    t = tile_at(i, s, 2)
                    if t:
                        normalise(f, g0 + (4 * t[0] + t[1]), t[1], n_in[t[1]])
                    t = tile_at(i, s, 5)
                    if t:
                        shift(f, g0 + (4 * t[0] + t[1]), t[1])
                    t = tile_at(i, s, 1)
                    if t:
                        g, q = g0 + (4 * t[0] + t[1]), t[1]
                        dve.wait_ge(n_loaded[q], 16 * ((l + 1) * uses(q, NT, 4) + t[0] + 1))
                        stats(f, "", g, n_in[q], n_bn[q], n_mv[q])
                    t = tile_at(i, s, 4)
                    if t:
                        g, q = g0 + (4 * t[0] + t[1]), t[1]
                        dve.wait_ge(f["ffn"], done(g))
                        stats(f, "2", g, blocks(6 + q % 2), n_bn2[q], n_mv2[q])
                pipeline(dve, 7, step)

            with dve.Fori(0, L - 1) as l:
                layer(l, False)
            layer(L - 1, True)


_INS = ["x", "src", "dst", "edge_attr_128", "L0_gnn_W_msg", "L0_gnn_b_msg", "L0_gnn_W_upd", "L0_gnn_b_upd",
        "L0_gnn_gamma", "L0_gnn_beta", "L1_gnn_Wemb", "L1_gnn_Wq", "L1_gnn_bq", "L1_gnn_Wk", "L1_gnn_bk",
        "L1_gnn_Wv", "L1_gnn_bv", "L1_gnn_Wo", "L1_gnn_bo", "L1_gnn_ln1_g", "L1_gnn_ln1_b", "L1_gnn_W1",
        "L1_gnn_b1", "L1_gnn_W2", "L1_gnn_b2", "L1_gnn_ln2_g", "L1_gnn_ln2_b"]


def kernel(**inputs):
    import numpy as np
    import concourse.bacc as bacc
    from concourse.bass_utils import run_bass_kernel_spmd

    nc = bacc.Bacc("TRN2", target_bir_lowering=False, num_devices=1)
    arrays, args = {}, []
    for name in _INS:
        arr = np.ascontiguousarray(inputs[name])
        arrays[f"in_{name}"] = arr
        args.append(nc.dram_tensor(f"in_{name}", arr.shape, mybir.dt.from_np(arr.dtype),
                                   kind="ExternalInput").ap())
    out = nc.dram_tensor("out_0", inputs["x"].shape, F32, kind="ExternalOutput").ap()
    build(nc, *args, out)
    r = run_bass_kernel_spmd(nc, [arrays], core_ids=[0])
    return r.results[0]["out_0"]
```

```python
from contextlib import ExitStack

import concourse.bass as bass
from concourse import mybir

F32 = mybir.dt.float32
BF16 = mybir.dt.bfloat16
I32 = mybir.dt.int32
ALU = mybir.AluOpType
ACT = mybir.ActivationFunctionType

P = 128
R = 4
TILE = P * R
LOW = 512
SEED = 8
EPS = 1e-5
SKIP = 1 << 20
HEADS = 8


def build(nc, x, src, dst, edge_attr, W_msg, b_msg, W_upd, b_upd, gamma, beta, Wemb, Wq, bq, Wk, bk,
          Wv, bv, Wo, bo, ln1_g, ln1_b, W1, b1, W2, b2, ln2_g, ln2_b, out):
    N, E, L = x.shape[0], src.shape[0], Wq.shape[0]
    HD = P // HEADS
    NT = -(-N // TILE)
    NROWS = NT * TILE
    TAIL = (N - (NT - 1) * TILE) // R
    EC = -(-E // TILE)
    EROWS = EC * TILE
    T = EROWS // P
    EP = E // T
    assert N % R == 0 and N < NROWS and E % T == 0 and EC % 2 == 1 and NROWS <= P * LOW

    h_tab = nc.dram_tensor("h_tab", (NROWS, P), F32, kind="Internal").ap()
    y_tab = nc.dram_tensor("y_tab", (NROWS, P), F32, kind="Internal").ap()
    x1_tab = nc.dram_tensor("x1_tab", (NROWS, P), F32, kind="Internal").ap()
    msg_tab = nc.dram_tensor("msg_tab", (NROWS, P), F32, kind="Internal").ap()
    sorted_tab = nc.dram_tensor("sorted_tab", (EROWS, 4), I32, kind="Internal").ap()
    dst_line = nc.dram_tensor("dst_line", (EROWS + R,), I32, kind="Internal").ap()

    ctx = ExitStack()
    with ctx:
        def sb(name, shape, dt=F32, stack=ctx):
            return stack.enter_context(nc.sbuf_tensor(name, shape, dt))

        def sem(name):
            return ctx.enter_context(nc.semaphore(name))

        ps = ctx.enter_context(nc.psum_tensor("ps", [P, 8, 512], F32))

        ident = sb("ident", [P, P])
        ones = sb("ones", [P, 512])
        head_sum = sb("head_sum", [P, P])
        before = sb("before", [P, P])
        earlier = sb("earlier", [P, P])
        eps = sb("eps", [P, 1])
        w_msg = sb("w_msg", [P, 2, P])
        w_upd = sb("w_upd", [P, 2, P])
        w_emb = sb("w_emb", [P, P])
        NV = 9
        VQ, VK, VV, VO, VG1, VB1, VF0, VF1, VF2 = range(NV)
        vec_rows = sb("vec_rows", [P, P])
        vec_cols = sb("vec_cols", [P, L * NV + 1])
        layer_cols = sb("layer_cols", [P, NV])
        folded = sb("folded", [P, 6])
        b_upd_row = sb("b_upd_row", [P, P])
        gamma_row = sb("gamma_row", [P, P])
        beta_row = sb("beta_row", [P, P])
        bo0_row = sb("bo0_row", [P, P])
        g2_row = sb("g2_row", [P, P])
        b2_row = sb("b2_row", [P, P])
        bo_row = sb("bo_row", [P, P])
        ending = sb("ending", [P, R], I32)
        b_upd_wide = sb("b_upd_wide", [P, R, P])
        bo0_wide = sb("bo0_wide", [P, R, P])

        const_loaded = sem("const_loaded")
        pool_passed = sem("pool_passed")
        dve_passed = sem("dve_passed")
        consts_made = sem("consts_made")
        consts_step = sem("consts_step")
        edges_loaded = sem("edges_loaded")
        columns_made = sem("columns_made")
        columns_copied = sem("columns_copied")
        sort_prep = sem("sort_prep")
        one_hot = sem("one_hot")
        counted = sem("counted")
        base_step = sem("base_step")
        row_base = sem("row_base")
        seeded = sem("seeded")
        table_copied = sem("table_copied")
        table_added = sem("table_added")
        row_hot = sem("row_hot")
        rank_ready = sem("rank_ready")
        looked_up = sem("looked_up")
        in_range_ready = sem("in_range_ready")
        found_ready = sem("found_ready")
        place_ready = sem("place_ready")
        payload_copied = sem("payload_copied")
        sorted_out = [sem(f"sorted_out{i}") for i in range(2)]
        sorted_done = sem("sorted_done")
        sorted_loaded = sem("sorted_loaded")
        dst_col_ready = sem("dst_col_ready")
        dst_line_out = sem("dst_line_out")
        dst_line_in = sem("dst_line_in")
        tables_step = sem("tables_step")
        tables_ready = sem("tables_ready")
        wide_made = sem("wide_made")
        msg_filled = sem("msg_filled")

        def named(k, names):
            return {n: sem(f"{k}_{n}") for n in names}

        edge = named("edge", ["idx", "idx_out", "turned", "turned_copy", "proj", "value", "sums", "den", "rows", "update",
                              "update_free"])
        m = edge | named("m", ["stats", "mean_var", "std", "rstd", "normed", "recip"])
        a = edge | named("a", ["key", "kq", "score", "clip", "exp", "recip", "attn"])
        gathered = [sem(f"gathered{i}") for i in range(4)]
        scattered = [sem(f"scattered{i}") for i in range(4)]
        m_done = sem("m_done")
        a_done = sem("a_done")

        node = named("node", ["stats", "mean_var", "std", "rstd", "normed", "turned", "turned_copy", "result",
                              "stored", "proj", "stats2", "mean_var2", "std2", "rstd2", "shift2", "normed2",
                              "scaled"])
        u = node | named("u", ["shifted", "joined", "joined_relu"])
        b = node
        f = node | named("f", ["hidden", "relu", "ffn", "shifted"])
        u_loaded = [sem(f"u_loaded{i}") for i in range(8)]
        msg_loaded = [sem(f"msg_loaded{i}") for i in range(4)]
        x1_loaded = [sem(f"x1_loaded{i}") for i in range(4)]
        n_loaded = [sem(f"n_loaded{i}") for i in range(4)]
        n_stored = [sem(f"n_stored{i}") for i in range(4)]
        weights_loaded = sem("weights_loaded")
        layer_step = sem("layer_step")
        folds_made = sem("folds_made")
        layer_ready = sem("layer_ready")

        with ExitStack() as sort_ctx:
            def st(name, shape, dt=F32):
                return sb(name, shape, dt, sort_ctx)
            low_hot = st("low_hot", [P, T, LOW], BF16)
            high_hot = st("high_hot", [P, T, P], BF16)
            dst_rows = st("dst_rows", [P, EROWS], I32)
            dst_i = st("dst_i", [P, T], I32)
            src_i = st("src_i", [P, T], I32)
            num_i = st("num_i", [P, T], I32)
            part_i = st("part_i", [P, T], I32)
            dst_c = st("dst_c", [P, T])
            high_c = st("high_c", [P, T])
            low_c = st("low_c", [P, T])
            payload = st("payload", [P, T, 4], I32)
            iota_i = st("iota_i", [P, LOW], I32)
            row_lo = st("row_lo", [P, 1])
            row_hi = st("row_hi", [P, 1])
            row_i = st("row_i", [P, 1], I32)
            table = st("table", [P, 2, LOW])
            counts = st("counts", [P, LOW])
            running = st("running", [P, LOW])
            row_start = st("row_start", [P, 1])
            in_range = st("in_range", [P, P])
            high_row = st("high_row", [P, 2, P])
            rank_in = st("rank_in", [P, T])
            found = st("found", [P, T])
            place = st("place", [P, 2], I32)
            load_out = st("load_out", [P, 2, 4], I32)

        wq, wk, wv, wo = (sb(f"w{n}", [P, P]) for n in "qkvo")
        w1 = sb("w1", [P, 2 * P])
        w2 = sb("w2", [P, 2, P])

        same = sb("same", [P, EROWS], BF16)
        src_idx = sb("src_idx", [P, EC, R], I32)
        dst_idx = sb("dst_idx", [P, EC, R], I32)
        edge_idx = sb("edge_idx", [P, EC, R], I32)
        last_idx = sb("last_idx", [P, EC, R], I32)

        with ExitStack() as table_ctx:
            def tb(name, shape, dt=F32):
                return sb(name, shape, dt, table_ctx)
            sorted_rows = tb("sorted_rows", [P, EC, R, 4], I32)
            dst_s = tb("dst_s", [P, EC, R], I32)
            dst_next = tb("dst_next", [P, EC, R], I32)
            dst_sorted = tb("dst_sorted", [P, EROWS], I32)
            same_next = tb("same_next", [P, EC, R])

        idx_a = [sb(f"idx_a{i}", [P, R], I32) for i in range(4)]
        idx_b = [sb(f"idx_b{i}", [P, R], I32) for i in range(4)]
        idx_c = [sb(f"idx_c{i}", [P, R], I32) for i in range(4)]
        rows_a = [sb(f"rows_a{i}", [P, R, P]) for i in range(4)]
        rows_b = [sb(f"rows_b{i}", [P, R, P]) for i in range(4)]
        upd = [sb(f"upd{i}", [P, R, P]) for i in range(4)]
        e_norm = sb("e_norm", [P, R, P])
        e_aT = sb("e_aT", [P, 512])
        e_bT = sb("e_bT", [P, 512])
        e_key = sb("e_key", [P, 512])
        e_kq = sb("e_kq", [P, 512])
        e_clip = sb("e_clip", [P, 512])
        e_exp = sb("e_exp", [P, 512])
        e_val = sb("e_val", [P, 512])
        e_sum = [sb(f"e_sum{i}", [P, 512]) for i in range(2)]
        e_den = [sb(f"e_den{i}", [P, 512]) for i in range(2)]
        e_rden = sb("e_rden", [P, 512])
        e_rinv = sb("e_rinv", [P, 512])
        e_attn = sb("e_attn", [P, 512])
        e_rc = sb("e_rc", [P, R])
        e_bn = sb("e_bn", [P, R, 6])
        e_mv = sb("e_mv", [P, R, 2])
        e_sd = sb("e_sd", [P, R])
        e_rs = sb("e_rs", [P, R])

        def ring(name, shape, dt=F32):
            return [sb(f"{name}{i}", shape, dt) for i in range(4)]
        n_in = [sb(f"n_in{i}", [P, R, P]) for i in range(8)]
        n_add = ring("n_add", [P, R, P])
        n_norm = [sb(f"n_norm{i}", [P, R, P]) for i in range(8)]
        n_T = ring("n_T", [P, 512])
        n_relu = ring("n_relu", [P, 2, 512])
        n_sum = ring("n_sum", [P, R, P])
        n_norm2 = ring("n_norm2", [P, R, P])
        n_scaled = ring("n_scaled", [P, R, P])
        n_out = ring("n_out", [P, R, P])
        n_bn = ring("n_bn", [P, R, 6])
        n_mv = ring("n_mv", [P, R, 2])
        n_sd = ring("n_sd", [P, R])
        n_rs = ring("n_rs", [P, R])
        n_bn2 = ring("n_bn2", [P, R, 6])
        n_mv2 = ring("n_mv2", [P, R, 2])
        n_sd2 = ring("n_sd2", [P, R])
        n_rs2 = ring("n_rs2", [P, R])
        n_sh2 = ring("n_sh2", [P, R])

        node_view = lambda tab: tab.rearrange("(n p j) f -> n p (j f)", p=P, j=R)
        flat = lambda t: t[:, :, :].rearrange("p j f -> p (j f)")
        wide = lambda row: row[:, :].unsqueeze(1).to_broadcast([P, R, P])
        bank = lambda n: ps[:, n, :]
        blocks = lambda n: ps[:, n, :].rearrange("p (j f) -> p j f", j=R)
        by_row = lambda t, j: t.rearrange("f (p j) -> f j p", j=R)[:, j, :]

        done = lambda g: g + (SEED + 1)
        freed = lambda g, depth: g + (SEED + 1 - depth)
        out_bank = lambda q, banks: 8 - banks + q % banks
        uses = lambda q, n, depth: (n - q + depth - 1) // depth

        def item_at(i, s, lag, depth, count):
            if isinstance(i, int):
                n = depth * i + s - lag
                return (n // depth, n % depth) if 0 <= n < count else None
            return i + (s - lag) // depth, (s - lag) % depth

        def steps(eng, count, lags, step, depth):
            first, end = -(-lags // depth), (count - 1) // depth
            if end <= first:
                first = end = 0
            for n in range(depth * first):
                step(n // depth, n % depth)
            if end:
                with eng.Fori(first, end) as i:
                    for s in range(depth):
                        step(i, s)
            for n in range(depth * end, count + lags):
                step(n // depth, n % depth)

        def tile_at(i, s, lag, depth=4):
            return item_at(i, s, lag, depth, NT)

        def pipeline(eng, lags, step, depth=4):
            steps(eng, NT, lags, step, depth)

        def chunk_at(i, s, lag):
            return item_at(i, s, lag, 4, EC)

        def chunks(eng, step):
            steps(eng, EC, 6, step, 4)

        def wait_alone(eng, s, value, passed):
            eng.wait_ge(s, value)
            eng.sem_inc(passed, 1)

        block = ctx.enter_context(nc.Block())

        @block.sync
        def _(sp):
            loads = [(w_msg[:, :, :], W_msg.rearrange("(c k) f -> k c f", k=P)),
                     (w_upd[:, :, :], W_upd.rearrange("(c k) f -> k c f", k=P)),
                     (w_emb[:, :], Wemb)]
            for n, v in ((VQ, bq), (VK, bk), (VV, bv), (VO, bo), (VG1, ln1_g), (VB1, ln1_b),
                         (VF0, b1[:, 0:P]), (VF1, b1[:, P:2 * P]), (VF2, b2)):
                loads.append((vec_rows[n * L:(n + 1) * L, :], v))
            loads.append((vec_rows[NV * L:NV * L + 1, :], b_msg.unsqueeze(0)))
            for t, v in ((b_upd_row, b_upd), (gamma_row, gamma), (beta_row, beta), (bo0_row, bo[0])):
                loads.append((t[:, :], v.partition_broadcast(P)))
            sp.wait_ge(consts_made, 1)
            sp.dma_start(dst_i[0:EP, :], dst.rearrange("(p t) -> p t", t=T)).then_inc(edges_loaded, 16)
            sp.dma_start(src_i[0:EP, :], src.rearrange("(p t) -> p t", t=T)).then_inc(edges_loaded, 16)
            sp.dma_start(dst_rows[:, 0:E], dst.partition_broadcast(P)).then_inc(edges_loaded, 16)
            for t, v in loads:
                sp.dma_start(t, v).then_inc(const_loaded, 16)

            sp.wait_ge(wide_made, 1)
            with sp.Fori(0, NT) as n:
                sp.dma_start(node_view(msg_tab)[n], flat(b_upd_wide)).then_inc(msg_filled, 16)

            sp.wait_ge(sorted_done, T)
            sp.dma_start(sorted_rows[:, :, :, :].rearrange("p c j w -> p c (j w)"),
                         sorted_tab.rearrange("(c p j) w -> p c (j w)", p=P, j=R)).then_inc(sorted_loaded, 16)
            sp.wait_ge(dst_col_ready, 2)
            sp.dma_start(dst_line[0:EROWS].rearrange("(c p j) -> p c j", p=P, j=R),
                         dst_s[:, :, :]).then_inc(dst_line_out, 16)
            sp.dma_start(dst_line[EROWS:EROWS + R].unsqueeze(0), ending[0:1, :]).then_inc(dst_line_out, 16)
            sp.wait_ge(dst_line_out, 32)
            sp.dma_start(dst_sorted[:, :], dst_line[0:EROWS].partition_broadcast(P)).then_inc(dst_line_in, 16)
            sp.dma_start(dst_next[:, :, :], dst_line[1:EROWS + 1].rearrange("(c p j) -> p c j", p=P, j=R)
                         ).then_inc(dst_line_in, 16)

            def load(dst_t, tab, n, is_tail, s):
                if is_tail:
                    rows = tab[(NT - 1) * TILE:N, :].rearrange("(p j) f -> p (j f)", j=R)
                    sp.dma_start(flat(dst_t)[0:TAIL, :], rows).then_inc(s, 16)
                else:
                    sp.dma_start(flat(dst_t), node_view_full(tab, n)).then_inc(s, 16)

            def node_view_full(tab, n):
                return tab[0:(tab.shape[0] // TILE) * TILE, :].rearrange("(n p j) f -> n p (j f)", p=P, j=R)[n]

            def number(t):
                return 4 * t[0] + t[1]

            sp.wait_ge(m_done, 1)
            sp.sem_inc(node["stored"], SEED)

            def update_step(i, s):
                t = tile_at(i, s, 0, 8)
                if t:
                    n = 8 * t[0] + t[1]
                    sp.wait_ge(u["result"], freed(n, 8))
                    load(n_in[t[1]], x, n, isinstance(n, int) and n == NT - 1, u_loaded[t[1]])
                t = tile_at(i, s, 1, 8)
                if t:
                    n = 8 * t[0] + t[1]
                    sp.wait_ge(u["proj"], freed(n, 4))
                    sp.dma_start(flat(n_add[t[1] % 4]), node_view(msg_tab)[n]).then_inc(msg_loaded[t[1] % 4], 16)
                t = tile_at(i, s, 8, 8)
                if t:
                    n = 8 * t[0] + t[1]
                    sp.wait_ge(u["result"], done(n))
                    sp.dma_start(node_view(x1_tab)[n], flat(n_out[t[1] % 4])).then_inc(n_stored[t[1] % 4], 16)
                t = tile_at(i, s, 9, 8)
                if t:
                    sp.wait_ge(n_stored[t[1] % 4], 16 * (2 * t[0] + t[1] // 4 + 1))
                    sp.sem_inc(u["stored"], 1)
            pipeline(sp, 10, update_step, 8)

            def embed_step(i, s):
                t = tile_at(i, s, 0)
                if t:
                    n = number(t)
                    sp.wait_ge(b["normed"], freed(NT + n, 4))
                    sp.dma_start(flat(n_in[t[1]]), node_view(x1_tab)[n]).then_inc(n_loaded[t[1]], 16)
                t = tile_at(i, s, 5)
                if t:
                    n = number(t)
                    sp.wait_ge(b["result"], done(NT + n))
                    sp.dma_start(node_view(h_tab)[n], flat(n_out[t[1]])).then_inc(n_stored[t[1]], 16)
                    sp.dma_start(node_view(y_tab)[n], flat(n_out[t[1]])).then_inc(n_stored[t[1]], 16)
                t = tile_at(i, s, 6)
                if t:
                    sp.wait_ge(n_stored[t[1]], 16 * uses(t[1], NT, 4) + 32 * (t[0] + 1))
                    sp.sem_inc(b["stored"], 1)
            pipeline(sp, 7, embed_step)

            def layer(l, is_last):
                for t, v in ((wq[:, :], Wq[l]), (wk[:, :], Wk[l]), (wv[:, :], Wv[l]), (wo[:, :], Wo[l]),
                             (w1[:, :], W1[l]), (w2[:, :, :], W2[l].rearrange("(c k) f -> k c f", k=P)),
                             (g2_row[:, :], ln2_g[l].partition_broadcast(P)),
                             (b2_row[:, :], ln2_b[l].partition_broadcast(P))):
                    sp.dma_start(t, v).then_inc(weights_loaded, 16)
                if not is_last:
                    sp.dma_start(bo_row[:, :], bo[l + 1].partition_broadcast(P)).then_inc(weights_loaded, 16)
                sp.wait_ge(a_done, l + 1)
                g0 = (l + 2) * NT

                def step(i, s):
                    t = tile_at(i, s, 0)
                    if t:
                        n = number(t)
                        sp.wait_ge(f["normed"], freed(g0 + n, 4))
                        sp.dma_start(flat(n_in[t[1]]), node_view(y_tab)[n]).then_inc(n_loaded[t[1]], 16)
                    t = tile_at(i, s, 4)
                    if t and is_last:
                        n = number(t)
                        sp.wait_ge(f["result"], freed(g0 + n, 4))
                        sp.dma_start(flat(n_add[t[1]]), node_view(x1_tab)[n]).then_inc(x1_loaded[t[1]], 16)
                    t = tile_at(i, s, 8)
                    if t:
                        n = number(t)
                        sp.wait_ge(f["result"], done(g0 + n))
                        if not is_last:
                            sp.dma_start(node_view(h_tab)[n], flat(n_out[t[1]])).then_inc(n_stored[t[1]], 16)
                            sp.dma_start(node_view(y_tab)[n], flat(n_out[t[1]])).then_inc(n_stored[t[1]], 16)
                        elif isinstance(n, int) and n == NT - 1:
                            rows = out[(NT - 1) * TILE:N, :].rearrange("(p j) f -> p (j f)", j=R)
                            sp.dma_start(rows, flat(n_out[t[1]])[0:TAIL, :]).then_inc(n_stored[t[1]], 32)
                        else:
                            sp.dma_start(node_view_full(out, n), flat(n_out[t[1]])).then_inc(n_stored[t[1]], 32)
                    t = tile_at(i, s, 9)
                    if t:
                        sp.wait_ge(n_stored[t[1]], 48 * uses(t[1], NT, 4) + 32 * (l * uses(t[1], NT, 4) + t[0] + 1))
                        sp.sem_inc(f["stored"], 1)
                pipeline(sp, 10, step)

            with sp.Fori(0, L - 1) as l:
                layer(l, False)
            layer(L - 1, True)

        @block.gpsimd
        def _(pool):
            made = [0]

            def step(ins):
                made[0] += 1
                ins.then_inc(consts_step, 1)
                pool.wait_ge(consts_step, made[0])

            step(pool.memset(dst_i[:, :], N))
            step(pool.memset(src_i[:, :], 0))
            step(pool.memset(dst_rows[:, E:EROWS], N))
            pool.sem_inc(consts_made, 1)
            step(pool.memset(ones[:, :], 1.0))
            step(pool.memset(ident[:, :], 0.0))
            step(pool.affine_select(out=ident[:, :], in_=ident[:, :], compare_op=ALU.not_equal, fill=1.0, base=0,
                                    pattern=[[-1, P]], channel_multiplier=1))
            step(pool.affine_select(out=before[:, :], in_=ones[:, 0:P], compare_op=ALU.is_ge, fill=0.0, base=-1,
                                    pattern=[[1, P]], channel_multiplier=-1))
            step(pool.affine_select(out=earlier[:, :], in_=ones[:, 0:P], compare_op=ALU.is_ge, fill=0.0, base=-1,
                                    pattern=[[-1, P]], channel_multiplier=1))
            hs = head_sum[:, :].rearrange("p (h d) -> p h d", h=HEADS)
            step(pool.memset(head_sum[:, :], float(HD) ** -0.5))
            step(pool.affine_select(out=hs, in_=hs, compare_op=ALU.is_ge, fill=0.0, base=0,
                                    pattern=[[-HD, HEADS], [0, HD]], channel_multiplier=1))
            step(pool.affine_select(out=hs, in_=hs, compare_op=ALU.is_ge, fill=0.0, base=HD - 1,
                                    pattern=[[HD, HEADS], [0, HD]], channel_multiplier=-1))
            step(pool.memset(eps[:, :], EPS))
            step(pool.iota(iota_i[:, :], pattern=[[1, LOW]], base=0, channel_multiplier=0))
            step(pool.iota(num_i[:, :], pattern=[[1, T]], base=0, channel_multiplier=T))
            step(pool.iota(row_i[:, :], pattern=[[0, 1]], base=0, channel_multiplier=LOW))
            step(pool.memset(ending[:, :], -1))
            pool.sem_inc(consts_made, 1)

            pool.sem_inc(payload_copied, SEED)

            def place_out(t, q, use, first):
                wait_alone(pool, place_ready, t + 1, pool_passed)
                if not first:
                    wait_alone(pool, sorted_out[q], 16 * use, pool_passed)
                pool.tensor_copy(load_out[:, q, :], payload[:, t, :] if isinstance(t, int) else
                                 payload[:, bass.ds(t, 1), :].rearrange("p a w -> p (a w)")
                                 ).then_inc(payload_copied, 1)
                wait_alone(pool, payload_copied, done(t), pool_passed)
                pool.indirect_dma_start(out=sorted_tab[:, :],
                                        out_offset=bass.IndirectOffsetOnAxis(ap=place[:, q:q + 1], axis=0),
                                        in_=load_out[:, q, :], in_offset=None).then_inc(sorted_out[q], 16)
            place_out(0, 0, 0, True)
            place_out(1, 1, 0, True)
            with pool.Fori(1, T // 2) as i:
                for q in range(2):
                    place_out(2 * i + q, q, i, False)
                    pool.sem_inc(sorted_done, 1)
            for q in range(2):
                wait_alone(pool, sorted_out[q], 16 * (T // 2), pool_passed)
                pool.sem_inc(sorted_done, 1)

            pool.wait_ge(tables_ready, 1)
            pool.wait_ge(msg_filled, 16 * NT)

            def edge_phase(s, tab_a, ia, tab_b, ib, out_tab, k):
                g0 = k * EC

                def cols(t, c):
                    return t[:, c, :] if isinstance(c, int) else \
                        t[:, bass.ds(c, 1), :].rearrange("p a j -> p (a j)")

                def gather(h, q):
                    c = 4 * h + q
                    wait_alone(pool, s["update"], freed(g0 + c, 4), pool_passed)
                    pool.tensor_copy(idx_a[q][:, :], cols(ia, c))
                    pool.tensor_copy(idx_b[q][:, :], cols(ib, c)).then_inc(s["idx"], 1)
                    wait_alone(pool, s["idx"], g0 + c + 1, pool_passed)
                    for t, ix, rows in ((tab_a, idx_a, rows_a), (tab_b, idx_b, rows_b)):
                        for j in range(R):
                            pool.indirect_dma_start(
                                out=rows[q][:, j, :], out_offset=None, in_=t[:, :],
                                in_offset=bass.IndirectOffsetOnAxis(ap=ix[q][:, j:j + 1], axis=0)
                            ).then_inc(gathered[q], 16)

                def scatter(h, q):
                    c = 4 * h + q
                    pool.tensor_copy(idx_c[q][:, :], cols(last_idx, c)).then_inc(s["idx_out"], 1)
                    wait_alone(pool, s["idx_out"], g0 + c + 1, pool_passed)
                    wait_alone(pool, s["update"], done(g0 + c), pool_passed)
                    for j in range(R):
                        pool.indirect_dma_start(
                            out=out_tab[:, :],
                            out_offset=bass.IndirectOffsetOnAxis(ap=idx_c[q][:, j:j + 1], axis=0),
                            in_=upd[q][:, j, :], in_offset=None, bounds_check=NROWS - 1, oob_is_err=False
                        ).then_inc(scattered[q], 16)

                def step(i, s_):
                    t = chunk_at(i, s_, 5)
                    if t:
                        wait_alone(pool, scattered[t[1]], 64 * (k * uses(t[1], EC, 4) + t[0] + 1), pool_passed)
                        pool.sem_inc(s["update_free"], 1)
                    t = chunk_at(i, s_, 0)
                    if t:
                        gather(*t)
                    t = chunk_at(i, s_, 4)
                    if t:
                        scatter(*t)
                chunks(pool, step)

            pool.sem_inc(m["update_free"], SEED)
            edge_phase(m, x, src_idx, edge_attr, edge_idx, msg_tab, 0)
            pool.sem_inc(m_done, 1)

            pool.sem_inc(u["scaled"], SEED)
            pool.sem_inc(u["shifted"], SEED)
            pool.sem_inc(u["result"], SEED)

            def update_step(i, s):
                t = tile_at(i, s, 6, 8)
                if t:
                    n, q = 8 * t[0] + t[1], t[1] % 4
                    wait_alone(pool, u["scaled"], done(n), pool_passed)
                    wait_alone(pool, u["result"], freed(n, 4), pool_passed)
                    pool.tensor_tensor(out=n_scaled[q][:, :, :], in0=n_norm2[q][:, :, :], in1=wide(beta_row),
                                       op=ALU.add).then_inc(u["shifted"], 1)
                t = tile_at(i, s, 5, 8)
                if t:
                    n, q = 8 * t[0] + t[1], t[1] % 4
                    wait_alone(pool, u["normed2"], done(n), pool_passed)
                    pool.tensor_tensor(out=n_norm2[q][:, :, :], in0=n_norm2[q][:, :, :], in1=wide(gamma_row),
                                       op=ALU.mult).then_inc(u["scaled"], 1)
                t = tile_at(i, s, 7, 8)
                if t:
                    n, q = 8 * t[0] + t[1], t[1] % 4
                    wait_alone(pool, u["joined_relu"], done(n), pool_passed)
                    wait_alone(pool, u["stored"], freed(n, 4), pool_passed)
                    pool.tensor_tensor(out=n_out[q][:, :, :], in0=n_scaled[q][:, :, :], in1=n_in[t[1]][:, :, :],
                                       op=ALU.add).then_inc(u["result"], 1)
            pipeline(pool, 10, update_step, 8)

            pool.sem_inc(f["scaled"], NT)
            pool.sem_inc(f["shifted"], SEED)

            def layer(l, is_last):
                wait_alone(pool, f["stored"], (l + 2) * NT + SEED, pool_passed)
                edge_phase(a, h_tab, src_idx, h_tab, dst_idx, y_tab, l + 1)
                pool.sem_inc(a_done, 1)
                g0 = (l + 2) * NT

                def step(i, s):
                    t = tile_at(i, s, 6)
                    if t:
                        g, q = g0 + (4 * t[0] + t[1]), t[1]
                        wait_alone(pool, f["normed2"], done(g), pool_passed)
                        pool.tensor_tensor(out=n_scaled[q][:, :, :], in0=n_norm2[q][:, :, :], in1=wide(g2_row),
                                           op=ALU.mult).then_inc(f["scaled"], 1)
                        wait_alone(pool, f["scaled"], done(g), pool_passed)
                        if is_last:
                            pool.tensor_tensor(out=n_norm2[q][:, :, :], in0=n_scaled[q][:, :, :], in1=wide(b2_row),
                                               op=ALU.add).then_inc(f["shifted"], 1)
                        else:
                            wait_alone(pool, f["stored"], freed(g, 4), pool_passed)
                            pool.tensor_tensor(out=n_out[q][:, :, :], in0=n_scaled[q][:, :, :], in1=wide(b2_row),
                                               op=ALU.add).then_inc(f["result"], 1)
                    t = tile_at(i, s, 7)
                    if t and is_last:
                        g, q = g0 + (4 * t[0] + t[1]), t[1]
                        wait_alone(pool, f["shifted"], done(4 * t[0] + t[1]), pool_passed)
                        wait_alone(pool, x1_loaded[q], 16 * (t[0] + 1), pool_passed)
                        wait_alone(pool, f["stored"], freed(g, 4), pool_passed)
                        pool.tensor_tensor(out=n_out[q][:, :, :], in0=n_norm2[q][:, :, :],
                                           in1=n_add[q][:, :, :], op=ALU.add).then_inc(f["result"], 1)
                pipeline(pool, 10, step)

            with pool.Fori(0, L - 1) as l:
                layer(l, False)
            layer(L - 1, True)

        @block.tensor
        def _(pe):
            pe.wait_ge(consts_made, 2)
            pe.wait_ge(const_loaded, 16 * 17)
            pe.transpose(ps[:, 7, 0:L * NV + 1], vec_rows[0:L * NV + 1, :],
                         ident[0:L * NV + 1, 0:L * NV + 1]).then_inc(columns_made, 1)

            def count(t, start=False, stop=False):
                pe.wait_ge(one_hot, t + 1)
                return pe.matmul(ps[:, 0, :], one(high_hot, t), one(low_hot, t), start=start, stop=stop,
                                 skip_group_check=True)

            def one(t3, t):
                return t3[:, t, :] if isinstance(t, int) else \
                    t3[:, bass.ds(t, 1), :].rearrange("p a f -> p (a f)")
            count(0, start=True)
            with pe.Fori(1, T - 1) as t:
                count(t)
            count(T - 1, stop=True).then_inc(counted, 1)
            pe.wait_ge(base_step, 2)
            pe.matmul(ps[:, 4, 0:1], before[:, :], running[:, LOW - 1:LOW], start=True,
                      stop=True).then_inc(row_base, 1)
            pe.wait_ge(base_step, 5)
            pe.matmul(ps[:, 1, :], ident[:, :], counts[:, :], start=True, stop=False,
                      skip_group_check=True).then_inc(table_added, 1)

            def look_up(t, q, first):
                pe.wait_ge(table_copied, t + 1)
                pe.wait_ge(row_hot, t + 1)
                pe.matmul(ps[:, 1, :], one(high_hot, t), one(low_hot, t), start=False, stop=False,
                          skip_group_check=True).then_inc(table_added, 1)
                if not first:
                    pe.wait_ge(place_ready, t - 1)
                pe.matmul(ps[:, 2 + q, :], high_row[:, q, :], table[:, q, :], start=True,
                          stop=True).then_inc(looked_up, 1)
            look_up(0, 0, True)
            look_up(1, 1, True)
            with pe.Fori(1, T // 2) as i:
                for q in range(2):
                    look_up(2 * i + q, q, False)

            for k in ("turned", "proj", "rows"):
                pe.sem_inc(edge[k], SEED)

            def message(i, s):
                t = chunk_at(i, s, 2)
                if t:
                    c, q = 4 * t[0] + t[1], t[1] % 2
                    pe.wait_ge(m["sums"], done(c))
                    pe.wait_ge(m["den"], done(c))
                    pe.wait_ge(m["update"], freed(c, 1))
                    for j in range(R):
                        pe.matmul(blocks(6)[:, j, :], by_row(e_sum[q][:, :], j), w_upd[:, 1, :], start=True,
                                  stop=True)
                    for j in range(R):
                        mm = pe.matmul(ps[:, 7, 2 * j:2 * j + 1], by_row(e_den[q][:, :], j), ident[:, 0:1],
                                       start=True, stop=True)
                    mm.then_inc(m["rows"], 1)
                t = chunk_at(i, s, 1)
                if t:
                    c = 4 * t[0] + t[1]
                    pe.wait_ge(m["normed"], done(c))
                    pe.wait_ge(m["turned_copy"], freed(c, 1))
                    for j in range(R):
                        pe.transpose(by_row(bank(0), j), e_norm[:, j, :], ident[:, :])
                    for j in range(R):
                        tr = pe.transpose(by_row(bank(1), j), rows_b[t[1]][:, j, :], ident[:, :])
                    tr.then_inc(m["turned"], 1)
                    pe.wait_ge(m["turned_copy"], done(c))
                    pe.wait_ge(m["value"], freed(c, 1))
                    pe.matmul(bank(2), w_msg[:, 0, :], e_aT[:, :], start=True, stop=False)
                    pe.matmul(bank(2), w_msg[:, 1, :], e_bT[:, :], start=False, stop=True).then_inc(m["proj"], 1)
            chunks(pe, message)

            for k in ("turned", "proj"):
                pe.sem_inc(node[k], SEED)

            def turn(s, n, q, rows):
                wait_q = q % 2
                pe.wait_ge(s["normed"], done(n))
                pe.wait_ge(s["turned_copy"], freed(n, 2))
                for j in range(R):
                    tr = pe.transpose(blocks(wait_q)[:, j, :], rows[:, j, :], ident[:, :])
                tr.then_inc(s["turned"], 1)

            def project(n, q, added, w, free):
                pe.wait_ge(node["turned_copy"], done(n))
                pe.wait_ge(free, freed(n, 4))
                pe.matmul(bank(out_bank(q, 4)), ident[:, :], flat(added), start=True, stop=False, skip_group_check=True)
                for j in range(R):
                    mm = pe.matmul(blocks(out_bank(q, 4))[:, j, :], n_T[q][:, j * P:(j + 1) * P], w, start=False,
                                   stop=j == R - 1, skip_group_check=True)
                mm.then_inc(node["proj"], 1)

            def update_step(i, s):
                t = tile_at(i, s, 3, 8)
                if t:
                    pe.wait_ge(msg_loaded[t[1] % 4], 16 * (2 * t[0] + t[1] // 4 + 1))
                    project(8 * t[0] + t[1], t[1] % 4, n_add[t[1] % 4], w_upd[:, 0, :], u["normed2"])
                t = tile_at(i, s, 2, 8)
                if t:
                    turn(u, 8 * t[0] + t[1], t[1] % 4, n_norm[t[1]])
            pipeline(pe, 10, update_step, 8)

            def embed_step(i, s):
                t = tile_at(i, s, 2)
                if t:
                    turn(b, NT + (4 * t[0] + t[1]), t[1], n_norm[t[1]])
                t = tile_at(i, s, 3)
                if t:
                    project(NT + (4 * t[0] + t[1]), t[1], bo0_wide, w_emb[:, :], b["result"])
            pipeline(pe, 7, embed_step)

            pe.sem_inc(a["score"], EC + SEED)
            for k in ("hidden", "ffn"):
                pe.sem_inc(f[k], 2 * NT + SEED)

            def layer(l, is_last):
                pe.wait_ge(layer_step, 2 * l + 1)
                for n, (w, v) in enumerate(((wq[:, :], VO), (wk[:, :], VO), (wv[:, :], VO),
                                            (w1[:, 0:P], VF2), (w1[:, P:2 * P], VF2))):
                    mm = pe.matmul(ps[:, 7, 2 * n:2 * n + 1], w, layer_cols[:, v:v + 1], start=True, stop=True)
                mm.then_inc(folds_made, 1)

                def attend(i, s):
                    t2 = chunk_at(i, s, 2)
                    if t2:
                        g2 = (l + 1) * EC + (4 * t2[0] + t2[1])
                        pe.wait_ge(a["kq"], done(g2))
                        pe.matmul(bank(5), head_sum[:, :], e_kq[:, :], start=True, stop=True
                                  ).then_inc(a["score"], 1)
                    t = chunk_at(i, s, 1)
                    if t:
                        g, q = (l + 1) * EC + (4 * t[0] + t[1]), t[1]
                        pe.wait_ge(gathered[q], 128 * ((l + 1) * uses(q, EC, 4) + t[0] + 1))
                        pe.wait_ge(a["turned_copy"], freed(g, 1))
                        for j in range(R):
                            pe.transpose(by_row(bank(0), j), rows_a[q][:, j, :], ident[:, :])
                        for j in range(R):
                            tr = pe.transpose(by_row(bank(1), j), rows_b[q][:, j, :], ident[:, :])
                        tr.then_inc(a["turned"], 1)
                        pe.wait_ge(a["turned_copy"], done(g))
                        pe.wait_ge(a["value"], freed(g, 1))
                        pe.matmul(bank(2), wk[:, :], e_aT[:, :], start=True, stop=True)
                        pe.matmul(bank(3), wq[:, :], e_bT[:, :], start=True, stop=True)
                        pe.matmul(bank(4), wv[:, :], e_aT[:, :], start=True, stop=True).then_inc(a["proj"], 1)
                    if t2:
                        pe.wait_ge(a["attn"], done(g2))
                        pe.wait_ge(a["update"], freed(g2, 1))
                        for j in range(R):
                            mm = pe.matmul(blocks(6)[:, j, :], by_row(e_attn[:, :], j), wo[:, :], start=True,
                                           stop=True)
                        mm.then_inc(a["rows"], 1)
                chunks(pe, attend)

                g0 = (l + 2) * NT

                def step(i, s):
                    t = tile_at(i, s, 1)
                    if t:
                        turn(f, g0 + (4 * t[0] + t[1]), t[1], n_norm[t[1]])
                    t = tile_at(i, s, 2)
                    if t:
                        g, q = g0 + (4 * t[0] + t[1]), t[1]
                        pe.wait_ge(f["turned_copy"], done(g))
                        pe.wait_ge(f["relu"], freed(g, 2))
                        for k in range(2):
                            mm = pe.matmul(bank(2 + 2 * (q % 2) + k), w1[:, k * P:(k + 1) * P], n_T[q][:, :],
                                           start=True, stop=True)
                        mm.then_inc(f["hidden"], 1)
                    t = tile_at(i, s, 4)
                    if t:
                        g, q = g0 + (4 * t[0] + t[1]), t[1]
                        pe.wait_ge(f["relu"], done(g))
                        pe.wait_ge(f["normed2"], freed(g, 2))
                        for j in range(R):
                            o, c = blocks(6 + q % 2)[:, j, :], slice(j * P, (j + 1) * P)
                            pe.matmul(o, n_T[q][:, c], ident[:, :], start=True, stop=False, is_transpose=True)
                            pe.matmul(o, n_relu[q][:, 0, c], w2[:, 0, :], start=False, stop=False)
                            mm = pe.matmul(o, n_relu[q][:, 1, c], w2[:, 1, :], start=False, stop=True)
                        mm.then_inc(f["ffn"], 1)
                pipeline(pe, 10, step)

            with pe.Fori(0, L - 1) as l:
                layer(l, False)
            layer(L - 1, True)

        @block.scalar
        def _(act):
            def copy_table(t, q):
                act.wait_ge(table_added, t + 1)
                if not isinstance(t, int) or t >= 2:
                    act.wait_ge(looked_up, t - 1)
                act.copy(table[:, q, :], ps[:, 1, :]).then_inc(table_copied, 1)
            copy_table(0, 0)
            copy_table(1, 1)
            with act.Fori(1, T // 2) as i:
                for q in range(2):
                    copy_table(2 * i + q, q)

            for k in ("std", "turned_copy", "value"):
                act.sem_inc(m[k], SEED)

            def message(i, s):
                t = chunk_at(i, s, 1)
                if t:
                    c = 4 * t[0] + t[1]
                    act.wait_ge(m["mean_var"], done(c))
                    act.activation(e_sd[:, :], e_mv[:, :, 1], ACT.Sqrt, bias=eps[:, 0:1]).then_inc(m["std"], 1)
                    act.wait_ge(m["turned"], done(c))
                    act.wait_ge(m["proj"], freed(c, 1))
                    act.activation(e_aT[:, :], bank(0), ACT.Relu)
                    act.copy(e_bT[:, :], bank(1)).then_inc(m["turned_copy"], 1)
                    act.wait_ge(m["proj"], done(c))
                    act.wait_ge(m["sums"], freed(c, 1))
                    act.activation(e_val[:, :], bank(2), ACT.Relu, bias=vec_cols[:, L * NV:L * NV + 1]
                                   ).then_inc(m["value"], 1)
            act.wait_ge(columns_copied, 1)
            chunks(act, message)

            for k in ("std", "turned_copy", "std2", "normed2"):
                act.sem_inc(node[k], SEED)
            act.sem_inc(u["joined_relu"], SEED)

            def std(s, key, g, q, mv, sd):
                act.wait_ge(s["mean_var" + key], done(g))
                act.activation(sd[q][:, :], mv[q][:, :, 1], ACT.Sqrt, bias=eps[:, 0:1]).then_inc(s["std" + key], 1)

            def copy_turned(s, n, q):
                act.wait_ge(s["turned"], done(n))
                act.wait_ge(s["proj"], freed(n, 4))
                act.activation(n_T[q][:, :], bank(q % 2), ACT.Relu).then_inc(s["turned_copy"], 1)

            def norm2(s, g, q, free, banks):
                act.wait_ge(s["shift2"], done(g))
                act.wait_ge(free, freed(g, 4))
                for j in range(R):
                    ins = act.activation(n_norm2[q][:, j, :], blocks(out_bank(q, banks))[:, j, :], ACT.Identity,
                                         bias=n_sh2[q][:, j:j + 1], scale=n_rs2[q][:, j:j + 1])
                ins.then_inc(s["normed2"], 1)

            def update_step(i, s):
                t = tile_at(i, s, 5, 8)
                if t:
                    norm2(u, 8 * t[0] + t[1], t[1] % 4, u["shifted"], 4)
                t = tile_at(i, s, 7, 8)
                if t:
                    n, q = 8 * t[0] + t[1], t[1] % 4
                    act.wait_ge(u["joined"], done(n))
                    act.activation(flat(n_scaled[q]), flat(n_scaled[q]), ACT.Relu).then_inc(u["joined_relu"], 1)
                t = tile_at(i, s, 4, 8)
                if t:
                    std(u, "2", 8 * t[0] + t[1], t[1] % 4, n_mv2, n_sd2)
                t = tile_at(i, s, 1, 8)
                if t:
                    std(u, "", 8 * t[0] + t[1], t[1] % 4, n_mv, n_sd)
                t = tile_at(i, s, 2, 8)
                if t:
                    copy_turned(u, 8 * t[0] + t[1], t[1] % 4)
            pipeline(act, 10, update_step, 8)

            def embed_step(i, s):
                t = tile_at(i, s, 2)
                if t:
                    copy_turned(b, NT + (4 * t[0] + t[1]), t[1])
                t = tile_at(i, s, 0)
                if t:
                    std(b, "", NT + (4 * t[0] + t[1]), t[1], n_mv, n_sd)
                t = tile_at(i, s, 3)
                if t:
                    n, q = NT + (4 * t[0] + t[1]), t[1]
                    act.wait_ge(b["proj"], done(n))
                    act.wait_ge(b["stored"], freed(n, 4))
                    act.copy(flat(n_out[q]), bank(out_bank(q, 4))).then_inc(b["result"], 1)
            pipeline(act, 7, embed_step)

            for k in ("key", "exp"):
                act.sem_inc(a[k], EC + SEED)
            act.sem_inc(f["relu"], 2 * NT + SEED)
            for k in ("std2", "normed2"):
                act.sem_inc(f[k], NT)

            def layer(l, is_last):
                act.wait_ge(layer_ready, l + 1)

                def attend(i, s):
                    t = chunk_at(i, s, 2)
                    if t:
                        g = (l + 1) * EC + (4 * t[0] + t[1])
                        act.wait_ge(a["clip"], done(g))
                        act.wait_ge(a["sums"], freed(g, 1))
                        act.activation(e_exp[:, :], e_clip[:, :], ACT.Exp).then_inc(a["exp"], 1)
                    t = chunk_at(i, s, 1)
                    if t:
                        g = (l + 1) * EC + (4 * t[0] + t[1])
                        act.wait_ge(a["turned"], done(g))
                        act.wait_ge(a["proj"], freed(g, 1))
                        act.copy(e_aT[:, :], bank(0))
                        act.copy(e_bT[:, :], bank(1)).then_inc(a["turned_copy"], 1)
                        act.wait_ge(a["proj"], done(g))
                        act.wait_ge(a["kq"], freed(g, 1))
                        act.activation(e_key[:, :], bank(2), ACT.Identity, bias=folded[:, 1:2]
                                       ).then_inc(a["key"], 1)
                chunks(act, attend)

                g0 = (l + 2) * NT

                def step(i, s):
                    t = tile_at(i, s, 3)
                    if t:
                        g, q = g0 + (4 * t[0] + t[1]), t[1]
                        act.wait_ge(f["hidden"], done(g))
                        for k in range(2):
                            ins = act.activation(n_relu[q][:, k, :], bank(2 + 2 * (q % 2) + k), ACT.Relu,
                                                 bias=folded[:, 3 + k:4 + k])
                        ins.then_inc(f["relu"], 1)
                    t = tile_at(i, s, 6)
                    if t:
                        std(f, "2", g0 + (4 * t[0] + t[1]), t[1], n_mv2, n_sd2)
                        norm2(f, g0 + (4 * t[0] + t[1]), t[1], f["result"], 2)
                    t = tile_at(i, s, 0)
                    if t:
                        std(f, "", g0 + (4 * t[0] + t[1]), t[1], n_mv, n_sd)
                    t = tile_at(i, s, 1)
                    if t:
                        g, q = g0 + (4 * t[0] + t[1]), t[1]
                        act.wait_ge(f["turned"], done(g))
                        act.wait_ge(f["ffn"], freed(g, 4))
                        act.activation(n_T[q][:, :], bank(q % 2), ACT.Identity, bias=folded[:, 5:6],
                                       scale=layer_cols[:, VG1:VG1 + 1]).then_inc(f["turned_copy"], 1)
                pipeline(act, 10, step)

            with act.Fori(0, L - 1) as l:
                layer(l, False)
            layer(L - 1, True)

        @block.vector
        def _(dve):
            dve.wait_ge(const_loaded, 16 * 17)
            dve.tensor_copy(b_upd_wide[:, :, :], wide(b_upd_row)).then_inc(wide_made, 1)
            dve.tensor_copy(bo0_wide[:, :, :], wide(bo0_row))
            dve.wait_ge(columns_made, 1)
            dve.tensor_copy(vec_cols[:, :], ps[:, 7, 0:L * NV + 1]).then_inc(columns_copied, 1)

            prepared = [0]

            def prep(ins):
                prepared[0] += 1
                ins.then_inc(sort_prep, 1)
                dve.wait_ge(sort_prep, prepared[0])
            dve.wait_ge(consts_made, 2)
            dve.wait_ge(edges_loaded, 48)
            prep(dve.tensor_scalar(part_i[:, :], dst_i[:, :], LOW - 1, None, ALU.bitwise_and))
            prep(dve.tensor_copy(low_c[:, :], part_i[:, :]))
            prep(dve.tensor_copy(dst_c[:, :], dst_i[:, :]))
            prep(dve.tensor_tensor(high_c[:, :], dst_c[:, :], low_c[:, :], ALU.subtract))
            prep(dve.tensor_copy(row_lo[:, :], row_i[:, :]))
            prep(dve.tensor_scalar(row_hi[:, :], row_lo[:, :], float(LOW), None, ALU.add))
            prep(dve.tensor_scalar(counts[:, :], iota_i[:, :], float(LOW), None, ALU.mult))
            prep(dve.tensor_copy(payload[:, :, 0], dst_i[:, :]))
            prep(dve.tensor_copy(payload[:, :, 1], src_i[:, :]))
            prep(dve.tensor_scalar(payload[:, :, 2], num_i[:, :], float(E - 1), None, ALU.min))
            prep(dve.tensor_copy(payload[:, :, 3], num_i[:, :]))

            def one(t3, t):
                return t3[:, t, :] if isinstance(t, int) else \
                    t3[:, bass.ds(t, 1), :].rearrange("p a f -> p (a f)")

            def col(t2, t):
                return t2[:, t:t + 1] if isinstance(t, int) else t2[:, bass.ds(t, 1)]

            with dve.Fori(0, T) as t:
                dve.tensor_scalar(one(high_hot, t), counts[:, 0:P], col(high_c, t), None, ALU.is_equal)
                dve.tensor_scalar(one(low_hot, t), iota_i[:, :], col(low_c, t), None,
                                  ALU.is_equal).then_inc(one_hot, 1)

            dve.wait_ge(counted, 1)
            dve.tensor_copy(counts[:, :], ps[:, 0, :]).then_inc(base_step, 1)
            dve.wait_ge(base_step, 1)
            dve.tensor_tensor_scan(running[:, :], ones[:, :], counts[:, :], 0.0, ALU.mult,
                                   ALU.add).then_inc(base_step, 1)
            dve.wait_ge(row_base, 1)
            dve.tensor_copy(row_start[:, :], ps[:, 4, 0:1]).then_inc(base_step, 1)
            dve.wait_ge(base_step, 3)
            dve.tensor_tensor(running[:, :], running[:, :], counts[:, :], ALU.subtract).then_inc(base_step, 1)
            dve.wait_ge(base_step, 4)
            dve.tensor_scalar(counts[:, :], running[:, :], row_start[:, 0:1], None, ALU.add).then_inc(base_step, 1)

            dst_rows_t = dst_rows[:, :].rearrange("p (e t) -> p t e", t=T)

            def rank_edges(t, q, first):
                if not first:
                    dve.wait_ge(row_hot, t)
                dve.tensor_scalar(in_range[:, :], one(dst_rows_t, t), row_hi[:, 0:1], None,
                                  ALU.is_lt).then_inc(in_range_ready, 1)
                if not first:
                    dve.wait_ge(rank_ready, t)
                dve.scalar_tensor_tensor(running[:, 0:P], one(dst_rows_t, t), col(dst_c, t), earlier[:, :],
                                         ALU.is_equal, ALU.mult, accum_out=col(rank_in, t)
                                         ).then_inc(rank_ready, 1)
                if not isinstance(t, int) or t >= 2:
                    dve.wait_ge(looked_up, t - 1)
                dve.wait_ge(in_range_ready, t + 1)
                dve.scalar_tensor_tensor(high_row[:, q, :], one(dst_rows_t, t), row_lo[:, 0:1], in_range[:, :],
                                         ALU.is_ge, ALU.mult).then_inc(row_hot, 1)

            def place_edges(t, q, landed):
                dve.wait_ge(looked_up, t + 1)
                if landed is not None:
                    dve.wait_ge(found_ready, t)
                dve.scalar_tensor_tensor(counts[:, :], ps[:, 2 + q, :], 1.0, one(low_hot, t), ALU.mult, ALU.mult,
                                         accum_out=col(found, t)).then_inc(found_ready, 1)
                dve.wait_ge(found_ready, t + 1)
                if landed is not None and not (isinstance(t, int) and t < 2):
                    dve.wait_ge(sorted_out[q], 16 * landed)
                dve.tensor_tensor(place[:, q:q + 1], col(found, t), col(rank_in, t),
                                  ALU.add).then_inc(place_ready, 1)
            dve.wait_ge(base_step, 5)
            rank_edges(0, 0, True)
            rank_edges(1, 1, False)
            place_edges(0, 0, None)
            rank_edges(2, 0, False)
            place_edges(1, 1, 0)
            with dve.Fori(1, T // 2 - 1) as i:
                rank_edges(2 * i + 1, 1, False)
                place_edges(2 * i, 0, i)
                rank_edges(2 * i + 2, 0, False)
                place_edges(2 * i + 1, 1, i)
            rank_edges(T - 1, 1, False)
            place_edges(T - 2, 0, T // 2 - 1)
            place_edges(T - 1, 1, T // 2 - 1)

            dve.wait_ge(sorted_loaded, 16)
            sorted_col = lambda k: sorted_rows[:, :, :, k]
            dve.tensor_copy(dst_s[:, :, :], sorted_col(0)).then_inc(dst_col_ready, 1)
            dve.tensor_copy(dst_idx[:, :, :], sorted_col(0)).then_inc(dst_col_ready, 1)
            dve.tensor_copy(src_idx[:, :, :], sorted_col(1))
            dve.tensor_copy(edge_idx[:, :, :], sorted_col(2))
            dve.wait_ge(dst_line_in, 32)
            dve.memset(same[:, 0:1], 0.0)
            dve.tensor_tensor(same[:, 1:EROWS], dst_sorted[:, 1:EROWS], dst_sorted[:, 0:EROWS - 1], ALU.is_equal)
            dve.tensor_tensor(same_next[:, :, :], dst_s[:, :, :], dst_next[:, :, :],
                              ALU.is_equal).then_inc(tables_step, 1)
            dve.wait_ge(tables_step, 1)
            dve.scalar_tensor_tensor(last_idx[:, :, :], same_next[:, :, :], float(SKIP), dst_s[:, :, :],
                                     ALU.mult, ALU.add).then_inc(tables_ready, 1)
            dve.wait_ge(tables_ready, 1)

            def same_of(c):
                return same[:, c * TILE:(c + 1) * TILE] if isinstance(c, int) else \
                    same[:, bass.ds(c * TILE, TILE)]

            def begin(c, t, q):
                return 0.0 if isinstance(c, int) and c == 0 else t[1 - q][:, 511:512]

            for k in ("stats", "mean_var", "rstd", "normed", "sums", "den", "recip", "update"):
                dve.sem_inc(m[k], SEED)

            def message(i, s):
                t1, t2 = chunk_at(i, s, 1), chunk_at(i, s, 2)
                if t2:
                    c, q = 4 * t2[0] + t2[1], t2[1] % 2
                    dve.wait_ge(m["rows"], freed(c, 2))
                    dve.wait_ge(m["den"], freed(c, 1))
                    dve.tensor_tensor_scan(e_den[q][:, :], same_of(c), ones[:, :], begin(c, e_den, q), ALU.mult,
                                           ALU.add).then_inc(m["den"], 1)
                    dve.wait_ge(m["value"], done(c))
                    dve.wait_ge(m["sums"], freed(c, 1))
                    dve.tensor_tensor_scan(e_sum[q][:, :], same_of(c), e_val[:, :], begin(c, e_sum, q), ALU.mult,
                                           ALU.add).then_inc(m["sums"], 1)
                if t1:
                    c, q = 4 * t1[0] + t1[1], t1[1]
                    dve.wait_ge(gathered[q], 128 * (t1[0] + 1))
                    for j in range(R):
                        ins = dve.bn_stats(e_bn[:, j, :], rows_a[q][:, j, :])
                    ins.then_inc(m["stats"], 1)
                    wait_alone(dve, m["stats"], done(c), dve_passed)
                    for j in range(R):
                        ins = dve.bn_aggr(e_mv[:, j, :], e_bn[:, j, :])
                    ins.then_inc(m["mean_var"], 1)
                    dve.wait_ge(m["std"], done(c))
                    dve.reciprocal(e_rs[:, :], e_sd[:, :]).then_inc(m["rstd"], 1)
                    dve.wait_ge(m["rstd"], done(c))
                    dve.wait_ge(m["turned"], freed(c, 1))
                    for j in range(R):
                        ins = dve.tensor_scalar(e_norm[:, j, :], rows_a[q][:, j, :], e_mv[:, j, 0:1],
                                                e_rs[:, j:j + 1], ALU.subtract, ALU.mult)
                    ins.then_inc(m["normed"], 1)
                if t2:
                    c, q = 4 * t2[0] + t2[1], t2[1]
                    dve.wait_ge(m["rows"], done(c))
                    cnt = ps[:, 7, 0:2 * R].rearrange("p (j k) -> p j k", k=2)[:, :, 0]
                    dve.reciprocal(e_rc[:, :], cnt).then_inc(m["recip"], 1)
                    dve.wait_ge(m["recip"], done(c))
                    dve.wait_ge(m["update_free"], freed(c, 4))
                    for j in range(R):
                        ins = dve.scalar_tensor_tensor(upd[q][:, j, :], blocks(6)[:, j, :], e_rc[:, j:j + 1],
                                                       b_upd_row[:, :], ALU.mult, ALU.add)
                    ins.then_inc(m["update"], 1)
            chunks(dve, message)

            def stats(s, key, g, src_blocks, bn):
                for j in range(R):
                    ins = dve.bn_stats(bn[:, j, :], src_blocks[:, j, :])
                ins.then_inc(s["stats" + key], 1)

            def mean_var(s, key, g, bn, mv):
                wait_alone(dve, s["stats" + key], done(g), dve_passed)
                for j in range(R):
                    ins = dve.bn_aggr(mv[:, j, :], bn[:, j, :])
                ins.then_inc(s["mean_var" + key], 1)

            def rstd(s, key, g, q, sd, rs):
                dve.wait_ge(s["std" + key], done(g))
                dve.reciprocal(rs[q][:, :], sd[q][:, :]).then_inc(s["rstd" + key], 1)

            def normalise(s, g, q, rows, normed, depth):
                dve.wait_ge(s["rstd"], done(g))
                dve.wait_ge(s["turned"], freed(g, depth))
                for j in range(R):
                    ins = dve.tensor_scalar(normed[:, j, :], rows[:, j, :], n_mv[q][:, j, 0:1],
                                            n_rs[q][:, j:j + 1], ALU.subtract, ALU.mult)
                ins.then_inc(s["normed"], 1)

            def shift(s, g, q):
                dve.wait_ge(s["rstd2"], done(g))
                dve.scalar_tensor_tensor(n_sh2[q][:, :], n_mv2[q][:, :, 0], -1.0, n_rs2[q][:, :], ALU.mult,
                                         ALU.mult).then_inc(s["shift2"], 1)

            for k in ("stats", "mean_var", "rstd", "normed", "stats2", "mean_var2", "rstd2", "shift2"):
                dve.sem_inc(node[k], SEED)
            dve.sem_inc(u["joined"], SEED)

            def update_step(i, s):
                t1, t2, t4, t5, t7 = (tile_at(i, s, lag, 8) for lag in (1, 2, 4, 5, 7))
                if t4:
                    n4, q4 = 8 * t4[0] + t4[1], t4[1] % 4
                    dve.wait_ge(u["proj"], done(n4))
                    stats(u, "2", n4, blocks(out_bank(q4, 4)), n_bn2[q4])
                if t5:
                    shift(u, 8 * t5[0] + t5[1], t5[1] % 4)
                if t2:
                    n2, q2 = 8 * t2[0] + t2[1], t2[1] % 4
                    rstd(u, "", n2, q2, n_sd, n_rs)
                if t7:
                    n7, q7 = 8 * t7[0] + t7[1], t7[1] % 4
                    dve.wait_ge(u["shifted"], done(n7))
                    dve.scalar_tensor_tensor(flat(n_scaled[q7]), flat(n_norm[t7[1]]), 0.0, flat(n_scaled[q7]),
                                             ALU.max, ALU.add).then_inc(u["joined"], 1)
                if t4:
                    mean_var(u, "2", n4, n_bn2[q4], n_mv2[q4])
                if t1:
                    n1, q1 = 8 * t1[0] + t1[1], t1[1] % 4
                    dve.wait_ge(u_loaded[t1[1]], 16 * (t1[0] + 1))
                    stats(u, "", n1, n_in[t1[1]], n_bn[q1])
                if t2:
                    normalise(u, n2, q2, n_in[t2[1]], n_norm[t2[1]], 8)
                if t4:
                    rstd(u, "2", n4, q4, n_sd2, n_rs2)
                if t1:
                    mean_var(u, "", n1, n_bn[q1], n_mv[q1])
            pipeline(dve, 10, update_step, 8)

            def embed_step(i, s):
                t0, t1, t2 = (tile_at(i, s, lag) for lag in (0, 1, 2))
                if t2:
                    n2, q2 = NT + (4 * t2[0] + t2[1]), t2[1]
                    normalise(b, n2, q2, n_in[q2], n_norm[q2], 4)
                if t0:
                    n0, q0 = NT + (4 * t0[0] + t0[1]), t0[1]
                    dve.wait_ge(n_loaded[q0], 16 * (t0[0] + 1))
                    stats(b, "", n0, n_in[q0], n_bn[q0])
                if t1:
                    rstd(b, "", NT + (4 * t1[0] + t1[1]), t1[1], n_sd, n_rs)
                if t0:
                    mean_var(b, "", n0, n_bn[q0], n_mv[q0])
            pipeline(dve, 7, embed_step)

            for k in ("kq", "clip", "attn"):
                dve.sem_inc(a[k], EC + SEED)
            dve.sem_inc(a["recip"], 2 * EC + SEED)
            for k in ("stats2", "mean_var2", "rstd2", "shift2"):
                dve.sem_inc(f[k], NT)

            def layer(l, is_last):
                count = (9 * l + 8) if is_last else (9 * l + 9)
                dve.wait_ge(weights_loaded, 16 * count)
                names = vec_cols[:, 0:NV * L].rearrange("p (n l) -> p n l", l=L)
                pick = names[:, :, l] if isinstance(l, int) else \
                    names[:, :, bass.ds(l, 1)].rearrange("p n a -> p (n a)")
                if not is_last:
                    dve.tensor_tensor(b2_row[:, :], b2_row[:, :], bo_row[:, :], ALU.add)
                dve.tensor_copy(layer_cols[:, :], pick).then_inc(layer_step, 1)
                dve.wait_ge(layer_step, 2 * l + 1)
                dve.wait_ge(folds_made, l + 1)
                fold = ps[:, 7, 0:10].rearrange("p (n k) -> p n k", k=2)[:, :, 0]
                dve.tensor_tensor(folded[:, 0:3], layer_cols[:, VQ:VV + 1], fold[:, 0:3], ALU.subtract)
                dve.tensor_tensor(folded[:, 3:5], layer_cols[:, VF0:VF1 + 1], fold[:, 3:5], ALU.subtract)
                dve.tensor_tensor(folded[:, 5:6], layer_cols[:, VB1:VB1 + 1], layer_cols[:, VF2:VF2 + 1],
                                  ALU.add).then_inc(layer_step, 1)
                dve.wait_ge(layer_step, 2 * l + 2)
                dve.sem_inc(layer_ready, 1)

                def attend(i, s):
                    t, t3 = chunk_at(i, s, 2), chunk_at(i, s, 3)
                    if t:
                        c, q = 4 * t[0] + t[1], t[1] % 2
                        g = (l + 1) * EC + c
                        dve.wait_ge(a["key"], done(g))
                        dve.wait_ge(a["score"], freed(g, 1))
                        dve.scalar_tensor_tensor(e_kq[:, :], bank(3), folded[:, 0:1], e_key[:, :], ALU.add,
                                                 ALU.mult).then_inc(a["kq"], 1)
                    if t3:
                        g3, q3 = (l + 1) * EC + (4 * t3[0] + t3[1]), t3[1]
                        dve.wait_ge(a["rows"], done(g3))
                        dve.wait_ge(a["update_free"], freed(g3, 4))
                        dve.tensor_tensor(flat(upd[q3]), bank(6), flat(rows_b[q3]), ALU.add
                                          ).then_inc(a["update"], 1)
                    if t:
                        dve.wait_ge(a["score"], done(g))
                        dve.wait_ge(a["exp"], freed(g, 1))
                        dve.tensor_scalar(e_clip[:, :], bank(5), -5.0, 5.0, ALU.max, ALU.min
                                          ).then_inc(a["clip"], 1)
                        dve.wait_ge(a["exp"], done(g))
                        dve.scalar_tensor_tensor(e_val[:, :], bank(4), folded[:, 2:3], e_exp[:, :], ALU.add,
                                                 ALU.mult).then_inc(a["value"], 1)
                        dve.wait_ge(a["den"], freed(g, 1))
                        dve.tensor_tensor_scan(e_den[q][:, :], same_of(c), e_exp[:, :], begin(c, e_den, q),
                                               ALU.mult, ALU.add).then_inc(a["den"], 1)
                        dve.wait_ge(a["value"], done(g))
                        dve.wait_ge(a["sums"], freed(g, 1))
                        dve.tensor_tensor_scan(e_sum[q][:, :], same_of(c), e_val[:, :], begin(c, e_sum, q),
                                               ALU.mult, ALU.add).then_inc(a["sums"], 1)
                        dve.wait_ge(a["den"], done(g))
                        dve.tensor_scalar(e_rden[:, :], e_den[q][:, :], 1e-6, None, ALU.add
                                          ).then_inc(a["recip"], 1)
                        dve.wait_ge(a["recip"], 2 * g + (SEED + 1))
                        dve.reciprocal(e_rinv[:, :], e_rden[:, :]).then_inc(a["recip"], 1)
                        dve.wait_ge(a["recip"], 2 * g + (SEED + 2))
                        dve.wait_ge(a["sums"], done(g))
                        dve.wait_ge(a["rows"], freed(g, 1))
                        dve.tensor_tensor(e_attn[:, :], e_sum[q][:, :], e_rinv[:, :], ALU.mult
                                          ).then_inc(a["attn"], 1)
                chunks(dve, attend)

                g0 = (l + 2) * NT

                def step(i, s):
                    t0, t1, t6 = (tile_at(i, s, lag) for lag in (0, 1, 6))
                    if t6:
                        g6, q6 = g0 + (4 * t6[0] + t6[1]), t6[1]
                        dve.wait_ge(f["ffn"], done(g6))
                        stats(f, "2", g6, blocks(out_bank(q6, 2)), n_bn2[q6])
                        mean_var(f, "2", g6, n_bn2[q6], n_mv2[q6])
                    if t0:
                        g0_, q0 = g0 + (4 * t0[0] + t0[1]), t0[1]
                        dve.wait_ge(n_loaded[q0], 16 * ((l + 1) * uses(q0, NT, 4) + t0[0] + 1))
                        stats(f, "", g0_, n_in[q0], n_bn[q0])
                    if t1:
                        g1, q1 = g0 + (4 * t1[0] + t1[1]), t1[1]
                        rstd(f, "", g1, q1, n_sd, n_rs)
                        normalise(f, g1, q1, n_in[q1], n_norm[q1], 4)
                    if t6:
                        rstd(f, "2", g6, q6, n_sd2, n_rs2)
                        shift(f, g6, q6)
                    if t0:
                        mean_var(f, "", g0_, n_bn[q0], n_mv[q0])
                pipeline(dve, 10, step)

            with dve.Fori(0, L - 1) as l:
                layer(l, False)
            layer(L - 1, True)


_INS = ["x", "src", "dst", "edge_attr_128", "L0_gnn_W_msg", "L0_gnn_b_msg", "L0_gnn_W_upd", "L0_gnn_b_upd",
        "L0_gnn_gamma", "L0_gnn_beta", "L1_gnn_Wemb", "L1_gnn_Wq", "L1_gnn_bq", "L1_gnn_Wk", "L1_gnn_bk",
        "L1_gnn_Wv", "L1_gnn_bv", "L1_gnn_Wo", "L1_gnn_bo", "L1_gnn_ln1_g", "L1_gnn_ln1_b", "L1_gnn_W1",
        "L1_gnn_b1", "L1_gnn_W2", "L1_gnn_b2", "L1_gnn_ln2_g", "L1_gnn_ln2_b"]


def kernel(**inputs):
    import numpy as np
    import concourse.bacc as bacc
    from concourse.bass_utils import run_bass_kernel_spmd

    nc = bacc.Bacc("TRN2", target_bir_lowering=False, num_devices=1)
    arrays, args = {}, []
    for name in _INS:
        arr = np.ascontiguousarray(inputs[name])
        arrays[f"in_{name}"] = arr
        args.append(nc.dram_tensor(f"in_{name}", arr.shape, mybir.dt.from_np(arr.dtype),
                                   kind="ExternalInput").ap())
    out = nc.dram_tensor("out_0", inputs["x"].shape, F32, kind="ExternalOutput").ap()
    build(nc, *args, out)
    r = run_bass_kernel_spmd(nc, [arrays], core_ids=[0])
    return r.results[0]["out_0"]
```

```python
from contextlib import ExitStack

import concourse.bass as bass
from concourse import mybir

F32 = mybir.dt.float32
BF16 = mybir.dt.bfloat16
F16 = mybir.dt.float16
I32 = mybir.dt.int32
ALU = mybir.AluOpType
ACT = mybir.ActivationFunctionType

P = 128
R = 4
TILE = P * R
LOW = 512
SEED = 8
EPS = 1e-5
SKIP = 1 << 20
HEADS = 8


def build(nc, x, src, dst, edge_attr, W_msg, b_msg, W_upd, b_upd, gamma, beta, Wemb, Wq, bq, Wk, bk,
          Wv, bv, Wo, bo, ln1_g, ln1_b, W1, b1, W2, b2, ln2_g, ln2_b, out):
    N, E, L = x.shape[0], src.shape[0], Wq.shape[0]
    HD = P // HEADS
    NT = -(-N // TILE)
    NROWS = NT * TILE
    TAIL = (N - (NT - 1) * TILE) // R
    EC = -(-E // TILE)
    EROWS = EC * TILE
    T = EROWS // P
    EP = E // T
    assert N % R == 0 and N < NROWS and E % T == 0 and EC % 2 == 1 and NROWS <= P * LOW

    h_tab = nc.dram_tensor("h_tab", (NROWS, P), F32, kind="Internal").ap()
    y_tab = nc.dram_tensor("y_tab", (NROWS, P), F32, kind="Internal").ap()
    x1_tab = nc.dram_tensor("x1_tab", (NROWS, P), F32, kind="Internal").ap()
    msg_tab = nc.dram_tensor("msg_tab", (NROWS, P), F32, kind="Internal").ap()
    sorted_tab = nc.dram_tensor("sorted_tab", (EROWS, 4), I32, kind="Internal").ap()
    dst_line = nc.dram_tensor("dst_line", (EROWS + R,), I32, kind="Internal").ap()

    ctx = ExitStack()
    with ctx:
        def sb(name, shape, dt=F32, stack=ctx):
            return stack.enter_context(nc.sbuf_tensor(name, shape, dt))

        def sem(name):
            return ctx.enter_context(nc.semaphore(name))

        ps = ctx.enter_context(nc.psum_tensor("ps", [P, 8, 512], F32))

        ident = sb("ident", [P, P])
        ones = sb("ones", [P, 512])
        head_sum = sb("head_sum", [P, P])
        before = sb("before", [P, P])
        earlier = sb("earlier", [P, P])
        eps = sb("eps", [P, 1])
        w_msg = sb("w_msg", [P, 2, P])
        w_upd = sb("w_upd", [P, 2, P])
        w_emb = sb("w_emb", [P, P])
        NV = 9
        VQ, VK, VV, VO, VG1, VB1, VF0, VF1, VF2 = range(NV)
        vec_rows = sb("vec_rows", [P, P])
        vec_cols = sb("vec_cols", [P, L * NV + 1])
        layer_cols = sb("layer_cols", [P, NV])
        folded = sb("folded", [P, 6])
        b_upd_row = sb("b_upd_row", [P, P])
        gamma_row = sb("gamma_row", [P, P])
        beta_row = sb("beta_row", [P, P])
        bo0_row = sb("bo0_row", [P, P])
        g2_row = sb("g2_row", [P, P])
        b2_row = sb("b2_row", [P, P])
        bo_row = sb("bo_row", [P, P])
        ending = sb("ending", [P, R], I32)
        b_upd_wide = sb("b_upd_wide", [P, R, P])

        const_loaded = sem("const_loaded")
        pool_passed = sem("pool_passed")
        dve_passed = sem("dve_passed")
        consts_made = sem("consts_made")
        consts_step = sem("consts_step")
        edges_loaded = sem("edges_loaded")
        dst_rows_loaded = sem("dst_rows_loaded")
        columns_made = sem("columns_made")
        columns_copied = sem("columns_copied")
        sort_prep = sem("sort_prep")
        one_hot = sem("one_hot")
        counted = sem("counted")
        base_step = sem("base_step")
        row_base = sem("row_base")
        seeded = sem("seeded")
        table_copied = sem("table_copied")
        table_added = sem("table_added")
        row_hot = sem("row_hot")
        rank_ready = sem("rank_ready")
        looked_up = sem("looked_up")
        in_range_ready = sem("in_range_ready")
        found_ready = sem("found_ready")
        place_ready = sem("place_ready")
        payload_copied = sem("payload_copied")
        sorted_out = [sem(f"sorted_out{i}") for i in range(4)]
        sorted_done = sem("sorted_done")
        sorted_loaded = sem("sorted_loaded")
        dst_col_ready = sem("dst_col_ready")
        dst_line_out = sem("dst_line_out")
        dst_line_in = sem("dst_line_in")
        tables_step = sem("tables_step")
        tables_ready = sem("tables_ready")
        wide_made = sem("wide_made")
        bo0_made = sem("bo0_made")
        msg_filled = sem("msg_filled")

        def named(k, names):
            return {n: sem(f"{k}_{n}") for n in names}

        edge = named("edge", ["idx", "turned", "turned_copy", "proj", "value", "sums", "den", "rows", "update",
                              "update_free"])
        m = edge | named("m", ["stats", "mean_var", "std", "rstd", "normed", "recip"])
        a = edge | named("a", ["key", "kq", "score", "clip", "exp", "recip", "attn"])
        gathered = [sem(f"gathered{i}") for i in range(4)]
        scattered = [sem(f"scattered{i}") for i in range(4)]
        m_done = sem("m_done")
        a_done = sem("a_done")

        node = named("node", ["stats", "mean_var", "std", "rstd", "normed", "turned", "turned_copy", "result",
                              "stored", "proj", "stats2", "mean_var2", "std2", "rstd2", "shift2", "normed2",
                              "scaled"])
        u = node | named("u", ["shifted", "joined", "joined_relu", "stats3", "mean_var3", "std3", "rstd3", "shift3",
                               "normed3", "turned3", "turned_copy3", "proj3", "embedded", "h_stored"])
        f = node | named("f", ["hidden", "relu", "ffn", "shifted"])
        u_loaded = [sem(f"u_loaded{i}") for i in range(8)]
        msg_loaded = [sem(f"msg_loaded{i}") for i in range(4)]
        x1_loaded = [sem(f"x1_loaded{i}") for i in range(4)]
        n_loaded = [sem(f"n_loaded{i}") for i in range(4)]
        n_stored = [sem(f"n_stored{i}") for i in range(4)]
        h_landed = [sem(f"h_landed{i}") for i in range(4)]
        weights_loaded = sem("weights_loaded")
        layer_step = sem("layer_step")
        folds_made = sem("folds_made")
        layer_ready = sem("layer_ready")

        with ExitStack() as sort_ctx:
            def st(name, shape, dt=F32):
                return sb(name, shape, dt, sort_ctx)
            low_hot = st("low_hot", [P, T, LOW], BF16)
            high_hot = st("high_hot", [P, T, P], BF16)
            dst_rows = st("dst_rows", [P, EROWS], I32)
            dst_i = st("dst_i", [P, T], I32)
            src_i = st("src_i", [P, T], I32)
            num_i = st("num_i", [P, T], I32)
            part_i = st("part_i", [P, T], I32)
            dst_c = st("dst_c", [P, T])
            high_c = st("high_c", [P, T])
            low_c = st("low_c", [P, T])
            payload = st("payload", [P, T, 4], I32)
            iota_i = st("iota_i", [P, LOW], I32)
            low_key = st("low_key", [P, LOW], F16)
            high_key = st("high_key", [P, P], F16)
            row_lo = st("row_lo", [P, 1])
            row_hi = st("row_hi", [P, 1])
            row_i = st("row_i", [P, 1], I32)
            table = st("table", [P, 2, LOW])
            counts = st("counts", [P, LOW])
            running = st("running", [P, LOW])
            row_start = st("row_start", [P, 1])
            in_range = st("in_range", [P, P])
            high_row = st("high_row", [P, 2, P])
            rank_in = st("rank_in", [P, T])
            found = st("found", [P, T])
            place = st("place", [P, 4], I32)
            load_out = st("load_out", [P, 4, 4], I32)

        wq, wk, wv, wo = (sb(f"w{n}", [P, P]) for n in "qkvo")
        w1 = sb("w1", [P, 2 * P])
        w2 = sb("w2", [P, 2, P])

        same = sb("same", [P, EROWS], BF16)
        src_idx = sb("src_idx", [P, EC, R], I32)
        dst_idx = sb("dst_idx", [P, EC, R], I32)
        edge_idx = sb("edge_idx", [P, EC, R], I32)
        last_idx = sb("last_idx", [P, EC, R], I32)

        idx_a = [sb(f"idx_a{i}", [P, R], I32) for i in range(4)]
        idx_b = [sb(f"idx_b{i}", [P, R], I32) for i in range(4)]
        idx_c = [sb(f"idx_c{i}", [P, R], I32) for i in range(4)]
        rows_a = [sb(f"rows_a{i}", [P, R, P]) for i in range(4)]
        rows_b = [sb(f"rows_b{i}", [P, R, P]) for i in range(4)]

        with ExitStack() as table_ctx:
            def tb(name, shape, dt=F32):
                return sb(name, shape, dt, table_ctx)
            sorted_rows = tb("sorted_rows", [P, EC, R, 4], I32)
            dst_s = tb("dst_s", [P, EC, R], I32)
            dst_next = tb("dst_next", [P, EC, R], I32)
            dst_sorted = tb("dst_sorted", [P, EROWS], I32)
            same_next = tb("same_next", [P, EC, R])

        upd = [sb(f"upd{i}", [P, R, P]) for i in range(4)]
        e_norm = sb("e_norm", [P, R, P])
        e_aT = sb("e_aT", [P, 512])
        e_bT = sb("e_bT", [P, 512])
        e_key = sb("e_key", [P, 512])
        e_kq = sb("e_kq", [P, 512])
        e_clip = sb("e_clip", [P, 512])
        e_exp = sb("e_exp", [P, 512])
        e_val = sb("e_val", [P, 512])
        e_sum = [sb(f"e_sum{i}", [P, 512]) for i in range(2)]
        e_den = [sb(f"e_den{i}", [P, 512]) for i in range(2)]
        e_rden = sb("e_rden", [P, 512])
        e_rinv = sb("e_rinv", [P, 512])
        e_attn = sb("e_attn", [P, 512])
        e_rc = sb("e_rc", [P, R])
        e_bn = sb("e_bn", [P, R, 6])
        e_mv = sb("e_mv", [P, R, 2])
        e_sd = sb("e_sd", [P, R])
        e_rs = sb("e_rs", [P, R])

        def ring(name, shape, dt=F32):
            return [sb(f"{name}{i}", shape, dt) for i in range(4)]
        bo0_wide = sb("bo0_wide", [P, R, P])
        n_in = [sb(f"n_in{i}", [P, R, P]) for i in range(8)]
        n_add = ring("n_add", [P, R, P])
        n_norm = [sb(f"n_norm{i}", [P, R, P]) for i in range(8)]
        n_T = ring("n_T", [P, 512])
        n_relu = ring("n_relu", [P, 2, 512])
        n_h = ring("n_h", [P, R, P])
        n_norm2 = ring("n_norm2", [P, R, P])
        n_scaled = ring("n_scaled", [P, R, P])
        n_out = ring("n_out", [P, R, P])
        n_bn = ring("n_bn", [P, R, 6])
        n_mv = ring("n_mv", [P, R, 2])
        n_sd = ring("n_sd", [P, R])
        n_rs = ring("n_rs", [P, R])
        n_bn2 = ring("n_bn2", [P, R, 6])
        n_mv2 = ring("n_mv2", [P, R, 2])
        n_sd2 = ring("n_sd2", [P, R])
        n_rs2 = ring("n_rs2", [P, R])
        n_sh2 = ring("n_sh2", [P, R])
        n_bn3 = ring("n_bn3", [P, R, 6])
        n_mv3 = ring("n_mv3", [P, R, 2])
        n_sd3 = ring("n_sd3", [P, R])
        n_rs3 = ring("n_rs3", [P, R])
        n_sh3 = ring("n_sh3", [P, R])
        n_norm3 = [t[:, 0, :].rearrange("p (j f) -> p j f", j=R) for t in n_relu]
        n_T3 = [t[:, 1, :] for t in n_relu]

        node_view = lambda tab: tab.rearrange("(n p j) f -> n p (j f)", p=P, j=R)
        flat = lambda t: t[:, :, :].rearrange("p j f -> p (j f)")
        wide = lambda row: row[:, :].unsqueeze(1).to_broadcast([P, R, P])
        bank = lambda n: ps[:, n, :]
        blocks = lambda n: ps[:, n, :].rearrange("p (j f) -> p j f", j=R)
        by_row = lambda t, j: t.rearrange("f (p j) -> f j p", j=R)[:, j, :]

        done = lambda g: g + (SEED + 1)
        freed = lambda g, depth: g + (SEED + 1 - depth)
        uses = lambda q, n, depth: (n - q + depth - 1) // depth

        def item_at(i, s, lag, depth, count):
            if isinstance(i, int):
                n = depth * i + s - lag
                return (n // depth, n % depth) if 0 <= n < count else None
            return i + (s - lag) // depth, (s - lag) % depth

        def steps(eng, count, lags, step, depth, ahead=0):
            first, end = -(-lags // depth), (count - 1 - ahead) // depth
            if end <= first:
                first = end = 0
            for n in range(depth * first):
                step(n // depth, n % depth)
            if end:
                with eng.Fori(first, end) as i:
                    for s in range(depth):
                        step(i, s)
            for n in range(depth * end, count + lags):
                step(n // depth, n % depth)

        def tile_at(i, s, lag, depth=4):
            return item_at(i, s, lag, depth, NT)

        def pipeline(eng, lags, step, depth=4):
            steps(eng, NT, lags, step, depth)

        def chunk_at(i, s, lag):
            return item_at(i, s, lag, 4, EC)

        def chunks(eng, step, ahead=0):
            steps(eng, EC, 6, step, 4, ahead)

        def wait_alone(eng, s, value, passed):
            eng.wait_ge(s, value)
            eng.sem_inc(passed, 1)

        block = ctx.enter_context(nc.Block())

        @block.sync
        def _(sp):
            loads = [(w_msg[:, :, :], W_msg.rearrange("(c k) f -> k c f", k=P)),
                     (w_upd[:, :, :], W_upd.rearrange("(c k) f -> k c f", k=P)),
                     (w_emb[:, :], Wemb)]
            for n, v in ((VQ, bq), (VK, bk), (VV, bv), (VO, bo), (VG1, ln1_g), (VB1, ln1_b),
                         (VF0, b1[:, 0:P]), (VF1, b1[:, P:2 * P]), (VF2, b2)):
                loads.append((vec_rows[n * L:(n + 1) * L, :], v))
            loads.append((vec_rows[NV * L:NV * L + 1, :], b_msg.unsqueeze(0)))
            for t, v in ((b_upd_row, b_upd), (gamma_row, gamma), (beta_row, beta), (bo0_row, bo[0])):
                loads.append((t[:, :], v.partition_broadcast(P)))
            sp.wait_ge(consts_made, 1)
            sp.dma_start(dst_i[0:EP, :], dst.rearrange("(p t) -> p t", t=T)).then_inc(edges_loaded, 16)
            sp.dma_start(src_i[0:EP, :], src.rearrange("(p t) -> p t", t=T)).then_inc(edges_loaded, 16)
            sp.dma_start(dst_rows[:, 0:E], dst.partition_broadcast(P)).then_inc(dst_rows_loaded, 16)
            for t, v in loads:
                sp.dma_start(t, v).then_inc(const_loaded, 16)

            sp.wait_ge(wide_made, 1)
            with sp.Fori(0, NT) as n:
                sp.dma_start(node_view(msg_tab)[n], flat(b_upd_wide)).then_inc(msg_filled, 16)

            sp.wait_ge(sorted_done, 1)
            sp.dma_start(sorted_rows[:, :, :, :].rearrange("p c j w -> p c (j w)"),
                         sorted_tab.rearrange("(c p j) w -> p c (j w)", p=P, j=R)).then_inc(sorted_loaded, 16)
            sp.wait_ge(dst_col_ready, 2)
            sp.dma_start(dst_line[0:EROWS].rearrange("(c p j) -> p c j", p=P, j=R),
                         dst_s[:, :, :]).then_inc(dst_line_out, 16)
            sp.dma_start(dst_line[EROWS:EROWS + R].unsqueeze(0), ending[0:1, :]).then_inc(dst_line_out, 16)
            sp.wait_ge(dst_line_out, 32)
            sp.dma_start(dst_sorted[:, :], dst_line[0:EROWS].partition_broadcast(P)).then_inc(dst_line_in, 16)
            sp.dma_start(dst_next[:, :, :], dst_line[1:EROWS + 1].rearrange("(c p j) -> p c j", p=P, j=R)
                         ).then_inc(dst_line_in, 16)

            def load(dst_t, tab, n, is_tail, s):
                if is_tail:
                    rows = tab[(NT - 1) * TILE:N, :].rearrange("(p j) f -> p (j f)", j=R)
                    sp.dma_start(flat(dst_t)[0:TAIL, :], rows).then_inc(s, 16)
                else:
                    sp.dma_start(flat(dst_t), node_view_full(tab, n)).then_inc(s, 16)

            def node_view_full(tab, n):
                return tab[0:(tab.shape[0] // TILE) * TILE, :].rearrange("(n p j) f -> n p (j f)", p=P, j=R)[n]

            def number(t):
                return 4 * t[0] + t[1]

            sp.wait_ge(m_done, 1)
            sp.sem_inc(node["stored"], SEED)
            sp.sem_inc(u["h_stored"], SEED)

            def update_step(i, s):
                t = tile_at(i, s, 0, 8)
                if t:
                    n = 8 * t[0] + t[1]
                    sp.wait_ge(u["result"], freed(n, 8))
                    load(n_in[t[1]], x, n, isinstance(n, int) and n == NT - 1, u_loaded[t[1]])
                    sp.wait_ge(u["proj"], freed(n, 4))
                    sp.dma_start(flat(n_add[t[1] % 4]), node_view(msg_tab)[n]).then_inc(msg_loaded[t[1] % 4], 16)
                t = tile_at(i, s, 7, 8)
                if t:
                    n = 8 * t[0] + t[1]
                    sp.wait_ge(u["result"], done(n))
                    sp.dma_start(node_view(x1_tab)[n], flat(n_out[t[1] % 4])).then_inc(n_stored[t[1] % 4], 16)
                t = tile_at(i, s, 11, 8)
                if t:
                    n, q = 8 * t[0] + t[1], t[1] % 4
                    sp.wait_ge(u["embedded"], done(n))
                    sp.dma_start(node_view(h_tab)[n], flat(n_h[q])).then_inc(h_landed[q], 16)
                    sp.dma_start(node_view(y_tab)[n], flat(n_h[q])).then_inc(h_landed[q], 16)
                t = tile_at(i, s, 9, 8)
                if t:
                    sp.wait_ge(n_stored[t[1] % 4], 16 * (2 * t[0] + t[1] // 4 + 1))
                    sp.sem_inc(u["stored"], 1)
                t = tile_at(i, s, 12, 8)
                if t:
                    sp.wait_ge(h_landed[t[1] % 4], 32 * (2 * t[0] + t[1] // 4 + 1))
                    sp.sem_inc(u["h_stored"], 1)
            pipeline(sp, 13, update_step, 8)

            def layer(l, is_last):
                for t, v in ((wq[:, :], Wq[l]), (wk[:, :], Wk[l]), (wv[:, :], Wv[l]), (wo[:, :], Wo[l]),
                             (w1[:, :], W1[l]), (w2[:, :, :], W2[l].rearrange("(c k) f -> k c f", k=P)),
                             (g2_row[:, :], ln2_g[l].partition_broadcast(P)),
                             (b2_row[:, :], ln2_b[l].partition_broadcast(P))):
                    sp.dma_start(t, v).then_inc(weights_loaded, 16)
                if not is_last:
                    sp.dma_start(bo_row[:, :], bo[l + 1].partition_broadcast(P)).then_inc(weights_loaded, 16)
                sp.wait_ge(a_done, l + 1)
                g0 = (l + 1) * NT

                def step(i, s):
                    t = tile_at(i, s, 0)
                    if t:
                        n = number(t)
                        sp.wait_ge(f["normed"], freed(g0 + n, 4))
                        sp.dma_start(flat(n_in[t[1]]), node_view(y_tab)[n]).then_inc(n_loaded[t[1]], 16)
                    t = tile_at(i, s, 5)
                    if t and is_last:
                        n = number(t)
                        sp.wait_ge(f["result"], freed(g0 + n, 4))
                        sp.dma_start(flat(n_add[t[1]]), node_view(x1_tab)[n]).then_inc(x1_loaded[t[1]], 16)
                    t = tile_at(i, s, 9)
                    if t:
                        n = number(t)
                        sp.wait_ge(f["result"], done(g0 + n))
                        if not is_last:
                            sp.dma_start(node_view(h_tab)[n], flat(n_out[t[1]])).then_inc(n_stored[t[1]], 16)
                            sp.dma_start(node_view(y_tab)[n], flat(n_out[t[1]])).then_inc(n_stored[t[1]], 16)
                        elif isinstance(n, int) and n == NT - 1:
                            rows = out[(NT - 1) * TILE:N, :].rearrange("(p j) f -> p (j f)", j=R)
                            sp.dma_start(rows, flat(n_out[t[1]])[0:TAIL, :]).then_inc(n_stored[t[1]], 32)
                        else:
                            sp.dma_start(node_view_full(out, n), flat(n_out[t[1]])).then_inc(n_stored[t[1]], 32)
                    t = tile_at(i, s, 10)
                    if t:
                        sp.wait_ge(n_stored[t[1]], 16 * uses(t[1], NT, 4) + 32 * (l * uses(t[1], NT, 4) + t[0] + 1))
                        sp.sem_inc(f["stored"], 1)
                pipeline(sp, 11, step)

            with sp.Fori(0, L - 1) as l:
                layer(l, False)
            layer(L - 1, True)

        @block.gpsimd
        def _(pool):
            made = [0]

            def step(ins):
                made[0] += 1
                ins.then_inc(consts_step, 1)
                pool.wait_ge(consts_step, made[0])

            step(pool.memset(dst_i[:, :], N))
            step(pool.memset(src_i[:, :], 0))
            step(pool.memset(dst_rows[:, E:EROWS], N))
            pool.sem_inc(consts_made, 1)
            step(pool.memset(ones[:, :], 1.0))
            step(pool.memset(ident[:, :], 0.0))
            step(pool.affine_select(out=ident[:, :], in_=ident[:, :], compare_op=ALU.not_equal, fill=1.0, base=0,
                                    pattern=[[-1, P]], channel_multiplier=1))
            step(pool.affine_select(out=before[:, :], in_=ones[:, 0:P], compare_op=ALU.is_ge, fill=0.0, base=-1,
                                    pattern=[[1, P]], channel_multiplier=-1))
            step(pool.affine_select(out=earlier[:, :], in_=ones[:, 0:P], compare_op=ALU.is_ge, fill=0.0, base=-1,
                                    pattern=[[-1, P]], channel_multiplier=1))
            hs = head_sum[:, :].rearrange("p (h d) -> p h d", h=HEADS)
            step(pool.memset(head_sum[:, :], float(HD) ** -0.5))
            step(pool.affine_select(out=hs, in_=hs, compare_op=ALU.is_ge, fill=0.0, base=0,
                                    pattern=[[-HD, HEADS], [0, HD]], channel_multiplier=1))
            step(pool.affine_select(out=hs, in_=hs, compare_op=ALU.is_ge, fill=0.0, base=HD - 1,
                                    pattern=[[HD, HEADS], [0, HD]], channel_multiplier=-1))
            step(pool.memset(eps[:, :], EPS))
            step(pool.iota(iota_i[:, :], pattern=[[1, LOW]], base=0, channel_multiplier=0))
            step(pool.iota(num_i[:, :], pattern=[[1, T]], base=0, channel_multiplier=T))
            step(pool.iota(row_i[:, :], pattern=[[0, 1]], base=0, channel_multiplier=LOW))
            step(pool.memset(ending[:, :], -1))
            pool.sem_inc(consts_made, 1)

            pool.sem_inc(payload_copied, SEED)

            def place_out(t, q, use, first):
                wait_alone(pool, place_ready, t + 1, pool_passed)
                if not first:
                    wait_alone(pool, sorted_out[q], 16 * use, pool_passed)
                pool.tensor_copy(load_out[:, q, :], payload[:, t, :] if isinstance(t, int) else
                                 payload[:, bass.ds(t, 1), :].rearrange("p a w -> p (a w)")
                                 ).then_inc(payload_copied, 1)
                wait_alone(pool, payload_copied, done(t), pool_passed)
                pool.indirect_dma_start(out=sorted_tab[:, :],
                                        out_offset=bass.IndirectOffsetOnAxis(ap=place[:, q:q + 1], axis=0),
                                        in_=load_out[:, q, :], in_offset=None).then_inc(sorted_out[q], 16)
            for q in range(4):
                place_out(q, q, 0, True)
            with pool.Fori(1, T // 4) as i:
                for q in range(4):
                    place_out(4 * i + q, q, i, False)
            for q in range(4):
                wait_alone(pool, sorted_out[q], 16 * (T // 4), pool_passed)
            pool.sem_inc(sorted_done, 1)

            def edge_phase(s, tab_a, tab_b, out_tab, k):
                g0 = k * EC

                def gather(h, q):
                    c = 4 * h + q
                    wait_alone(pool, s["update"], freed(g0 + c, 4), pool_passed)
                    wait_alone(pool, s["idx"], g0 + c + 1, pool_passed)
                    for t, ix, rows in ((tab_a, idx_a, rows_a), (tab_b, idx_b, rows_b)):
                        for j in range(R):
                            pool.indirect_dma_start(
                                out=rows[q][:, j, :], out_offset=None, in_=t[:, :],
                                in_offset=bass.IndirectOffsetOnAxis(ap=ix[q][:, j:j + 1], axis=0)
                            ).then_inc(gathered[q], 16)

                def scatter(h, q):
                    c = 4 * h + q
                    if s is m and isinstance(c, int) and c == 0:
                        pool.wait_ge(msg_filled, 16 * NT)
                    wait_alone(pool, s["update"], done(g0 + c), pool_passed)
                    for j in range(R):
                        pool.indirect_dma_start(
                            out=out_tab[:, :],
                            out_offset=bass.IndirectOffsetOnAxis(ap=idx_c[q][:, j:j + 1], axis=0),
                            in_=upd[q][:, j, :], in_offset=None, bounds_check=NROWS - 1, oob_is_err=False
                        ).then_inc(scattered[q], 16)

                def step(i, s_):
                    t = chunk_at(i, s_, 0)
                    if t:
                        gather(*t)
                    t = chunk_at(i, s_, 5)
                    if t:
                        wait_alone(pool, scattered[t[1]], 64 * (k * uses(t[1], EC, 4) + t[0] + 1), pool_passed)
                        pool.sem_inc(s["update_free"], 1)
                    t = chunk_at(i, s_, 4)
                    if t:
                        scatter(*t)
                chunks(pool, step)

            pool.sem_inc(m["update_free"], SEED)
            edge_phase(m, x, edge_attr, msg_tab, 0)
            pool.sem_inc(m_done, 1)

            pool.sem_inc(u["scaled"], SEED)
            pool.sem_inc(u["shifted"], SEED)
            pool.sem_inc(u["result"], SEED)

            def update_step(i, s):
                t = tile_at(i, s, 5, 8)
                if t:
                    n, q = 8 * t[0] + t[1], t[1] % 4
                    wait_alone(pool, u["normed2"], done(n), pool_passed)
                    pool.tensor_tensor(out=n_norm2[q][:, :, :], in0=n_norm2[q][:, :, :], in1=wide(gamma_row),
                                       op=ALU.mult).then_inc(u["scaled"], 1)
                    wait_alone(pool, u["scaled"], done(n), pool_passed)
                    wait_alone(pool, u["result"], freed(n, 4), pool_passed)
                    pool.tensor_tensor(out=n_scaled[q][:, :, :], in0=n_norm2[q][:, :, :], in1=wide(beta_row),
                                       op=ALU.add).then_inc(u["shifted"], 1)
                t = tile_at(i, s, 6, 8)
                if t:
                    n, q = 8 * t[0] + t[1], t[1] % 4
                    wait_alone(pool, u["joined_relu"], done(n), pool_passed)
                    wait_alone(pool, u["stored"], freed(n, 4), pool_passed)
                    wait_alone(pool, u["normed3"], freed(n, 4), pool_passed)
                    pool.tensor_tensor(out=n_out[q][:, :, :], in0=n_scaled[q][:, :, :], in1=n_in[t[1]][:, :, :],
                                       op=ALU.add).then_inc(u["result"], 1)
            pipeline(pool, 13, update_step, 8)

            pool.sem_inc(f["shifted"], SEED)
            wait_alone(pool, u["h_stored"], NT + SEED, pool_passed)

            def layer(l, is_last):
                wait_alone(pool, f["stored"], (l + 1) * NT + SEED, pool_passed)
                edge_phase(a, h_tab, h_tab, y_tab, l + 1)
                pool.sem_inc(a_done, 1)
                g0 = (l + 1) * NT

                def step(i, s):
                    t = tile_at(i, s, 6)
                    if t:
                        g, q = g0 + (4 * t[0] + t[1]), t[1]
                        wait_alone(pool, f["normed2"], done(g), pool_passed)
                        pool.tensor_tensor(out=n_scaled[q][:, :, :], in0=n_norm2[q][:, :, :], in1=wide(g2_row),
                                           op=ALU.mult).then_inc(f["scaled"], 1)
                        wait_alone(pool, f["scaled"], done(g), pool_passed)
                        if is_last:
                            pool.tensor_tensor(out=n_norm2[q][:, :, :], in0=n_scaled[q][:, :, :], in1=wide(b2_row),
                                               op=ALU.add).then_inc(f["shifted"], 1)
                        else:
                            wait_alone(pool, f["stored"], freed(g, 4), pool_passed)
                            pool.tensor_tensor(out=n_out[q][:, :, :], in0=n_scaled[q][:, :, :], in1=wide(b2_row),
                                               op=ALU.add).then_inc(f["result"], 1)
                    t = tile_at(i, s, 7)
                    if t and is_last:
                        g, q = g0 + (4 * t[0] + t[1]), t[1]
                        wait_alone(pool, f["shifted"], done(4 * t[0] + t[1]), pool_passed)
                        wait_alone(pool, x1_loaded[q], 16 * (t[0] + 1), pool_passed)
                        wait_alone(pool, f["stored"], freed(g, 4), pool_passed)
                        pool.tensor_tensor(out=n_out[q][:, :, :], in0=n_norm2[q][:, :, :],
                                           in1=n_add[q][:, :, :], op=ALU.add).then_inc(f["result"], 1)
                pipeline(pool, 10, step)

            with pool.Fori(0, L - 1) as l:
                layer(l, False)
            layer(L - 1, True)

        @block.tensor
        def _(pe):
            def count(t, start=False, stop=False):
                pe.wait_ge(one_hot, t + 1)
                return pe.matmul(ps[:, 0, :], one(high_hot, t), one(low_hot, t), start=start, stop=stop,
                                 skip_group_check=True)

            def one(t3, t):
                return t3[:, t, :] if isinstance(t, int) else \
                    t3[:, bass.ds(t, 1), :].rearrange("p a f -> p (a f)")
            for t in range(4):
                count(t, start=t == 0)
            with pe.Fori(1, T // 4 - 1) as i:
                for k in range(4):
                    count(4 * i + k)
            for t in range(T - 4, T - 1):
                count(t)
            count(T - 1, stop=True).then_inc(counted, 1)
            pe.wait_ge(base_step, 2)
            pe.matmul(ps[:, 4, 0:1], before[:, :], running[:, LOW - 1:LOW], start=True,
                      stop=True).then_inc(row_base, 1)
            pe.wait_ge(consts_made, 2)
            pe.wait_ge(const_loaded, 16 * 17)
            pe.transpose(ps[:, 7, 0:L * NV + 1], vec_rows[0:L * NV + 1, :],
                         ident[0:L * NV + 1, 0:L * NV + 1]).then_inc(columns_made, 1)

            pe.wait_ge(base_step, 5)
            pe.matmul(ps[:, 1, :], ident[:, :], counts[:, :], start=True, stop=False,
                      skip_group_check=True).then_inc(table_added, 1)

            def look_up(t, q, first):
                pe.wait_ge(table_copied, t + 1)
                pe.wait_ge(row_hot, t + 1)
                pe.matmul(ps[:, 1, :], one(high_hot, t), one(low_hot, t), start=False, stop=False,
                          skip_group_check=True).then_inc(table_added, 1)
                if not first:
                    pe.wait_ge(place_ready, t - 1)
                pe.matmul(ps[:, 2 + q, :], high_row[:, q, :], table[:, q, :], start=True,
                          stop=True).then_inc(looked_up, 1)
            look_up(0, 0, True)
            look_up(1, 1, True)
            with pe.Fori(1, T // 2) as i:
                for q in range(2):
                    look_up(2 * i + q, q, False)

            for k in ("turned", "proj", "rows"):
                pe.sem_inc(edge[k], SEED)

            def message(i, s):
                t = chunk_at(i, s, 2)
                if t:
                    c, q = 4 * t[0] + t[1], t[1] % 2
                    pe.wait_ge(m["sums"], done(c))
                    pe.wait_ge(m["den"], done(c))
                    pe.wait_ge(m["update"], freed(c, 1))
                    for j in range(R):
                        pe.matmul(blocks(6)[:, j, :], by_row(e_sum[q][:, :], j), w_upd[:, 1, :], start=True,
                                  stop=True)
                    for j in range(R):
                        mm = pe.matmul(ps[:, 7, 2 * j:2 * j + 1], by_row(e_den[q][:, :], j), ident[:, 0:1],
                                       start=True, stop=True)
                    mm.then_inc(m["rows"], 1)
                t = chunk_at(i, s, 1)
                if t:
                    c = 4 * t[0] + t[1]
                    pe.wait_ge(m["normed"], done(c))
                    pe.wait_ge(m["turned_copy"], freed(c, 1))
                    for j in range(R):
                        pe.transpose(by_row(bank(0), j), e_norm[:, j, :], ident[:, :])
                    for j in range(R):
                        tr = pe.transpose(by_row(bank(1), j), rows_b[t[1]][:, j, :], ident[:, :])
                    tr.then_inc(m["turned"], 1)
                    pe.wait_ge(m["turned_copy"], done(c))
                    pe.wait_ge(m["value"], freed(c, 1))
                    pe.matmul(bank(2), w_msg[:, 0, :], e_aT[:, :], start=True, stop=False)
                    pe.matmul(bank(2), w_msg[:, 1, :], e_bT[:, :], start=False, stop=True).then_inc(m["proj"], 1)
            chunks(pe, message)

            for k in ("turned", "proj"):
                pe.sem_inc(node[k], SEED)

            def turn(s, n, q, rows):
                pe.wait_ge(s["normed"], done(n))
                pe.wait_ge(s["turned_copy"], freed(n, 2))
                for j in range(R):
                    tr = pe.transpose(blocks(q % 2)[:, j, :], rows[:, j, :], ident[:, :])
                tr.then_inc(s["turned"], 1)

            def project(target, added, rows_T, w, finished):
                pe.matmul(bank(target), ident[:, :], flat(added), start=True, stop=False, skip_group_check=True)
                for j in range(R):
                    mm = pe.matmul(blocks(target)[:, j, :], rows_T[:, j * P:(j + 1) * P], w, start=False,
                                   stop=j == R - 1, skip_group_check=True)
                mm.then_inc(finished, 1)

            for k in ("turned3", "proj3"):
                pe.sem_inc(u[k], SEED)
            pe.wait_ge(bo0_made, 1)

            def update_step(i, s):
                t = tile_at(i, s, 10, 8)
                if t:
                    n, q = 8 * t[0] + t[1], t[1] % 4
                    pe.wait_ge(u["turned_copy3"], done(n))
                    pe.wait_ge(u["embedded"], freed(n, 2))
                    project(6 + q % 2, bo0_wide, n_T3[q], w_emb[:, :], u["proj3"])
                t = tile_at(i, s, 3, 8)
                if t:
                    n, q = 8 * t[0] + t[1], t[1] % 4
                    pe.wait_ge(msg_loaded[q], 16 * (2 * t[0] + t[1] // 4 + 1))
                    pe.wait_ge(u["turned_copy"], done(n))
                    pe.wait_ge(u["normed2"], freed(n, 2))
                    project(4 + q % 2, n_add[q], n_T[q], w_upd[:, 0, :], u["proj"])
                t = tile_at(i, s, 2, 8)
                if t:
                    turn(u, 8 * t[0] + t[1], t[1] % 4, n_norm[t[1]])
                t = tile_at(i, s, 8, 8)
                if t:
                    n, q = 8 * t[0] + t[1], t[1] % 4
                    pe.wait_ge(u["normed3"], done(n))
                    pe.wait_ge(u["turned_copy3"], freed(n, 2))
                    for j in range(R):
                        tr = pe.transpose(blocks(2 + q % 2)[:, j, :], n_norm3[q][:, j, :], ident[:, :])
                    tr.then_inc(u["turned3"], 1)
            pipeline(pe, 13, update_step, 8)

            pe.sem_inc(a["score"], EC + SEED)
            for k in ("hidden", "ffn"):
                pe.sem_inc(f[k], NT + SEED)

            def layer(l, is_last):
                pe.wait_ge(layer_step, 2 * l + 1)
                for n, (w, v) in enumerate(((wq[:, :], VO), (wk[:, :], VO), (wv[:, :], VO),
                                            (w1[:, 0:P], VF2), (w1[:, P:2 * P], VF2))):
                    mm = pe.matmul(ps[:, 7, 2 * n:2 * n + 1], w, layer_cols[:, v:v + 1], start=True, stop=True)
                mm.then_inc(folds_made, 1)

                def attend(i, s):
                    t2 = chunk_at(i, s, 2)
                    if t2:
                        g2 = (l + 1) * EC + (4 * t2[0] + t2[1])
                        pe.wait_ge(a["kq"], done(g2))
                        pe.matmul(bank(5), head_sum[:, :], e_kq[:, :], start=True, stop=True
                                  ).then_inc(a["score"], 1)
                    t = chunk_at(i, s, 1)
                    if t:
                        g, q = (l + 1) * EC + (4 * t[0] + t[1]), t[1]
                        pe.wait_ge(gathered[q], 128 * ((l + 1) * uses(q, EC, 4) + t[0] + 1))
                        pe.wait_ge(a["turned_copy"], freed(g, 1))
                        for j in range(R):
                            pe.transpose(by_row(bank(0), j), rows_a[q][:, j, :], ident[:, :])
                        for j in range(R):
                            tr = pe.transpose(by_row(bank(1), j), rows_b[q][:, j, :], ident[:, :])
                        tr.then_inc(a["turned"], 1)
                        pe.wait_ge(a["turned_copy"], done(g))
                        pe.wait_ge(a["value"], freed(g, 1))
                        pe.matmul(bank(2), wk[:, :], e_aT[:, :], start=True, stop=True)
                        pe.matmul(bank(3), wq[:, :], e_bT[:, :], start=True, stop=True)
                        pe.matmul(bank(4), wv[:, :], e_aT[:, :], start=True, stop=True).then_inc(a["proj"], 1)
                    if t2:
                        pe.wait_ge(a["attn"], done(g2))
                        pe.wait_ge(a["update"], freed(g2, 1))
                        for j in range(R):
                            mm = pe.matmul(blocks(6)[:, j, :], by_row(e_attn[:, :], j), wo[:, :], start=True,
                                           stop=True)
                        mm.then_inc(a["rows"], 1)
                chunks(pe, attend)

                g0 = (l + 1) * NT

                def step(i, s):
                    t = tile_at(i, s, 1)
                    if t:
                        turn(f, g0 + (4 * t[0] + t[1]), t[1], n_norm[t[1]])
                    t = tile_at(i, s, 2)
                    if t:
                        g, q = g0 + (4 * t[0] + t[1]), t[1]
                        pe.wait_ge(f["turned_copy"], done(g))
                        pe.wait_ge(f["relu"], freed(g, 2))
                        for k in range(2):
                            mm = pe.matmul(bank(2 + 2 * (q % 2) + k), w1[:, k * P:(k + 1) * P], n_T[q][:, :],
                                           start=True, stop=True)
                        mm.then_inc(f["hidden"], 1)
                    t = tile_at(i, s, 4)
                    if t:
                        g, q = g0 + (4 * t[0] + t[1]), t[1]
                        pe.wait_ge(f["relu"], done(g))
                        pe.wait_ge(f["normed2"], freed(g, 2))
                        for j in range(R):
                            o, c = blocks(6 + q % 2)[:, j, :], slice(j * P, (j + 1) * P)
                            pe.matmul(o, n_T[q][:, c], ident[:, :], start=True, stop=False, is_transpose=True)
                            pe.matmul(o, n_relu[q][:, 0, c], w2[:, 0, :], start=False, stop=False)
                            mm = pe.matmul(o, n_relu[q][:, 1, c], w2[:, 1, :], start=False, stop=True)
                        mm.then_inc(f["ffn"], 1)
                pipeline(pe, 10, step)

            with pe.Fori(0, L - 1) as l:
                layer(l, False)
            layer(L - 1, True)

        @block.scalar
        def _(act):
            def copy_table(t, q):
                act.wait_ge(table_added, t + 1)
                if not isinstance(t, int) or t >= 2:
                    act.wait_ge(looked_up, t - 1)
                act.copy(table[:, q, :], ps[:, 1, :]).then_inc(table_copied, 1)
            copy_table(0, 0)
            copy_table(1, 1)
            with act.Fori(1, T // 2) as i:
                for q in range(2):
                    copy_table(2 * i + q, q)

            for k in ("std", "turned_copy", "value"):
                act.sem_inc(m[k], SEED)

            def message(i, s):
                t = chunk_at(i, s, 1)
                if t:
                    c = 4 * t[0] + t[1]
                    act.wait_ge(m["mean_var"], done(c))
                    act.activation(e_sd[:, :], e_mv[:, :, 1], ACT.Sqrt, bias=eps[:, 0:1]).then_inc(m["std"], 1)
                    act.wait_ge(m["turned"], done(c))
                    act.wait_ge(m["proj"], freed(c, 1))
                    act.activation(e_aT[:, :], bank(0), ACT.Relu)
                    act.copy(e_bT[:, :], bank(1)).then_inc(m["turned_copy"], 1)
                    act.wait_ge(m["proj"], done(c))
                    act.wait_ge(m["sums"], freed(c, 1))
                    act.activation(e_val[:, :], bank(2), ACT.Relu, bias=vec_cols[:, L * NV:L * NV + 1]
                                   ).then_inc(m["value"], 1)
            act.wait_ge(columns_copied, 1)
            chunks(act, message)

            for k in ("std", "turned_copy", "std2", "normed2"):
                act.sem_inc(node[k], SEED)
            for k in ("joined_relu", "std3", "normed3", "turned_copy3", "embedded"):
                act.sem_inc(u[k], SEED)

            def std(s, key, g, q, mv, sd):
                act.wait_ge(s["mean_var" + key], done(g))
                act.activation(sd[q][:, :], mv[q][:, :, 1], ACT.Sqrt, bias=eps[:, 0:1]).then_inc(s["std" + key], 1)

            def norm(s, key, g, rows, out_rows, sh, rs):
                act.wait_ge(s["shift" + key], done(g))
                for j in range(R):
                    ins = act.activation(out_rows[:, j, :], rows[:, j, :], ACT.Identity, bias=sh[:, j:j + 1],
                                         scale=rs[:, j:j + 1])
                ins.then_inc(s["normed" + key], 1)

            def update_step(i, s):
                t5, t9, t4, t8, t10, t1, t2, t7, t6 = (tile_at(i, s, lag, 8) for lag in (5, 9, 4, 8, 10, 1, 2, 7, 6))
                if t5:
                    n, q = 8 * t5[0] + t5[1], t5[1] % 4
                    act.wait_ge(u["shifted"], freed(n, 4))
                    norm(u, "2", n, blocks(4 + q % 2), n_norm2[q], n_sh2[q], n_rs2[q])
                if t9:
                    n, q = 8 * t9[0] + t9[1], t9[1] % 4
                    act.wait_ge(u["turned3"], done(n))
                    act.wait_ge(u["proj3"], freed(n, 4))
                    act.activation(n_T3[q], bank(2 + q % 2), ACT.Relu).then_inc(u["turned_copy3"], 1)
                if t4:
                    std(u, "2", 8 * t4[0] + t4[1], t4[1] % 4, n_mv2, n_sd2)
                if t8:
                    n, q = 8 * t8[0] + t8[1], t8[1] % 4
                    act.wait_ge(u["turned3"], freed(n, 4))
                    norm(u, "3", n, n_out[q], n_norm3[q], n_sh3[q], n_rs3[q])
                if t10:
                    n, q = 8 * t10[0] + t10[1], t10[1] % 4
                    act.wait_ge(u["proj3"], done(n))
                    act.wait_ge(u["h_stored"], freed(n, 4))
                    act.copy(flat(n_h[q]), bank(6 + q % 2)).then_inc(u["embedded"], 1)
                if t1:
                    std(u, "", 8 * t1[0] + t1[1], t1[1] % 4, n_mv, n_sd)
                if t2:
                    n, q = 8 * t2[0] + t2[1], t2[1] % 4
                    act.wait_ge(u["turned"], done(n))
                    act.wait_ge(u["proj"], freed(n, 4))
                    act.activation(n_T[q][:, :], bank(q % 2), ACT.Relu).then_inc(u["turned_copy"], 1)
                if t7:
                    std(u, "3", 8 * t7[0] + t7[1], t7[1] % 4, n_mv3, n_sd3)
                if t6:
                    n, q = 8 * t6[0] + t6[1], t6[1] % 4
                    act.wait_ge(u["joined"], done(n))
                    act.activation(flat(n_scaled[q]), flat(n_scaled[q]), ACT.Relu).then_inc(u["joined_relu"], 1)
            pipeline(act, 13, update_step, 8)

            for k in ("key", "exp"):
                act.sem_inc(a[k], EC + SEED)
            act.sem_inc(f["relu"], NT + SEED)

            def layer(l, is_last):
                act.wait_ge(layer_ready, l + 1)

                def attend(i, s):
                    t = chunk_at(i, s, 2)
                    if t:
                        g = (l + 1) * EC + (4 * t[0] + t[1])
                        act.wait_ge(a["clip"], done(g))
                        act.wait_ge(a["sums"], freed(g, 1))
                        act.activation(e_exp[:, :], e_clip[:, :], ACT.Exp).then_inc(a["exp"], 1)
                    t = chunk_at(i, s, 1)
                    if t:
                        g = (l + 1) * EC + (4 * t[0] + t[1])
                        act.wait_ge(a["turned"], done(g))
                        act.wait_ge(a["proj"], freed(g, 1))
                        act.copy(e_aT[:, :], bank(0))
                        act.copy(e_bT[:, :], bank(1)).then_inc(a["turned_copy"], 1)
                        act.wait_ge(a["proj"], done(g))
                        act.wait_ge(a["kq"], freed(g, 1))
                        act.activation(e_key[:, :], bank(2), ACT.Identity, bias=folded[:, 1:2]
                                       ).then_inc(a["key"], 1)
                chunks(act, attend)

                g0 = (l + 1) * NT

                def step(i, s):
                    t = tile_at(i, s, 3)
                    if t:
                        g, q = g0 + (4 * t[0] + t[1]), t[1]
                        act.wait_ge(f["hidden"], done(g))
                        for k in range(2):
                            ins = act.activation(n_relu[q][:, k, :], bank(2 + 2 * (q % 2) + k), ACT.Relu,
                                                 bias=folded[:, 3 + k:4 + k])
                        ins.then_inc(f["relu"], 1)
                    t = tile_at(i, s, 6)
                    if t:
                        g, q = g0 + (4 * t[0] + t[1]), t[1]
                        std(f, "2", g, q, n_mv2, n_sd2)
                        act.wait_ge(f["result"], freed(g, 4))
                        norm(f, "2", g, blocks(6 + q % 2), n_norm2[q], n_sh2[q], n_rs2[q])
                    t = tile_at(i, s, 0)
                    if t:
                        std(f, "", g0 + (4 * t[0] + t[1]), t[1], n_mv, n_sd)
                    t = tile_at(i, s, 1)
                    if t:
                        g, q = g0 + (4 * t[0] + t[1]), t[1]
                        act.wait_ge(f["turned"], done(g))
                        act.wait_ge(f["ffn"], freed(g, 4))
                        act.activation(n_T[q][:, :], bank(q % 2), ACT.Identity, bias=folded[:, 5:6],
                                       scale=layer_cols[:, VG1:VG1 + 1]).then_inc(f["turned_copy"], 1)
                pipeline(act, 10, step)

            with act.Fori(0, L - 1) as l:
                layer(l, False)
            layer(L - 1, True)

        @block.vector
        def _(dve):
            prepared = [0]

            def prep(ins):
                prepared[0] += 1
                ins.then_inc(sort_prep, 1)
                dve.wait_ge(sort_prep, prepared[0])
            dve.wait_ge(consts_made, 2)
            dve.wait_ge(edges_loaded, 32)
            prep(dve.tensor_scalar(part_i[:, :], dst_i[:, :], LOW - 1, None, ALU.bitwise_and))
            prep(dve.tensor_copy(low_c[:, :], part_i[:, :]))
            prep(dve.tensor_copy(dst_c[:, :], dst_i[:, :]))
            prep(dve.tensor_tensor(high_c[:, :], dst_c[:, :], low_c[:, :], ALU.subtract))
            prep(dve.tensor_copy(row_lo[:, :], row_i[:, :]))
            prep(dve.tensor_scalar(row_hi[:, :], row_lo[:, :], float(LOW), None, ALU.add))
            prep(dve.tensor_copy(low_key[:, :], iota_i[:, :]))
            prep(dve.tensor_scalar(high_key[:, :], iota_i[:, 0:P], float(LOW), None, ALU.mult))
            prep(dve.tensor_copy(payload[:, :, 0], dst_i[:, :]))
            prep(dve.tensor_copy(payload[:, :, 1], src_i[:, :]))
            prep(dve.tensor_scalar(payload[:, :, 2], num_i[:, :], float(E - 1), None, ALU.min))
            prep(dve.tensor_copy(payload[:, :, 3], num_i[:, :]))

            def one(t3, t):
                return t3[:, t, :] if isinstance(t, int) else \
                    t3[:, bass.ds(t, 1), :].rearrange("p a f -> p (a f)")

            def col(t2, t):
                return t2[:, t:t + 1] if isinstance(t, int) else t2[:, bass.ds(t, 1)]

            with dve.Fori(0, T // 4) as i:
                for k in range(4):
                    t = 4 * i + k
                    dve.tensor_scalar(one(high_hot, t), high_key[:, :], col(high_c, t), None, ALU.is_equal)
                    dve.tensor_scalar(one(low_hot, t), low_key[:, :], col(low_c, t), None,
                                      ALU.is_equal).then_inc(one_hot, 1)

            dve.wait_ge(const_loaded, 16 * 17)
            dve.tensor_copy(b_upd_wide[:, :, :], wide(b_upd_row)).then_inc(wide_made, 1)

            dve.wait_ge(counted, 1)
            dve.tensor_copy(counts[:, :], ps[:, 0, :]).then_inc(base_step, 1)
            dve.wait_ge(base_step, 1)
            dve.tensor_tensor_scan(running[:, :], ones[:, :], counts[:, :], 0.0, ALU.mult,
                                   ALU.add).then_inc(base_step, 1)
            dve.wait_ge(row_base, 1)
            dve.tensor_copy(row_start[:, :], ps[:, 4, 0:1]).then_inc(base_step, 1)
            dve.wait_ge(base_step, 3)
            dve.tensor_tensor(running[:, :], running[:, :], counts[:, :], ALU.subtract).then_inc(base_step, 1)
            dve.wait_ge(base_step, 4)
            dve.tensor_scalar(counts[:, :], running[:, :], row_start[:, 0:1], None, ALU.add).then_inc(base_step, 1)

            dst_rows_t = dst_rows[:, :].rearrange("p (e t) -> p t e", t=T)

            def rank_edges(t, q, first):
                if not first:
                    dve.wait_ge(row_hot, t)
                dve.tensor_scalar(in_range[:, :], one(dst_rows_t, t), row_hi[:, 0:1], None,
                                  ALU.is_lt).then_inc(in_range_ready, 1)
                if not first:
                    dve.wait_ge(rank_ready, t)
                dve.scalar_tensor_tensor(running[:, 0:P], one(dst_rows_t, t), col(dst_c, t), earlier[:, :],
                                         ALU.is_equal, ALU.mult, accum_out=col(rank_in, t)
                                         ).then_inc(rank_ready, 1)
                if not isinstance(t, int) or t >= 2:
                    dve.wait_ge(looked_up, t - 1)
                dve.wait_ge(in_range_ready, t + 1)
                dve.scalar_tensor_tensor(high_row[:, q, :], one(dst_rows_t, t), row_lo[:, 0:1], in_range[:, :],
                                         ALU.is_ge, ALU.mult).then_inc(row_hot, 1)

            def place_edges(t, q, landed):
                dve.wait_ge(looked_up, t + 1)
                if not isinstance(t, int) or t:
                    dve.wait_ge(found_ready, t)
                dve.scalar_tensor_tensor(counts[:, :], ps[:, 2 + q % 2, :], 1.0, one(low_hot, t), ALU.mult, ALU.mult,
                                         accum_out=col(found, t)).then_inc(found_ready, 1)
                dve.wait_ge(found_ready, t + 1)
                if not isinstance(t, int) or t >= 4:
                    dve.wait_ge(sorted_out[q], 16 * landed)
                dve.tensor_tensor(place[:, q:q + 1], col(found, t), col(rank_in, t),
                                  ALU.add).then_inc(place_ready, 1)
            dve.wait_ge(columns_made, 1)
            dve.tensor_copy(vec_cols[:, :], ps[:, 7, 0:L * NV + 1]).then_inc(columns_copied, 1)
            dve.wait_ge(base_step, 5)
            dve.wait_ge(dst_rows_loaded, 16)
            rank_edges(0, 0, True)
            rank_edges(1, 1, False)
            place_edges(0, 0, 0)

            def rank_and_place(t, q, landed):
                rank_edges(t + 1, (q + 1) % 2, False)
                place_edges(t, q, landed)
            for t in range(1, 4):
                rank_and_place(t, t, 0)
            with dve.Fori(1, T // 4 - 1) as i:
                for q in range(4):
                    rank_and_place(4 * i + q, q, i)
            for q in range(3):
                rank_and_place(T - 4 + q, q, T // 4 - 1)
            place_edges(T - 1, 3, T // 4 - 1)

            for k in ("stats", "mean_var", "rstd", "normed", "sums", "den", "recip", "update"):
                dve.sem_inc(m[k], SEED)

            dve.wait_ge(sorted_loaded, 16)
            sorted_col = lambda k: sorted_rows[:, :, :, k]
            dve.tensor_copy(dst_s[:, :, :], sorted_col(0)).then_inc(dst_col_ready, 1)
            dve.tensor_copy(dst_idx[:, :, :], sorted_col(0)).then_inc(dst_col_ready, 1)
            dve.tensor_copy(src_idx[:, :, :], sorted_col(1))
            dve.tensor_copy(edge_idx[:, :, :], sorted_col(2)).then_inc(dst_col_ready, 1)

            def cols(t, c):
                return t[:, c, :] if isinstance(c, int) else \
                    t[:, bass.ds(c, 1), :].rearrange("p a j -> p (a j)")

            def set_indices(h, q, ib, k):
                if not (isinstance(h, int) and isinstance(k, int) and k == 0 and h == 0):
                    dve.wait_ge(gathered[q], 128 * (k * uses(q, EC, 4) + h))
                dve.tensor_copy(idx_a[q][:, :], cols(src_idx, 4 * h + q))
                dve.tensor_copy(idx_b[q][:, :], cols(ib, 4 * h + q)).then_inc(edge["idx"], 1)
            dve.wait_ge(dst_col_ready, 3)
            for n in range(2):
                set_indices(0, n, edge_idx, 0)
            dve.wait_ge(dst_line_in, 32)
            dve.tensor_tensor(same_next[:, :, :], dst_s[:, :, :], dst_next[:, :, :],
                              ALU.is_equal).then_inc(tables_step, 1)
            dve.wait_ge(tables_step, 1)
            dve.scalar_tensor_tensor(last_idx[:, :, :], same_next[:, :, :], float(SKIP), dst_s[:, :, :],
                                     ALU.mult, ALU.add).then_inc(tables_ready, 1)
            dve.memset(same[:, 0:1], 0.0)
            dve.tensor_tensor(same[:, 1:EROWS], dst_sorted[:, 1:EROWS], dst_sorted[:, 0:EROWS - 1],
                              ALU.is_equal).then_inc(tables_ready, 1)
            dve.wait_ge(tables_ready, 2)

            def same_of(c):
                return same[:, c * TILE:(c + 1) * TILE] if isinstance(c, int) else \
                    same[:, bass.ds(c * TILE, TILE)]

            def begin(c, t, q):
                return 0.0 if isinstance(c, int) and c == 0 else t[1 - q][:, 511:512]

            def message(i, s):
                t1, t2, ahead = chunk_at(i, s, 1), chunk_at(i, s, 2), chunk_at(i, s, -2)
                if ahead:
                    set_indices(*ahead, edge_idx, 0)
                if t2:
                    c, q = 4 * t2[0] + t2[1], t2[1] % 2
                    dve.wait_ge(m["rows"], freed(c, 2))
                    dve.wait_ge(m["den"], freed(c, 1))
                    dve.tensor_tensor_scan(e_den[q][:, :], same_of(c), ones[:, :], begin(c, e_den, q), ALU.mult,
                                           ALU.add).then_inc(m["den"], 1)
                    dve.wait_ge(m["value"], done(c))
                    dve.wait_ge(m["sums"], freed(c, 1))
                    dve.tensor_tensor_scan(e_sum[q][:, :], same_of(c), e_val[:, :], begin(c, e_sum, q), ALU.mult,
                                           ALU.add).then_inc(m["sums"], 1)
                if t1:
                    c, q = 4 * t1[0] + t1[1], t1[1]
                    dve.wait_ge(gathered[q], 128 * (t1[0] + 1))
                    for j in range(R):
                        ins = dve.bn_stats(e_bn[:, j, :], rows_a[q][:, j, :])
                    ins.then_inc(m["stats"], 1)
                    wait_alone(dve, m["stats"], done(c), dve_passed)
                    for j in range(R):
                        ins = dve.bn_aggr(e_mv[:, j, :], e_bn[:, j, :])
                    ins.then_inc(m["mean_var"], 1)
                    dve.wait_ge(m["std"], done(c))
                    dve.reciprocal(e_rs[:, :], e_sd[:, :]).then_inc(m["rstd"], 1)
                    dve.wait_ge(m["rstd"], done(c))
                    dve.wait_ge(m["turned"], freed(c, 1))
                    for j in range(R):
                        ins = dve.tensor_scalar(e_norm[:, j, :], rows_a[q][:, j, :], e_mv[:, j, 0:1],
                                                e_rs[:, j:j + 1], ALU.subtract, ALU.mult)
                    ins.then_inc(m["normed"], 1)
                if t2:
                    c, q = 4 * t2[0] + t2[1], t2[1]
                    dve.wait_ge(m["rows"], done(c))
                    cnt = ps[:, 7, 0:2 * R].rearrange("p (j k) -> p j k", k=2)[:, :, 0]
                    dve.reciprocal(e_rc[:, :], cnt).then_inc(m["recip"], 1)
                    dve.wait_ge(m["recip"], done(c))
                    dve.wait_ge(m["update_free"], freed(c, 4))
                    dve.tensor_copy(idx_c[q][:, :], cols(last_idx, c))
                    for j in range(R):
                        ins = dve.scalar_tensor_tensor(upd[q][:, j, :], blocks(6)[:, j, :], e_rc[:, j:j + 1],
                                                       b_upd_row[:, :], ALU.mult, ALU.add)
                    ins.then_inc(m["update"], 1)
            chunks(dve, message, 2)

            def stats(s, key, g, src_blocks, bn):
                for j in range(R):
                    ins = dve.bn_stats(bn[:, j, :], src_blocks[:, j, :])
                ins.then_inc(s["stats" + key], 1)

            def mean_var(s, key, g, bn, mv):
                wait_alone(dve, s["stats" + key], done(g), dve_passed)
                for j in range(R):
                    ins = dve.bn_aggr(mv[:, j, :], bn[:, j, :])
                ins.then_inc(s["mean_var" + key], 1)

            def rstd(s, key, g, q, sd, rs):
                dve.wait_ge(s["std" + key], done(g))
                dve.reciprocal(rs[q][:, :], sd[q][:, :]).then_inc(s["rstd" + key], 1)

            def normalise(s, g, q, rows, normed, depth):
                dve.wait_ge(s["rstd"], done(g))
                dve.wait_ge(s["turned"], freed(g, depth))
                for j in range(R):
                    ins = dve.tensor_scalar(normed[:, j, :], rows[:, j, :], n_mv[q][:, j, 0:1],
                                            n_rs[q][:, j:j + 1], ALU.subtract, ALU.mult)
                ins.then_inc(s["normed"], 1)

            def shift(s, key, g, mv, rs, sh):
                dve.wait_ge(s["rstd" + key], done(g))
                dve.scalar_tensor_tensor(sh[:, :], mv[:, :, 0], -1.0, rs[:, :], ALU.mult,
                                         ALU.mult).then_inc(s["shift" + key], 1)

            for k in ("stats", "mean_var", "rstd", "normed", "stats2", "mean_var2", "rstd2", "shift2"):
                dve.sem_inc(node[k], SEED)
            for k in ("joined", "stats3", "mean_var3", "rstd3", "shift3"):
                dve.sem_inc(u[k], SEED)
            dve.tensor_copy(bo0_wide[:, :, :], wide(bo0_row)).then_inc(bo0_made, 1)

            def update_step(i, s):
                t0, t1, t2, t4, t5, t6, t7, t8 = (tile_at(i, s, lag, 8) for lag in (0, 1, 2, 4, 5, 6, 7, 8))
                if t4:
                    n4, q4 = 8 * t4[0] + t4[1], t4[1] % 4
                    dve.wait_ge(u["proj"], done(n4))
                    stats(u, "2", n4, blocks(4 + q4 % 2), n_bn2[q4])
                if t5:
                    q5 = t5[1] % 4
                    shift(u, "2", 8 * t5[0] + t5[1], n_mv2[q5], n_rs2[q5], n_sh2[q5])
                if t2:
                    n2, q2 = 8 * t2[0] + t2[1], t2[1] % 4
                    rstd(u, "", n2, q2, n_sd, n_rs)
                if t8:
                    n8, q8 = 8 * t8[0] + t8[1], t8[1] % 4
                    rstd(u, "3", n8, q8, n_sd3, n_rs3)
                if t4:
                    mean_var(u, "2", n4, n_bn2[q4], n_mv2[q4])
                if t8:
                    shift(u, "3", n8, n_mv3[q8], n_rs3[q8], n_sh3[q8])
                if t6:
                    n6, q6 = 8 * t6[0] + t6[1], t6[1] % 4
                    dve.wait_ge(u["shifted"], done(n6))
                    dve.scalar_tensor_tensor(flat(n_scaled[q6]), flat(n_norm[t6[1]]), 0.0, flat(n_scaled[q6]),
                                             ALU.max, ALU.add).then_inc(u["joined"], 1)
                if t2:
                    normalise(u, n2, q2, n_in[t2[1]], n_norm[t2[1]], 8)
                if t1:
                    n1, q1 = 8 * t1[0] + t1[1], t1[1] % 4
                    mean_var(u, "", n1, n_bn[q1], n_mv[q1])
                if t7:
                    n7, q7 = 8 * t7[0] + t7[1], t7[1] % 4
                    dve.wait_ge(u["result"], done(n7))
                    stats(u, "3", n7, n_out[q7], n_bn3[q7])
                if t0:
                    n0, q0 = 8 * t0[0] + t0[1], t0[1] % 4
                    dve.wait_ge(u_loaded[t0[1]], 16 * (t0[0] + 1))
                    stats(u, "", n0, n_in[t0[1]], n_bn[q0])
                if t4:
                    rstd(u, "2", n4, q4, n_sd2, n_rs2)
                if t7:
                    mean_var(u, "3", n7, n_bn3[q7], n_mv3[q7])
            pipeline(dve, 13, update_step, 8)

            for k in ("kq", "clip", "attn"):
                dve.sem_inc(a[k], EC + SEED)
            dve.sem_inc(a["recip"], 2 * EC + SEED)

            def layer(l, is_last):
                count = (9 * l + 8) if is_last else (9 * l + 9)
                dve.wait_ge(weights_loaded, 16 * count)
                names = vec_cols[:, 0:NV * L].rearrange("p (n l) -> p n l", l=L)
                pick = names[:, :, l] if isinstance(l, int) else \
                    names[:, :, bass.ds(l, 1)].rearrange("p n a -> p (n a)")
                if not is_last:
                    dve.tensor_tensor(b2_row[:, :], b2_row[:, :], bo_row[:, :], ALU.add)
                dve.tensor_copy(layer_cols[:, :], pick).then_inc(layer_step, 1)
                dve.wait_ge(layer_step, 2 * l + 1)
                dve.wait_ge(folds_made, l + 1)
                fold = ps[:, 7, 0:10].rearrange("p (n k) -> p n k", k=2)[:, :, 0]
                dve.tensor_tensor(folded[:, 0:3], layer_cols[:, VQ:VV + 1], fold[:, 0:3], ALU.subtract)
                dve.tensor_tensor(folded[:, 3:5], layer_cols[:, VF0:VF1 + 1], fold[:, 3:5], ALU.subtract)
                dve.tensor_tensor(folded[:, 5:6], layer_cols[:, VB1:VB1 + 1], layer_cols[:, VF2:VF2 + 1],
                                  ALU.add).then_inc(layer_step, 1)
                dve.wait_ge(layer_step, 2 * l + 2)
                dve.sem_inc(layer_ready, 1)

                for n in range(2):
                    set_indices(0, n, dst_idx, l + 1)

                def attend(i, s):
                    t, t3, ahead = chunk_at(i, s, 2), chunk_at(i, s, 3), chunk_at(i, s, -2)
                    if ahead:
                        set_indices(*ahead, dst_idx, l + 1)
                    if t:
                        c, q = 4 * t[0] + t[1], t[1] % 2
                        g = (l + 1) * EC + c
                        dve.wait_ge(a["key"], done(g))
                        dve.wait_ge(a["score"], freed(g, 1))
                        dve.scalar_tensor_tensor(e_kq[:, :], bank(3), folded[:, 0:1], e_key[:, :], ALU.add,
                                                 ALU.mult).then_inc(a["kq"], 1)
                    if t3:
                        g3, q3 = (l + 1) * EC + (4 * t3[0] + t3[1]), t3[1]
                        dve.wait_ge(a["rows"], done(g3))
                        dve.wait_ge(a["update_free"], freed(g3, 4))
                        dve.tensor_copy(idx_c[q3][:, :], cols(last_idx, 4 * t3[0] + q3))
                        dve.tensor_tensor(flat(upd[q3]), bank(6), flat(rows_b[q3]), ALU.add
                                          ).then_inc(a["update"], 1)
                    if t:
                        dve.wait_ge(a["score"], done(g))
                        dve.wait_ge(a["exp"], freed(g, 1))
                        dve.tensor_scalar(e_clip[:, :], bank(5), -5.0, 5.0, ALU.max, ALU.min
                                          ).then_inc(a["clip"], 1)
                        dve.wait_ge(a["exp"], done(g))
                        dve.scalar_tensor_tensor(e_val[:, :], bank(4), folded[:, 2:3], e_exp[:, :], ALU.add,
                                                 ALU.mult).then_inc(a["value"], 1)
                        dve.wait_ge(a["den"], freed(g, 1))
                        dve.tensor_tensor_scan(e_den[q][:, :], same_of(c), e_exp[:, :], begin(c, e_den, q),
                                               ALU.mult, ALU.add).then_inc(a["den"], 1)
                        dve.wait_ge(a["value"], done(g))
                        dve.wait_ge(a["sums"], freed(g, 1))
                        dve.tensor_tensor_scan(e_sum[q][:, :], same_of(c), e_val[:, :], begin(c, e_sum, q),
                                               ALU.mult, ALU.add).then_inc(a["sums"], 1)
                        dve.wait_ge(a["den"], done(g))
                        dve.tensor_scalar(e_rden[:, :], e_den[q][:, :], 1e-6, None, ALU.add
                                          ).then_inc(a["recip"], 1)
                        dve.wait_ge(a["recip"], 2 * g + (SEED + 1))
                        dve.reciprocal(e_rinv[:, :], e_rden[:, :]).then_inc(a["recip"], 1)
                        dve.wait_ge(a["recip"], 2 * g + (SEED + 2))
                        dve.wait_ge(a["sums"], done(g))
                        dve.wait_ge(a["rows"], freed(g, 1))
                        dve.tensor_tensor(e_attn[:, :], e_sum[q][:, :], e_rinv[:, :], ALU.mult
                                          ).then_inc(a["attn"], 1)
                chunks(dve, attend, 2)

                g0 = (l + 1) * NT

                def step(i, s):
                    t0, t1, t6 = (tile_at(i, s, lag) for lag in (0, 1, 6))
                    if t6:
                        g6, q6 = g0 + (4 * t6[0] + t6[1]), t6[1]
                        dve.wait_ge(f["ffn"], done(g6))
                        stats(f, "2", g6, blocks(6 + q6 % 2), n_bn2[q6])
                        mean_var(f, "2", g6, n_bn2[q6], n_mv2[q6])
                    if t0:
                        g0_, q0 = g0 + (4 * t0[0] + t0[1]), t0[1]
                        dve.wait_ge(n_loaded[q0], 16 * (l * uses(q0, NT, 4) + t0[0] + 1))
                        stats(f, "", g0_, n_in[q0], n_bn[q0])
                    if t1:
                        g1, q1 = g0 + (4 * t1[0] + t1[1]), t1[1]
                        rstd(f, "", g1, q1, n_sd, n_rs)
                        normalise(f, g1, q1, n_in[q1], n_norm[q1], 4)
                    if t6:
                        rstd(f, "2", g6, q6, n_sd2, n_rs2)
                        shift(f, "2", g6, n_mv2[q6], n_rs2[q6], n_sh2[q6])
                    if t0:
                        mean_var(f, "", g0_, n_bn[q0], n_mv[q0])
                pipeline(dve, 10, step)

            with dve.Fori(0, L - 1) as l:
                layer(l, False)
            layer(L - 1, True)


_INS = ["x", "src", "dst", "edge_attr_128", "L0_gnn_W_msg", "L0_gnn_b_msg", "L0_gnn_W_upd", "L0_gnn_b_upd",
        "L0_gnn_gamma", "L0_gnn_beta", "L1_gnn_Wemb", "L1_gnn_Wq", "L1_gnn_bq", "L1_gnn_Wk", "L1_gnn_bk",
        "L1_gnn_Wv", "L1_gnn_bv", "L1_gnn_Wo", "L1_gnn_bo", "L1_gnn_ln1_g", "L1_gnn_ln1_b", "L1_gnn_W1",
        "L1_gnn_b1", "L1_gnn_W2", "L1_gnn_b2", "L1_gnn_ln2_g", "L1_gnn_ln2_b"]


def kernel(**inputs):
    import numpy as np
    import concourse.bacc as bacc
    from concourse.bass_utils import run_bass_kernel_spmd

    nc = bacc.Bacc("TRN2", target_bir_lowering=False, num_devices=1)
    arrays, args = {}, []
    for name in _INS:
        arr = np.ascontiguousarray(inputs[name])
        arrays[f"in_{name}"] = arr
        args.append(nc.dram_tensor(f"in_{name}", arr.shape, mybir.dt.from_np(arr.dtype),
                                   kind="ExternalInput").ap())
    out = nc.dram_tensor("out_0", inputs["x"].shape, F32, kind="ExternalOutput").ap()
    build(nc, *args, out)
    r = run_bass_kernel_spmd(nc, [arrays], core_ids=[0])
    return r.results[0]["out_0"]
```
